# Optimizing a Trainium2 kernel written in Bass

```python
import numpy as np
import jax
import jax.numpy as jnp

def _softmax(x, axis=-1):
    return jax.nn.softmax(x, axis=axis)

def _gelu(x):
    return jax.nn.gelu(x, approximate=True)

def _silu(x):
    return jax.nn.silu(x)

def _sigmoid(x):
    return jax.nn.sigmoid(x)

def _layernorm(x, axis=-1, eps=1e-05):
    m = jnp.mean(x, axis=axis, keepdims=True)
    v = jnp.var(x, axis=axis, keepdims=True)
    return (x - m) / jnp.sqrt(v + eps)

def _scatter_add(tgt, idx, src, axis=0):
    return tgt.at[idx].add(src)

def _segment_sum(src, seg, n):
    return jax.ops.segment_sum(src, seg, n)
kernel_name = 'mk_prb_d1_jaxref_r4_d8c6cd'

def setup_inputs(seed: int=0):
    np.random.seed(seed)
    _w = jnp.asarray

    def _L0_attn_setup():
        import math
        import jax, jax.numpy as jnp
        import numpy as np
        D_MODEL = 256
        D_STATE = 64
        D_CONV = 4
        HEADDIM = 64
        EXPAND = 2
        NGROUPS = 1
        CHUNK = 64
        LORA = 48
        THETA_CLIP = math.pi / 2
        D_INNER = EXPAND * D_MODEL
        NHEADS = D_INNER // HEADDIM
        NBLK = D_STATE // 2
        CONV_DIM = D_INNER + 2 * NGROUPS * D_STATE
        D_IN_PROJ = 2 * D_INNER + 2 * NGROUPS * D_STATE + NHEADS
        BATCH, SEQ = (2, 512)
        RMS_EPS = 1e-05

        def _forward(x, in_proj_w, conv_w, conv_b, dt_bias, lambda_base, theta_base, theta_w1, theta_w2, viscosity_eta, D, norm_w, out_proj_w):
            Bsz, L, _ = x.shape
            zxbcdt = x @ in_proj_w.T
            z = zxbcdt[..., :D_INNER]
            xBC = zxbcdt[..., D_INNER:D_INNER + CONV_DIM]
            dt = jax.nn.softplus(zxbcdt[..., -NHEADS:] + dt_bias)
            xp = jnp.pad(xBC, ((0, 0), (D_CONV - 1, 0), (0, 0)))
            conv = conv_b
            for k in range(D_CONV):
                conv = conv + xp[:, k:k + L, :] * conv_w[:, k]
            xBC = jax.nn.silu(conv)
            x_ssm = xBC[..., :D_INNER].reshape(Bsz, L, NHEADS, HEADDIM)
            Bg = xBC[..., D_INNER:D_INNER + NGROUPS * D_STATE].reshape(Bsz, L, NGROUPS, D_STATE)
            Cg = xBC[..., D_INNER + NGROUPS * D_STATE:].reshape(Bsz, L, NGROUPS, D_STATE)
            rep = NHEADS // NGROUPS
            Bh = jnp.repeat(Bg, rep, axis=2)
            Ch = jnp.repeat(Cg, rep, axis=2)
            B_c = jax.lax.complex(Bh[..., 0::2], Bh[..., 1::2])
            C_c = jax.lax.complex(Ch[..., 0::2], Ch[..., 1::2])
            lora = jnp.tanh(x @ theta_w1) @ theta_w2
            theta = jnp.clip(theta_base[None, None] + lora.reshape(Bsz, L, NHEADS, NBLK), -THETA_CLIP, THETA_CLIP)
            lambda_eff = lambda_base[None, None] + viscosity_eta[None, None] * theta ** 2
            log_z = jax.lax.complex(-lambda_eff * dt[..., None], theta * dt[..., None])
            x_disc = x_ssm * dt[..., None]
            Nc = L // CHUNK

            def chunkify(a):
                return a.reshape(Bsz, Nc, CHUNK, *a.shape[2:]).swapaxes(0, 1)
            mask = jnp.tril(jnp.ones((CHUNK, CHUNK), bool))[None, :, :, None, None]
            state0 = jnp.zeros((Bsz, NHEADS, HEADDIM, NBLK), jnp.complex64)

            def step(state, inp):
                lz, bc, cc, xc = inp
                cumlog = jnp.cumsum(lz, axis=1)
                diff = cumlog[:, :, None] - cumlog[:, None, :]
                real = jnp.where(mask, diff.real, -60.0)
                A = jnp.where(mask, jnp.exp(jax.lax.complex(real, diff.imag)), 0.0)
                scaled_B = A * bc[:, :, None]
                S_intra = jnp.einsum('btshk,bshp->bthpk', scaled_B, xc.astype(jnp.complex64))
                S_total = jnp.exp(cumlog)[:, :, :, None, :] * state[:, None] + S_intra
                y = jnp.einsum('bthk,bthpk->bthp', cc, S_total).real
                return (S_total[:, -1], y)
            _, ys = jax.lax.scan(step, state0, (chunkify(log_z), chunkify(B_c), chunkify(C_c), chunkify(x_disc)))
            y = ys.swapaxes(0, 1).reshape(Bsz, L, NHEADS, HEADDIM)
            y = y + x_ssm * D[None, None, :, None]
            y = y.reshape(Bsz, L, D_INNER)
            g = y * jax.nn.silu(z)
            g = g * jax.lax.rsqrt(jnp.mean(g * g, axis=-1, keepdims=True) + RMS_EPS) * norm_w
            return g @ out_proj_w.T
        key = jax.random.key(seed)
        ks = jax.random.split(key, 12)
        x = jax.random.normal(ks[0], (BATCH, SEQ, D_MODEL), jnp.float32)
        in_proj_w = jax.random.normal(ks[1], (D_IN_PROJ, D_MODEL), jnp.float32) * 0.02
        conv_w = jax.random.normal(ks[2], (CONV_DIM, D_CONV), jnp.float32) * 0.2
        conv_b = jnp.zeros((CONV_DIM,), jnp.float32)
        dt = jnp.exp(jax.random.uniform(ks[3], (NHEADS,)) * (math.log(0.1) - math.log(0.001)) + math.log(0.001))
        dt = jnp.maximum(dt, 0.0001)
        dt_bias = dt + jnp.log(-jnp.expm1(-dt))
        lambda_base = jax.random.uniform(ks[4], (NHEADS, NBLK), minval=1.0, maxval=16.0)
        theta_base = jax.random.uniform(ks[5], (NHEADS, NBLK), minval=-math.pi / 16, maxval=math.pi / 16)
        theta_w1 = jax.random.normal(ks[6], (D_MODEL, LORA), jnp.float32) * 0.01
        theta_w2 = jax.random.uniform(ks[7], (LORA, NHEADS * NBLK), minval=-0.01, maxval=0.01)
        viscosity_eta = jax.random.normal(ks[8], (NHEADS, NBLK), jnp.float32) * 0.01
        D = jnp.ones((NHEADS,), jnp.float32)
        norm_w = jnp.ones((D_INNER,), jnp.float32)
        out_proj_w = jax.random.normal(ks[9], (D_MODEL, D_INNER), jnp.float32) * 0.02
        return dict(x=x, in_proj_w=in_proj_w, conv_w=conv_w, conv_b=conv_b, dt_bias=dt_bias, lambda_base=lambda_base, theta_base=theta_base, theta_w1=theta_w1, theta_w2=theta_w2, viscosity_eta=viscosity_eta, D=D, norm_w=norm_w, out_proj_w=out_proj_w)
    _L0_attn_in = _L0_attn_setup()

    def _L0_ffn_setup():
        import jax, jax.numpy as jnp
        import numpy as np
        B, S, H, E = (4, 512, 256, 8)
        key = jax.random.key(seed)
        k1, k2, k3 = jax.random.split(key, 3)
        scale_w = 1.0 / np.sqrt(H)
        return {'x': jax.random.normal(k1, (B, S, H), dtype=jnp.float32), 'router_w': jax.random.normal(k2, (H, E), dtype=jnp.float32) * scale_w, 'router_b': jnp.zeros((E,), dtype=jnp.float32), 'expert_w': jax.random.normal(k3, (E, H, H), dtype=jnp.float32) * scale_w, 'expert_b': jnp.zeros((E, H), dtype=jnp.float32)}
    _L0_ffn_in = _L0_ffn_setup()
    _d = {'L0_attn_x': _L0_attn_in['x'], 'L0_attn_in_proj_w': _L0_attn_in['in_proj_w'], 'L0_attn_conv_w': _L0_attn_in['conv_w'], 'L0_attn_conv_b': _L0_attn_in['conv_b'], 'L0_attn_dt_bias': _L0_attn_in['dt_bias'], 'L0_attn_lambda_base': _L0_attn_in['lambda_base'], 'L0_attn_theta_base': _L0_attn_in['theta_base'], 'L0_attn_theta_w1': _L0_attn_in['theta_w1'], 'L0_attn_theta_w2': _L0_attn_in['theta_w2'], 'L0_attn_viscosity_eta': _L0_attn_in['viscosity_eta'], 'L0_attn_D': _L0_attn_in['D'], 'L0_attn_norm_w': _L0_attn_in['norm_w'], 'L0_attn_out_proj_w': _L0_attn_in['out_proj_w'], 'L0_ffn_router_w': _L0_ffn_in['router_w'], 'L0_ffn_router_b': _L0_ffn_in['router_b'], 'L0_ffn_expert_w': _L0_ffn_in['expert_w'], 'L0_ffn_expert_b': _L0_ffn_in['expert_b']}
    _x0 = _d['L0_attn_x']
    _d['L0_attn_x'] = jax.random.normal(jax.random.fold_in(jax.random.key(seed), 1), (8, 1024, 256), dtype=_x0.dtype)
    del _x0
    return _d

def reference(L0_attn_x, L0_attn_in_proj_w, L0_attn_conv_w, L0_attn_conv_b, L0_attn_dt_bias, L0_attn_lambda_base, L0_attn_theta_base, L0_attn_theta_w1, L0_attn_theta_w2, L0_attn_viscosity_eta, L0_attn_D, L0_attn_norm_w, L0_attn_out_proj_w, L0_ffn_router_w, L0_ffn_router_b, L0_ffn_expert_w, L0_ffn_expert_b):

    def _L0_attn_ref(x, in_proj_w, conv_w, conv_b, dt_bias, lambda_base, theta_base, theta_w1, theta_w2, viscosity_eta, D, norm_w, out_proj_w):
        import math
        import jax, jax.numpy as jnp
        import numpy as np
        D_MODEL = 256
        D_STATE = 64
        D_CONV = 4
        HEADDIM = 64
        EXPAND = 2
        NGROUPS = 1
        CHUNK = 64
        LORA = 48
        THETA_CLIP = math.pi / 2
        D_INNER = EXPAND * D_MODEL
        NHEADS = D_INNER // HEADDIM
        NBLK = D_STATE // 2
        CONV_DIM = D_INNER + 2 * NGROUPS * D_STATE
        D_IN_PROJ = 2 * D_INNER + 2 * NGROUPS * D_STATE + NHEADS
        BATCH, SEQ = (2, 512)
        RMS_EPS = 1e-05

        def _forward(x, in_proj_w, conv_w, conv_b, dt_bias, lambda_base, theta_base, theta_w1, theta_w2, viscosity_eta, D, norm_w, out_proj_w):
            Bsz, L, _ = x.shape
            zxbcdt = x @ in_proj_w.T
            z = zxbcdt[..., :D_INNER]
            xBC = zxbcdt[..., D_INNER:D_INNER + CONV_DIM]
            dt = jax.nn.softplus(zxbcdt[..., -NHEADS:] + dt_bias)
            xp = jnp.pad(xBC, ((0, 0), (D_CONV - 1, 0), (0, 0)))
            conv = conv_b
            for k in range(D_CONV):
                conv = conv + xp[:, k:k + L, :] * conv_w[:, k]
            xBC = jax.nn.silu(conv)
            x_ssm = xBC[..., :D_INNER].reshape(Bsz, L, NHEADS, HEADDIM)
            Bg = xBC[..., D_INNER:D_INNER + NGROUPS * D_STATE].reshape(Bsz, L, NGROUPS, D_STATE)
            Cg = xBC[..., D_INNER + NGROUPS * D_STATE:].reshape(Bsz, L, NGROUPS, D_STATE)
            rep = NHEADS // NGROUPS
            Bh = jnp.repeat(Bg, rep, axis=2)
            Ch = jnp.repeat(Cg, rep, axis=2)
            B_c = jax.lax.complex(Bh[..., 0::2], Bh[..., 1::2])
            C_c = jax.lax.complex(Ch[..., 0::2], Ch[..., 1::2])
            lora = jnp.tanh(x @ theta_w1) @ theta_w2
            theta = jnp.clip(theta_base[None, None] + lora.reshape(Bsz, L, NHEADS, NBLK), -THETA_CLIP, THETA_CLIP)
            lambda_eff = lambda_base[None, None] + viscosity_eta[None, None] * theta ** 2
            log_z = jax.lax.complex(-lambda_eff * dt[..., None], theta * dt[..., None])
            x_disc = x_ssm * dt[..., None]
            Nc = L // CHUNK

            def chunkify(a):
                return a.reshape(Bsz, Nc, CHUNK, *a.shape[2:]).swapaxes(0, 1)
            mask = jnp.tril(jnp.ones((CHUNK, CHUNK), bool))[None, :, :, None, None]
            state0 = jnp.zeros((Bsz, NHEADS, HEADDIM, NBLK), jnp.complex64)

            def step(state, inp):
                lz, bc, cc, xc = inp
                cumlog = jnp.cumsum(lz, axis=1)
                diff = cumlog[:, :, None] - cumlog[:, None, :]
                real = jnp.where(mask, diff.real, -60.0)
                A = jnp.where(mask, jnp.exp(jax.lax.complex(real, diff.imag)), 0.0)
                scaled_B = A * bc[:, :, None]
                S_intra = jnp.einsum('btshk,bshp->bthpk', scaled_B, xc.astype(jnp.complex64))
                S_total = jnp.exp(cumlog)[:, :, :, None, :] * state[:, None] + S_intra
                y = jnp.einsum('bthk,bthpk->bthp', cc, S_total).real
                return (S_total[:, -1], y)
            _, ys = jax.lax.scan(step, state0, (chunkify(log_z), chunkify(B_c), chunkify(C_c), chunkify(x_disc)))
            y = ys.swapaxes(0, 1).reshape(Bsz, L, NHEADS, HEADDIM)
            y = y + x_ssm * D[None, None, :, None]
            y = y.reshape(Bsz, L, D_INNER)
            g = y * jax.nn.silu(z)
            g = g * jax.lax.rsqrt(jnp.mean(g * g, axis=-1, keepdims=True) + RMS_EPS) * norm_w
            return g @ out_proj_w.T
        return _forward(x, in_proj_w, conv_w, conv_b, dt_bias, lambda_base, theta_base, theta_w1, theta_w2, viscosity_eta, D, norm_w, out_proj_w)

    def _L0_ffn_ref(x, router_w, router_b, expert_w, expert_b):
        import jax, jax.numpy as jnp
        import numpy as np
        B, S, H, E = (4, 512, 256, 8)
        b, s, h = x.shape
        xt = x.reshape(b * s, h)
        logits = xt @ router_w + router_b
        probs = jax.nn.softmax(logits, axis=-1)
        gate = jnp.max(probs, axis=-1)
        idx = jnp.argmax(probs, axis=-1)
        out_all = jnp.einsum('th,ehd->ted', xt, expert_w) + expert_b[None, :, :]
        e_out = jnp.take_along_axis(out_all, idx[:, None, None], axis=1)[:, 0, :]
        y = gate[:, None] * e_out
        return y.reshape(b, s, h)
    x = L0_attn_x
    xn = _layernorm(x, axis=-1)
    x = x + _L0_attn_ref(xn, L0_attn_in_proj_w, L0_attn_conv_w, L0_attn_conv_b, L0_attn_dt_bias, L0_attn_lambda_base, L0_attn_theta_base, L0_attn_theta_w1, L0_attn_theta_w2, L0_attn_viscosity_eta, L0_attn_D, L0_attn_norm_w, L0_attn_out_proj_w) + _L0_ffn_ref(xn, L0_ffn_router_w, L0_ffn_router_b, L0_ffn_expert_w, L0_ffn_expert_b)
    return x

_drawn_inputs = setup_inputs


def setup_inputs(seed=0):
    import zlib

    import numpy as np

    out = dict(_drawn_inputs(seed))
    spreads = {'L0_attn_conv_b': (0.0, 0.1),
     'L0_attn_D': (1.0, 0.2),
     'L0_attn_norm_w': (1.0, 0.2),
     'L0_ffn_router_b': (0.0, 0.1),
     'L0_ffn_expert_b': (0.0, 0.1)}
    factors = {'L0_attn_dt_bias': 64.0,
     'L0_attn_lambda_base': 8.0,
     'L0_attn_theta_base': 8.0,
     'L0_attn_theta_w1': 8.0,
     'L0_attn_theta_w2': 8.0,
     'L0_attn_viscosity_eta': 8.0}
    for name, (base, spread) in spreads.items():
        noise = np.random.default_rng([zlib.crc32(name.encode()), seed]).standard_normal(out[name].shape)
        drawn = base * np.exp(spread * noise) if base else spread * noise
        out[name] = jnp.asarray(drawn.astype(out[name].dtype))
    for name, factor in factors.items():
        out[name] = (out[name] * factor).astype(out[name].dtype)
    return out
```

```python
import concourse.bass as bass
from concourse import mybir
from contextlib import ExitStack
import math

F32 = mybir.dt.float32
I32 = mybir.dt.int32
ALU = mybir.AluOpType
ACT = mybir.ActivationFunctionType
AX_X = mybir.AxisListType.X

P = 128
BATCH, SEQ, D_MODEL = 8, 1024, 256
TOKENS = BATCH * SEQ
KT = D_MODEL // P
D_INNER, HEADS, HEADDIM, NBLK, LORA, D_CONV = 512, 8, 64, 32, 48, 4
PAIRS = HEADS // 2
TILES = TOKENS // P
EXPERTS = 8
SLOT_TILES = TILES + EXPERTS
SLOTS = SLOT_TILES * P
MT = 256
TPM = MT // P
CH = 64
CPT, CPM = P // CH, MT // CH
MPS = SEQ // MT
MACROS = TOKENS // MT
XBC_T = 5
GROUP = 4
LN_EPS, RMS_EPS = 1e-5, 1e-5
ROUND = 1.5 * 2.0 ** 23
TWO_PI = 2.0 * math.pi
MAX_DECAY = 60.0
LEVELS = int(math.log2(CH))
TRIG = TWO_PI * (1.0 - 2.0 ** -22)

CONST, _at = {}, 0
for _n, _w in (("ident", P), ("causal", P), ("before", P), ("ones", P), ("restart", MT), ("tilestart", TILES * EXPERTS),
               ("first", EXPERTS), ("slot", SLOT_TILES), ("quarter", 1), ("halfpi", 1), ("minushalf", 8), ("ownhead", 2)):
    CONST[_n] = (_at, _w)
    _at += _w
CONST_W = _at
COLS, _at = {}, 0
for _n, _w in (("conv_w", XBC_T * D_CONV), ("conv_b", XBC_T), ("D", PAIRS), ("norm_w", PAIRS), ("lb", PAIRS), ("eta", PAIRS)):
    COLS[_n] = (_at, _w)
    _at += _w
COLS_W = _at


def mixer_and_experts(nc, x, const, halvings, cols, w_in, w_small, w_lora1, w_lora2, w_out, rows, w_exp, b_exp, out):
    ctx = ExitStack()
    with ctx:
        def sb(name, shape, dt=F32):
            return ctx.enter_context(nc.sbuf_tensor(name, shape, dt))

        def sem(name):
            return ctx.enter_context(nc.semaphore(name))

        def scratch(name, shape):
            return nc.dram_tensor(name, shape, F32, kind="Internal").ap()

        xnT_d = scratch("xnT_d", (P, KT, TOKENS))
        dtT_d = scratch("dtT_d", (HEADS, TOKENS))
        table_d = scratch("table_d", (SLOTS, D_MODEL))
        expert_d = scratch("expert_d", (SLOTS, D_MODEL))

        cst = sb("cst", [P, CONST_W])
        col = sb("col", [P, COLS_W])
        win = sb("win", [P, KT, (XBC_T + PAIRS) * P])
        wsm = sb("wsm", [P, KT, 2 * HEADS])
        wl1 = sb("wl1", [P, KT, LORA])
        wl2 = sb("wl2", [LORA + 1, PAIRS * P])
        wout = sb("wout", [P, PAIRS, D_MODEL])
        rowc = sb("rowc", [P, 2 * HEADS])
        eta2 = sb("eta2", [P, PAIRS])
        dt_tok = sb("dt_tok", [P, TILES, HEADS])
        gate = sb("gate", [P, TILES])
        slot_of = sb("slot_of", [P, TILES], I32)
        tile_expert = sb("tile_expert", [P, SLOT_TILES], I32)
        halve = sb("halve", [P, 1], I32)

        class Region:

            def __init__(self, name, width):
                self.t, self.width, self.at = sb(name, [P, width]), width, 0

            def again(self):
                self.at = 0

            def take(self, *dims):
                n = math.prod(dims)
                assert self.at + n <= self.width
                v = self.t[:, self.at:self.at + n]
                self.at += n
                if len(dims) == 2:
                    v = v.rearrange("p (a b) -> p a b", a=dims[0])
                if len(dims) == 3:
                    v = v.rearrange("p (a b c) -> p a b c", a=dims[0], b=dims[1])
                return v

        r_tokens, r_route = Region("r_tokens", TILES * D_MODEL), Region("r_route", 6144)
        r_tiles, r_expw = Region("r_tiles", 6144), Region("r_expw", 6144)
        r_mixer = Region("r_mixer", 5200)

        pst = [ctx.enter_context(nc.psum_tensor(f"ps{n}", [P, 2, 512], F32)) for n in range(4)]

        def bank(n):
            return pst[n // 2][:, n % 2, :]

        def k(name):
            a, w = CONST[name]
            return cst[:, a:a + w]

        def c(name, n=0, w=1):
            a = COLS[name][0] + n
            return col[:, a:a + w]

        ident = k("ident")

        xn_all = r_tokens.take(TILES, D_MODEL)
        logits = r_route.take(TILES, EXPERTS)
        a_in = [r_tiles.take(GROUP, D_MODEL) for _ in range(2)]
        a_xn = [r_tiles.take(GROUP, D_MODEL) for _ in range(2)]
        a_xT = [r_tiles.take(KT, GROUP * P) for _ in range(2)]
        stats = sb("stats", [P, GROUP, nc.vector.BN_STATS_DIM])
        mv = sb("mv", [P, GROUP, nc.vector.BN_AGGR_DIM])
        veps = sb("veps", [P, GROUP])
        rstd = [sb(f"rstd{b}", [P, GROUP]) for b in range(2)]
        shift = [sb(f"shift{b}", [P, GROUP]) for b in range(2)]

        weights_in = sem("weights_in")
        N_WEIGHTS = 9
        a_loaded = [sem(f"a_loaded{b}") for b in range(2)]
        a_stats, a_mv, a_veps, a_rstd = sem("a_stats"), sem("a_mv"), sem("a_veps"), sem("a_rstd")
        a_shift, a_norm, a_kept = sem("a_shift"), [sem(f"a_norm{b}") for b in range(2)], [sem(f"a_kept{b}") for b in range(2)]
        a_turned, a_evac = [sem(f"a_turned{b}") for b in range(2)], [sem(f"a_evac{b}") for b in range(2)]
        a_small, a_read = [sem(f"a_small{b}") for b in range(2)], [sem(f"a_read{b}") for b in range(2)]
        a_stored = [sem(f"a_stored{b}") for b in range(2)]
        passed = sem("passed")
        pads_zero, zeroed = sem("pads_zero"), sem("zeroed")

        GROUPS = TILES // GROUP
        HALF = GROUPS // 2
        GT = GROUP * P
        a_T = [pst[0], pst[1]]
        a_S = [bank(4), bank(5)]

        with nc.Block() as block:
            @block.sync
            def _(sp):
                for dst, src in ((cst[:, :], const), (col[:, :], cols), (win[:, :, :], w_in), (wsm[:, :, :], w_small),
                                 (wl1[:, :, :], w_lora1), (wl2[:, :], w_lora2), (wout[:, :, :], w_out),
                                 (rowc[:, 0:HEADS], rows[0:1, 0:HEADS].broadcast_to([P, HEADS])),
                                 (rowc[:, HEADS:], rows[0:1, HEADS:2 * HEADS].broadcast_to([P, HEADS]))):
                    sp.dma_start(dst, src).then_inc(weights_in, 16)
                with sp.Fori(0, HALF) as i:
                    for b in range(2):
                        g = 2 * i + b
                        sp.wait_ge(a_norm[b], GROUP * i)
                        sp.wait_ge(a_kept[b], GROUP * i)
                        sp.dma_start(a_in[b], x[bass.ds(g * GT, GT), :].rearrange("(t p) d -> p t d", p=P)).then_inc(a_loaded[b], 16)

            @block.vector
            def _(dve):
                with dve.Fori(0, HALF) as i:
                    for b in range(2):
                        g = 2 * i + b
                        dve.wait_ge(a_loaded[b], 16 * i + 16)
                        for t in range(GROUP):
                            nc.vector.bn_stats(stats[:, t, :], a_in[b][:, t, :]).then_inc(a_stats, 1)
                        for t in range(GROUP):
                            if t == 0:
                                dve.wait_ge(a_stats, GROUP * (g + 1))
                                dve.sem_inc(passed, 1)
                            nc.vector.bn_aggr(mv[:, t, :], stats[:, t, :]).then_inc(a_mv, 1)
                        dve.wait_ge(a_mv, GROUP * (g + 1))
                        dve.wait_ge(a_rstd, g)
                        nc.vector.tensor_scalar(veps[:, :], mv[:, :, 1], LN_EPS, None, ALU.add).then_inc(a_veps, 1)
                        dve.wait_ge(a_rstd, g + 1)
                        dve.wait_ge(a_kept[b], GROUP * i)
                        nc.vector.scalar_tensor_tensor(shift[b][:, :], mv[:, :, 0], -1.0, rstd[b][:, :], ALU.mult, ALU.mult).then_inc(a_shift, 1)
                        dve.wait_ge(a_shift, g + 1)
                        dve.wait_ge(a_turned[b], i)
                        for t in range(GROUP):
                            nc.vector.tensor_scalar(a_xn[b][:, t, :], a_in[b][:, t, :], rstd[b][:, t:t + 1], shift[b][:, t:t + 1],
                                                    ALU.mult, ALU.add).then_inc(a_norm[b], 1)
                        dve.wait_ge(a_small[b], i + 1)
                        dve.wait_ge(weights_in, 16 * N_WEIGHTS)
                        small = a_S[b][:, 0:GROUP * 2 * HEADS].rearrange("p (t e) -> p t e", t=GROUP)
                        nc.vector.tensor_tensor(dt_tok[:, bass.ds(g * GROUP, GROUP), :], small[:, :, 0:HEADS],
                                                rowc[:, None, 0:HEADS].broadcast_to([P, GROUP, HEADS]), ALU.add).then_inc(a_read[b], 1)
                        nc.vector.tensor_tensor(logits[:, bass.ds(g * GROUP, GROUP), :], small[:, :, HEADS:],
                                                rowc[:, None, HEADS:].broadcast_to([P, GROUP, HEADS]), ALU.add).then_inc(a_read[b], 1)

            @block.gpsimd
            def _(pool):
                pool.memset(r_expw.t[:, 0:2048], 0.0).then_inc(zeroed, 1)
                pool.wait_ge(weights_in, 16 * N_WEIGHTS)
                with pool.Fori(0, HALF) as i:
                    for b in range(2):
                        g = 2 * i + b
                        pool.wait_ge(a_veps, g + 1)
                        pool.wait_ge(a_norm[b], GROUP * i)
                        pool.wait_ge(a_kept[b], GROUP * i)
                        nc.gpsimd.tensor_tensor(rstd[b][:, :], veps[:, :], k("minushalf")[:, 0:GROUP], ALU.pow).then_inc(a_rstd, 1)

            @block.scalar
            def _(act):
                act.wait_ge(zeroed, 1)
                for n in range(SLOT_TILES // 8):
                    act.dma_start(table_d[n * 8 * P:(n + 1) * 8 * P, :].rearrange("(t p) d -> p t d", p=P),
                                  r_expw.t[:, 0:2048].rearrange("p (t d) -> p t d", t=8)).then_inc(pads_zero, 16)
                act.wait_ge(weights_in, 16 * N_WEIGHTS)
                with act.Fori(0, HALF) as i:
                    for b in range(2):
                        g = 2 * i + b
                        act.wait_ge(a_shift, g + 1)
                        act.sem_inc(passed, 1)
                        for t in range(GROUP):
                            nc.scalar.activation(xn_all[:, bass.ds(g * GROUP + t, 1), :], a_in[b][:, t:t + 1, :], ACT.Identity,
                                                 bias=shift[b][:, t:t + 1], scale=rstd[b][:, t:t + 1]).then_inc(a_kept[b], 1)
                        act.wait_ge(a_turned[b], i + 1)
                        act.wait_ge(a_stored[b], 16 * i)
                        act.wait_ge(a_small[b], i)
                        nc.scalar.activation(a_xT[b], a_T[b][:, :, :], ACT.Copy).then_inc(a_evac[b], 1)
                        act.wait_ge(a_evac[b], i + 1)
                        act.dma_start(xnT_d[:, :, bass.ds(g * GT, GT)], a_xT[b]).then_inc(a_stored[b], 16)
                for b in range(2):
                    act.wait_ge(a_stored[b], 16 * HALF)
                act.wait_ge(pads_zero, 16 * (SLOT_TILES // 8))

            @block.tensor
            def _(pe):
                pe.wait_ge(weights_in, 16 * N_WEIGHTS)
                with pe.Fori(0, HALF) as i:
                    for b in range(2):
                        pe.wait_ge(a_norm[b], GROUP * (i + 1))
                        pe.wait_ge(a_evac[b], i)
                        for kt in range(KT):
                            for t in range(GROUP):
                                last = nc.tensor.transpose(a_T[b][:, kt, t * P:(t + 1) * P], a_xn[b][:, t, kt * P:(kt + 1) * P], ident)
                        last.then_inc(a_turned[b], 1)
                        pe.wait_ge(a_evac[b], i + 1)
                        pe.wait_ge(a_read[b], 2 * i)
                        for t in range(GROUP):
                            for kt in range(KT):
                                last = nc.tensor.matmul(a_S[b][:, t * 2 * HEADS:(t + 1) * 2 * HEADS], a_xT[b][:, kt, t * P:(t + 1) * P],
                                                        wsm[:, kt, :], start=(kt == 0), stop=(kt == KT - 1))
                        last.then_inc(a_small[b], 1)

        TE = TILES * EXPERTS
        r_route.again()
        logits = r_route.take(TILES, EXPERTS)
        f1, f2, f3, f4, f5, onehot = (r_route.take(TILES, EXPERTS) for _ in range(6))
        incl = r_route.take(EXPERTS, TILES)
        dtT = r_route.take(4, P)
        t64 = [r_route.take(TILES) for _ in range(4)]
        e8 = [r_route.take(EXPERTS) for _ in range(6)]
        ge = r_route.take(SLOT_TILES, EXPERTS)
        ends = r_route.take(SLOT_TILES)
        most = r_route.take(EXPERTS)
        lam_rows = r_tiles.t[:, 0:2 * HEADS * NBLK].rearrange("p (n h k) -> p n h k", n=2, h=HEADS)
        e8i = sb("e8i", [P, EXPERTS], I32)
        rv, ra, rp, scattered, dt_stored, r_ew = (sem(n) for n in ("rv", "ra", "rp", "scattered", "dt_stored", "r_ew"))
        w8 = r_expw.take(KT * EXPERTS, D_MODEL)
        b8 = r_expw.take(EXPERTS, D_MODEL)

        def over(v, *shape):
            return v.broadcast_to([P, *shape])

        with nc.Block() as block:
            @block.sync
            def _(sp):
                sp.dma_start(w8, w_exp).then_inc(r_ew, 16)
                sp.dma_start(b8, b_exp.rearrange("e d -> (e d)")[None, :].broadcast_to([P, EXPERTS * D_MODEL]).rearrange("p (e d) -> p e d", e=EXPERTS)).then_inc(r_ew, 16)
                sp.dma_start(r_tiles.t[:, 0:2 * HEADS * NBLK], rows[0:1, 2 * HEADS:].broadcast_to([P, 2 * HEADS * NBLK])).then_inc(r_ew, 16)
                sp.wait_ge(ra, 3)
                for n in range(4):
                    sp.dma_start(dtT_d[:, n * 16 * P:(n + 1) * 16 * P].rearrange("h (t s) -> t h s", s=P),
                                 dtT[:, n, :]).then_inc(dt_stored, 16)
                sp.wait_ge(dt_stored, 64)
                sp.wait_ge(r_ew, 48)

            @block.vector
            def _(dve):
                done = [0]

                def step(ins):
                    done[0] += 1
                    ins.then_inc(rv, 1)
                    dve.wait_ge(rv, done[0])

                u = dt_tok[:, :, :]
                step(nc.vector.scalar_tensor_tensor(f1, u, -1.0, u, ALU.mult, ALU.max))
                step(nc.vector.tensor_reduce(t64[0], logits, AX_X, ALU.max))
                step(nc.vector.tensor_tensor(f2, logits, over(t64[0][:, :, None], TILES, EXPERTS), ALU.subtract))
                dve.wait_ge(ra, 1)
                step(nc.vector.tensor_scalar(f4, f3, 1.0, None, ALU.add))
                step(nc.vector.tensor_scalar(f5, f4, -1.0, 2.0 ** -24, ALU.add, ALU.max))
                step(nc.vector.reciprocal(f5, f5))
                step(nc.vector.tensor_tensor(f5, f5, f3, ALU.mult))
                step(nc.vector.tensor_scalar(f1, f4, 1.0, None, ALU.is_equal))
                dve.wait_ge(ra, 2)
                step(nc.vector.tensor_tensor(f4, f4, f5, ALU.mult))
                step(nc.vector.tensor_tensor(f1, f1, f3, ALU.mult))
                step(nc.vector.tensor_tensor(f4, f4, f1, ALU.max))
                step(nc.vector.scalar_tensor_tensor(u, u, 0.0, f4, ALU.max, ALU.add))
                step(nc.vector.tensor_reduce(t64[1], onehot, AX_X, ALU.add))
                step(nc.vector.reciprocal(gate[:, :], t64[1]))
                step(nc.vector.tensor_tensor(f1, logits, over(t64[0][:, :, None], TILES, EXPERTS), ALU.is_equal))
                step(nc.vector.tensor_tensor(f1, f1, over(k("first")[:, None, :], TILES, EXPERTS), ALU.mult))
                step(nc.vector.tensor_reduce(t64[2], f1, AX_X, ALU.max))
                step(nc.vector.tensor_tensor(onehot, f1, over(t64[2][:, :, None], TILES, EXPERTS), ALU.is_equal))
                assert done[0] == 18
                dve.wait_ge(rp, 2)
                step(nc.vector.tensor_copy(f2.rearrange("p t e -> p (t e)"), bank(3)))
                by_expert = bank(2).rearrange("p (t e) -> p e t", t=TILES)
                step(nc.vector.tensor_copy(f3.rearrange("p a b -> p (a b)").rearrange("p (e t) -> p e t", e=EXPERTS), by_expert))
                counts = f3.rearrange("p a b -> p (a b)")
                step(nc.vector.tensor_tensor_scan(incl.rearrange("p e t -> p (e t)"), k("tilestart"), counts, 0.0, ALU.mult, ALU.add))
                step(nc.vector.tensor_scalar(e8[0], incl[:, :, TILES - 1], float(P - 1), None, ALU.add))
                step(nc.vector.tensor_copy(e8i[:, :], e8[0]))
                step(nc.vector.tensor_scalar(e8i[:, :], e8i[:, :], int(math.log2(P)), None, ALU.logical_shift_right))
                step(nc.vector.tensor_copy(e8[1], e8i[:, :]))
                step(nc.vector.tensor_tensor_scan(e8[2], k("ones")[:, 0:EXPERTS], e8[1], 0.0, ALU.mult, ALU.add))
                step(nc.vector.tensor_tensor(e8[3], e8[2], e8[1], ALU.subtract))
                step(nc.vector.tensor_scalar(e8[3], e8[3], float(P), None, ALU.mult))
                step(nc.vector.tensor_tensor(f4.rearrange("p a b -> p (a b)"), incl.rearrange("p e t -> p (e t)"), counts, ALU.subtract))
                earlier = f4.rearrange("p a b -> p (a b)").rearrange("p (e t) -> p t e", e=EXPERTS)
                step(nc.vector.tensor_tensor(f2, f2, earlier, ALU.add))
                step(nc.vector.tensor_tensor(f2, f2, over(e8[3][:, None, :], TILES, EXPERTS), ALU.add))
                step(nc.vector.tensor_tensor(f2, f2, onehot, ALU.mult))
                step(nc.vector.tensor_reduce(t64[3], f2, AX_X, ALU.add))
                step(nc.vector.tensor_copy(slot_of[:, :], t64[3]))
                assert done[0] == 34
                step(nc.vector.tensor_tensor(ge, over(k("slot")[:, :, None], SLOT_TILES, EXPERTS), over(e8[2][:, None, :], SLOT_TILES, EXPERTS), ALU.is_ge))
                step(nc.vector.tensor_reduce(ends, ge, AX_X, ALU.add))
                step(nc.vector.tensor_scalar(ends, ends, float(EXPERTS - 1), None, ALU.min))
                step(nc.vector.tensor_copy(tile_expert[:, :], ends))
                dve.wait_ge(r_ew, 48)
                for n in range(2):
                    step(nc.vector.scalar_tensor_tensor(lam_rows[:, n], lam_rows[:, n], -1.0, lam_rows[:, n], ALU.mult, ALU.max))
                step(nc.vector.scalar_tensor_tensor(lam_rows[:, 0], lam_rows[:, 1], (math.pi / 2) ** 2, lam_rows[:, 0], ALU.mult, ALU.add))
                step(nc.vector.tensor_reduce(most, lam_rows[:, 0], AX_X, ALU.max))
                dve.wait_ge(rp, 4)
                step(nc.vector.tensor_tensor(f1, bank(5).rearrange("p (t h) -> p t h", t=TILES), over(most[:, None, :], TILES, HEADS), ALU.mult))
                step(nc.vector.tensor_reduce(t64[0][:, 0:1], f1.rearrange("p t h -> p (t h)"), AX_X, ALU.max))
                step(nc.vector.tensor_scalar(t64[0][:, 0:1], t64[0][:, 0:1], MAX_DECAY, None, ALU.is_gt))
                step(nc.vector.tensor_copy(halve[:, :], t64[0][:, 0:1]))
                step(nc.vector.tensor_scalar(wl2[:, :], wl2[:, :], 1.0 / TWO_PI, None, ALU.mult))
                for q in range(PAIRS):
                    step(nc.vector.tensor_scalar(wout[:, q, :], wout[:, q, :], c("norm_w", q), None, ALU.mult))

            @block.scalar
            def _(act):
                act.wait_ge(rv, 1)
                nc.scalar.activation(f3, f1, ACT.Exp, scale=-1.0).then_inc(ra, 1)
                act.wait_ge(rv, 8)
                nc.scalar.activation(onehot, f2, ACT.Exp)
                nc.scalar.activation(f4, f4, ACT.Ln).then_inc(ra, 1)
                act.wait_ge(rp, 3)
                nc.scalar.activation(dtT.rearrange("p n s -> p (n s)"), bank(4), ACT.Copy).then_inc(ra, 1)

            @block.tensor
            def _(pe):
                pe.wait_ge(rv, 18)
                flat = onehot.rearrange("p t e -> p (t e)")
                nc.tensor.matmul(bank(3), k("before"), flat, start=True, stop=True).then_inc(rp, 1)
                nc.tensor.matmul(bank(2), k("ones"), flat, start=True, stop=True).then_inc(rp, 1)
                dt_flat = dt_tok[:, :, :].rearrange("p t h -> p (t h)")
                for n in range(4):
                    last = nc.tensor.transpose(bank(4)[:, n * P:(n + 1) * P], dt_flat[:, n * P:(n + 1) * P], ident)
                last.then_inc(rp, 1)
                nc.tensor.matmul(bank(5), k("ones"), dt_flat, start=True, stop=True).then_inc(rp, 1)

            @block.gpsimd
            def _(pool):
                pool.wait_ge(rv, 34)
                for t in range(TILES):
                    pool.indirect_dma_start(table_d, bass.IndirectOffsetOnAxis(ap=slot_of[:, t:t + 1], axis=0), xn_all[:, t, :], None).then_inc(scattered, 16)
                pool.wait_ge(scattered, 16 * TILES)

        r_tiles.again()
        e_in = [r_tiles.take(GROUP, D_MODEL) for _ in range(2)]
        e_xT = [r_tiles.take(KT, GROUP * P) for _ in range(2)]
        e_out = [r_tiles.take(GROUP, D_MODEL) for _ in range(2)]
        e_loaded, e_turned, e_evac, e_mm, e_added, e_stored = ([sem(f"{n}{b}") for b in range(2)] for n in (
            "e_loaded", "e_turned", "e_evac", "e_mm", "e_added", "e_stored"))
        E_HALF = SLOT_TILES // GROUP // 2
        e_T = [pst[0], pst[1]]
        e_Y = [pst[2], pst[3]]

        with nc.Block() as block:
            @block.sync
            def _(sp):
                with sp.Fori(0, E_HALF) as i:
                    for b in range(2):
                        sp.wait_ge(e_turned[b], i)
                        sp.dma_start(e_in[b], table_d[bass.ds((2 * i + b) * GT, GT), :].rearrange("(t p) d -> p t d", p=P)).then_inc(e_loaded[b], 16)

            @block.tensor
            def _(pe):
                with pe.Fori(0, E_HALF) as i:
                    for b in range(2):
                        pe.wait_ge(e_loaded[b], 16 * i + 16)
                        pe.wait_ge(e_evac[b], i)
                        for t in range(GROUP):
                            for kt in range(KT):
                                last = nc.tensor.transpose(e_T[b][:, kt, t * P:(t + 1) * P], e_in[b][:, t, kt * P:(kt + 1) * P], ident)
                        last.then_inc(e_turned[b], 1)
                    for b in range(2):
                        pe.wait_ge(e_evac[b], i + 1)
                        pe.wait_ge(e_added[b], GROUP * i)
                        for t in range(GROUP):
                            e = pe.value_load(tile_expert[0:1, bass.ds((2 * i + b) * GROUP + t, 1)], min_val=0, max_val=EXPERTS - 1)
                            for kt in range(KT):
                                last = nc.tensor.matmul(e_Y[b][:, t // 2, (t % 2) * D_MODEL:(t % 2 + 1) * D_MODEL],
                                                        e_xT[b][:, kt, t * P:(t + 1) * P],
                                                        w8[:, bass.ds(e + kt * EXPERTS, 1), :].rearrange("p o d -> p (o d)"),
                                                        start=(kt == 0), stop=(kt == KT - 1))
                        last.then_inc(e_mm[b], 1)

            @block.scalar
            def _(act):
                with act.Fori(0, E_HALF) as i:
                    for b in range(2):
                        act.wait_ge(e_turned[b], i + 1)
                        act.wait_ge(e_mm[b], i)
                        nc.scalar.activation(e_xT[b], e_T[b][:, :, :], ACT.Copy).then_inc(e_evac[b], 1)
                    for b in range(2):
                        act.wait_ge(e_added[b], GROUP * (i + 1))
                        act.dma_start(expert_d[bass.ds((2 * i + b) * GT, GT), :].rearrange("(t p) d -> p t d", p=P), e_out[b]).then_inc(e_stored[b], 16)
                for b in range(2):
                    act.wait_ge(e_stored[b], 16 * E_HALF)

            @block.vector
            def _(dve):
                with dve.Fori(0, E_HALF) as i:
                    for b in range(2):
                        dve.wait_ge(e_mm[b], i + 1)
                        dve.wait_ge(e_stored[b], 16 * i)
                        for t in range(GROUP):
                            e = dve.value_load(tile_expert[0:1, bass.ds((2 * i + b) * GROUP + t, 1)], min_val=0, max_val=EXPERTS - 1)
                            nc.vector.tensor_tensor(e_out[b][:, t, :], e_Y[b][:, t // 2, (t % 2) * D_MODEL:(t % 2 + 1) * D_MODEL],
                                                    b8[:, bass.ds(e, 1), :].rearrange("p o d -> p (o d)"), ALU.add).then_inc(e_added[b], 1)

        r_tokens.again(), r_route.again(), r_tiles.again(), r_expw.again()
        theta, lam, decay, phase, frac, whole, wave, eneg = (r_tokens.take(PAIRS, MT) for _ in range(8))
        quad = whole
        wave_dec, quad_dec, quad_grow = theta, lam, phase
        rep = r_expw.take(6, MT)
        c_in = [r_tokens.take(PAIRS, MT) for _ in range(2)]
        c_own = [r_tokens.take(PAIRS, MT) for _ in range(2)]
        grow = [r_tokens.take(PAIRS, MT) for _ in range(2)]
        b_up = [r_tokens.take(PAIRS, MT) for _ in range(2)]
        z_gate = [r_route.take(PAIRS, MT) for _ in range(2)]
        x_skip = [r_route.take(PAIRS, MT) for _ in range(2)]
        x_dt = [r_route.take(TPM, D_INNER) for _ in range(2)]
        end_dec = sb("end_dec", [P, CPM, PAIRS])
        head_dec = [sb(f"head_dec{b}", [P, CPM, PAIRS * 2]) for b in range(2)]
        x_pre = [r_expw.take(XBC_T, MT + D_CONV - 1) for _ in range(2)]
        conv = r_expw.take(XBC_T, MT)
        xbc = r_mixer.take(XBC_T, MT)
        xn_in = [r_mixer.take(KT, MT) for _ in range(2)]
        dt_in = [r_mixer.take(PAIRS, MT) for _ in range(2)]
        zero_dec = sb("zero_dec", [P, PAIRS * 2])
        cb_part = [sb(f"cb_part{n}", [P, MT])[:, :] for n in range(2)]
        hidden = sb("hidden", [LORA + 1, MT])
        b_tok = [r_tiles.take(PAIRS, P) for _ in range(2)]
        att = [r_tiles.take(HEADS, P) for _ in range(2)]
        g = [r_tiles.take(PAIRS, P) for _ in range(2)]
        gsq = r_tiles.take(PAIRS, P)
        state_in = [sb(f"state_in{b}", [P, PAIRS, P]) for b in range(2)]
        state = sb("state", [P, PAIRS, HEADDIM])
        level_signs, level_masks = r_mixer.take(LEVELS, P), r_tiles.take(LEVELS + 1, P)
        part_att = conv[:, 0:2, :].rearrange("p n (a t) -> p (n a) t", a=2)
        level_e, level_b, level_c = ([v[1][:, :, n * P:(n + 1) * P] for n in range(2)] for v in (b_up, c_in, c_own))
        x_tile = [sb(f"x_tile{b}", [P, D_MODEL]) for b in range(2)]
        e_tile = [sb(f"e_tile{b}", [P, D_MODEL]) for b in range(2)]
        o_tile = [sb(f"o_tile{b}", [P, D_MODEL]) for b in range(2)]
        e_index = [sb(f"e_index{b}", [P, 1], I32) for b in range(2)]
        ms = [sb(f"ms{b}", [P, 1]) for b in range(2)]
        rms = [sb(f"rms{b}", [P, 1]) for b in range(2)]

        bank_a, bank_b, bank_t, bank_u = bank(0), bank(1), bank(2), bank(3)
        bank_s, bank_y, bank_o = pst[2], bank(6), bank(7)

        made = {n: sem(n) for n in (
            "xproj", "zproj", "thproj",
            "xturned",
            "bturned", "scored", "yout", "oproj",
            "upd",
            "xevac", "zevac",
            "lamsq", "lamd",
            "silu",
            "trig", "negd", "expd",
            "bevac", "squared",
            "fabs",
            "halo", "convd",
            "clipped", "rsum", "psum", "rounded",
            "xdt",
            "grown", "bup", "wavedec", "cwave", "cin", "dwave", "cown",
            "masked", "gated", "gsum", "meansq", "xplus", "final",
            "stated",
            "angle", "lamdt", "fracd", "xd", "xskip", "headdec",
            "cb",
            "quadgrow", "bquad", "quaddec", "cquad", "dquad",
            "rmsd", "eidx",
            "statein",
            "repd",
            "tail",
            "apart", "signed", "lcdec", "lmasked",
            "lsum",
            "lexpd",
            "lbdec",
            "lscored",
        )}
        s = made
        xn_loaded, dt_loaded = [sem(f"xn_loaded{b}") for b in range(2)], [sem(f"dt_loaded{b}") for b in range(2)]
        x_loaded, e_loaded2, o_stored = ([sem(f"{n}{b}") for b in range(2)] for n in ("x_loaded", "e_gathered", "o_stored"))
        m_ready, m_zero, table_in = sem("m_ready"), sem("m_zero"), sem("table_in")

        REPS = 16

        def expand(v, *shape):
            return v.broadcast_to([v.shape[0], *shape])



        def two_ago(m, halved, per):
            if halved:
                return per * m
            return per * (m - 1) if not (isinstance(m, int) and m == 0) else 0

        def reference(v, ch, level):
            half = CH >> (level + 1)
            blocks = v[:, :, ch * P:(ch + 1) * P].rearrange("p q (n w) -> p q n w", w=2 * half)
            return [blocks[:, q] for q in range(PAIRS)], [blocks[:, q, :, half - 1:half].broadcast_to([P, P // (2 * half), 2 * half]) for q in range(PAIRS)]

        def sync_mixer(sp, halved):
            def load(i, j, first=False):
                m, b = MPS * i + j, j % 2
                if not first:
                    sp.wait_ge(s["zproj"], two_ago(m, halved, 2))
                    sp.wait_ge(s["lamdt"], two_ago(m, halved, 1))
                    sp.wait_ge(s["angle"], two_ago(m, halved, 1))
                    sp.sem_inc(passed, 1)
                sp.dma_start(xn_in[b], xnT_d[:, :, bass.ds(m * MT, MT)]).then_inc(xn_loaded[b], 16)
                for e in range(2):
                    src = dtT_d.rearrange("(q e) t -> e q t", e=2)[e:e + 1, :, bass.ds(m * MT, MT)]
                    sp.dma_start(dt_in[b][e * HEADDIM:(e + 1) * HEADDIM, :, :],
                                 src.broadcast_to([HEADDIM, PAIRS, MT])).then_inc(dt_loaded[b], 16)

            def replicate(i, j):
                m = MPS * i + j
                sp.wait_ge(s["cown"], m)
                sp.sem_inc(passed, 1)
                sp.wait_ge(s["silu"], m + 1)
                for n, base in enumerate((2, 3, 0, 1)):
                    for at in range(0, P, NBLK):
                        sp.dma_start(rep[at:at + NBLK, n, :], xbc[base * NBLK:(base + 1) * NBLK, XBC_T - 1, :]).then_inc(s["repd"], 16)

            def load_x(i, j, ch):
                t = (MPS * i + j) * TPM + ch
                n = MPS * i + j
                sp.wait_ge(s["xplus"], TPM * n)
                sp.dma_start(x_tile[ch][:, :], x[bass.ds(t * P, P), :]).then_inc(x_loaded[ch], 16)

            def store(i, j, ch):
                t = (MPS * i + j) * TPM + ch
                sp.wait_ge(s["final"], t + 1)
                sp.dma_start(out[bass.ds(t * P, P), :], o_tile[ch][:, :]).then_inc(o_stored[ch], 16)

            def body(i, js, last):
                for j in js:
                    for ch in range(TPM):
                        load_x(i, j, ch)
                    if not (last and j == MPS - 1):
                        replicate(i, j + 1)
                    if not (last and j >= MPS - 2):
                        load(i, j + 2)
                    for ch in range(TPM):
                        store(i, j, ch)

            if halved:
                sp.dma_start(level_signs, halvings[:, 0:LEVELS, :]).then_inc(table_in, 16)
                sp.dma_start(level_masks, halvings[:, LEVELS:, :]).then_inc(table_in, 16)
                sp.wait_ge(table_in, 32)
                with sp.Fori(0, BATCH) as i:
                    for j in range(MPS):
                        load(i, j)
                        replicate(i, j)
                        for ch in range(TPM):
                            load_x(i, j, ch)
                        for ch in range(TPM):
                            store(i, j, ch)
            else:
                load(0, 0, True)
                load(0, 1, True)
                replicate(0, 0)
                with sp.Fori(0, BATCH - 1) as i:
                    body(i, range(MPS), False)
                body(BATCH - 1, range(MPS), True)
            for ch in range(TPM):
                sp.wait_ge(o_stored[ch], 16 * MACROS)

        def tensor_mixer(pe, halved):
            epos = grow[1] if halved else decay

            def parity(j):
                return 0 if halved else j % 2

            def project(dst, n, b):
                for kt in range(KT):
                    last = nc.tensor.matmul(dst, win[:, kt, n * P:(n + 1) * P], xn_in[b][:, kt, :], start=(kt == 0), stop=(kt == KT - 1))
                return last

            def front_x(i, j):
                m, n, b = MPS * i + j, 2 * i + j // 2, j % 2
                pe.wait_ge(xn_loaded[b], 16 * n + 16)
                pe.wait_ge(s["zevac"], 2 * m)
                project(bank_a[:, 0:MT], 0, b)
                project(bank_a[:, MT:], 1, b).then_inc(s["xproj"], 1)
                project(bank_b[:, 0:MT], 2, b)
                project(bank_b[:, MT:], 3, b).then_inc(s["xproj"], 1)
                pe.wait_ge(s["xevac"], 3 * m + 1)
                project(bank_a[:, 0:MT], 4, b)
                for kt in range(KT):
                    last = nc.tensor.matmul(bank_a[0:LORA, MT:], wl1[:, kt, :], xn_in[b][:, kt, :], start=(kt == 0), stop=(kt == KT - 1))
                last.then_inc(s["xproj"], 1)

            def front_theta(i, j):
                m = MPS * i + j
                pe.wait_ge(s["xevac"], 3 * m + 3)
                for q in range(PAIRS):
                    dst = (bank_b, bank_a)[q // 2][:, (q % 2) * MT:(q % 2 + 1) * MT]
                    last = nc.tensor.matmul(dst, wl2[:, q * P:(q + 1) * P], hidden[:, :], start=True, stop=True)
                    if q % 2:
                        last.then_inc(s["thproj"], 1)

            def front_z(i, j):
                m, b = MPS * i + j, j % 2
                for h, dst in enumerate((bank_b, bank_a)):
                    pe.wait_ge(s["clipped"], 2 * m + h + 1)
                    project(dst[:, 0:MT], XBC_T + 2 * h, b)
                    project(dst[:, MT:], XBC_T + 2 * h + 1, b).then_inc(s["zproj"], 1)

            def front_turn(i, j):
                m = MPS * i + j
                pe.wait_ge(s["silu"], m + 1)
                pe.wait_ge(s["bevac"], TPM * m)
                for ch in range(TPM):
                    pe.wait_ge(s["xdt"], TPM * m + ch)
                    for q in range(PAIRS):
                        last = nc.tensor.transpose(bank_t[:, q * P:(q + 1) * P], xbc[:, q, ch * P:(ch + 1) * P], ident)
                    last.then_inc(s["xturned"], 1)

            def back_scores(i, j, ch):
                m, b, t = MPS * i + j, parity(j), (MPS * i + j) * TPM + ch
                here = slice(ch * P, (ch + 1) * P)
                pe.wait_ge(s["bup"], 4 * (m + 1))
                pe.wait_ge(s["xdt"], TPM * (m + 1))
                pe.wait_ge(s["bevac"], t)
                for q in range(PAIRS):
                    last = nc.tensor.transpose(bank_t[:, q * P:(q + 1) * P], b_up[b][:, q, here], ident)
                last.then_inc(s["bturned"], 1)
                pe.wait_ge(s["cown"], m + 1)
                if halved:
                    for level in range(LEVELS + 1):
                        ln, lb = LEVELS * t + level, level % 2
                        pe.wait_ge(s["lmasked"], 2 * ((LEVELS + 1) * t + level))
                        if level < LEVELS:
                            pe.wait_ge(s["lbdec"], ln + 1)
                            pe.wait_ge(s["lcdec"], ln + 1)
                        for e in range(2):
                            part = slice(e * HEADDIM, (e + 1) * HEADDIM)
                            for q in range(PAIRS):
                                lhs, rhs = (level_b[lb][part, q, :], level_c[lb][part, q, :]) if level < LEVELS else (wave[part, q, here], c_own[b][part, q, here])
                                last = nc.tensor.matmul(bank_s[:, e, q * P:(q + 1) * P], lhs, rhs, start=True, stop=True)
                            last.then_inc(s["lscored"], 1)
                    return
                pe.wait_ge(s["grown"], m + 1)
                pe.wait_ge(s["masked"], 2 * t)
                for q in range(PAIRS):
                    for e in range(2):
                        part = slice(e * HEADDIM, (e + 1) * HEADDIM)
                        last = nc.tensor.matmul(bank_s[:, e, q * P:(q + 1) * P], grow[b][part, q, here], c_own[b][part, q, here], start=True, stop=True)
                        if q == PAIRS - 1:
                            last.then_inc(s["scored"], 1)

            def back_update(i, j, ch, c):
                b, t = parity(j), (MPS * i + j) * TPM + ch
                u, rows_c = CPT * t + c, slice(c * CH, (c + 1) * CH)
                pe.wait_ge(s["bevac"], t + 1)
                pe.wait_ge(s["stated"], 2 * u)
                for q in range(PAIRS):
                    last = nc.tensor.matmul(bank_u[:, q * P:(q + 1) * P], b_tok[ch][rows_c, q, :], x_dt[j % 2][rows_c, ch, q * P:(q + 1) * P], start=True, stop=True)
                last.then_inc(s["upd"], 1)

            def back_y(i, j, ch):
                b, t = parity(j), (MPS * i + j) * TPM + ch
                pe.wait_ge(s["masked"], 2 * t + 2)
                pe.wait_ge(s["cin"], MPS * i + j + 1)
                pe.wait_ge(s["gated"], t)
                pe.wait_ge(s["statein"], CPT * t + 1)
                for q in range(PAIRS):
                    dst = bank_y[:, q * P:(q + 1) * P]
                    for e in range(2):
                        nc.tensor.matmul(dst[e * HEADDIM:(e + 1) * HEADDIM, :], x_dt[j % 2][:, ch, q * P + e * HEADDIM:q * P + (e + 1) * HEADDIM],
                                         att[ch][:, e * PAIRS + q, :], start=True, stop=False, skip_group_check=True)
                    for n in range(CPT):
                        here = slice(n * CH, (n + 1) * CH)
                        last = nc.tensor.matmul(dst[:, here], state_in[n][:, q, :], c_in[b][:, q, ch * P + n * CH:ch * P + (n + 1) * CH],
                                                start=False, stop=True, skip_group_check=True)
                last.then_inc(s["yout"], 1)

            def back_out(i, j, ch):
                t = (MPS * i + j) * TPM + ch
                pe.wait_ge(s["gsum"], t + 1)
                pe.wait_ge(s["final"], t)
                for q in range(PAIRS):
                    nc.tensor.matmul(bank_o[:, 0:D_MODEL], g[ch][:, q, :], wout[:, q, :], start=(q == 0), stop=(q == PAIRS - 1))
                pe.wait_ge(s["squared"], t + 1)
                for q in range(PAIRS):
                    last = nc.tensor.matmul(bank_o[:, D_MODEL:D_MODEL + 1], gsq[:, q, :], k("ones")[:, 0:1], start=(q == 0), stop=(q == PAIRS - 1))
                last.then_inc(s["oproj"], 1)

            def body(i, js, last):
                for j in js:
                    more = not (last and j == MPS - 1)
                    if more:
                        front_x(i, j + 1)
                    back_scores(i, j, 0)
                    back_update(i, j, 0, 0)
                    if more:
                        front_theta(i, j + 1)
                    back_update(i, j, 0, 1)
                    back_scores(i, j, 1)
                    back_y(i, j, 0)
                    back_update(i, j, 1, 0)
                    if more:
                        front_z(i, j + 1)
                    back_update(i, j, 1, 1)
                    back_out(i, j, 0)
                    back_y(i, j, 1)
                    if more:
                        front_turn(i, j + 1)
                    back_out(i, j, 1)

            pe.wait_ge(m_ready, 2)
            if halved:
                with pe.Fori(0, BATCH) as i:
                    for j in range(MPS):
                        front_x(i, j)
                        front_theta(i, j)
                        front_z(i, j)
                        front_turn(i, j)
                        for ch in range(TPM):
                            back_scores(i, j, ch)
                            for part in range(CPT):
                                back_update(i, j, ch, part)
                            back_y(i, j, ch)
                            back_out(i, j, ch)
            else:
                front_x(0, 0)
                front_theta(0, 0)
                front_z(0, 0)
                front_turn(0, 0)
                with pe.Fori(0, BATCH - 1) as i:
                    body(i, range(MPS), False)
                body(BATCH - 1, range(MPS), True)

        def scalar_mixer(act, halved):
            epos = grow[1] if halved else decay

            def parity(j):
                return 0 if halved else j % 2

            def front_x(i, j):
                m, b = MPS * i + j, j % 2
                act.wait_ge(s["convd"], 15 * m)
                act.wait_ge(s["halo"], m)
                for n, (dst, w) in enumerate(((bank_a, 2), (bank_b, 2), (bank_a, 1))):
                    act.wait_ge(s["xproj"], 3 * m + n + 1)
                    src = dst[:, 0:w * MT].rearrange("p (n t) -> p n t", n=w)
                    nc.scalar.activation(x_pre[b][:, 2 * n:2 * n + w, D_CONV - 1:], src, ACT.Copy)
                    for d in range(w):
                        ct = 2 * n + d
                        last = nc.scalar.activation(conv[:, ct, :], src[:, d, :], ACT.Identity, bias=c("conv_b", ct),
                                                    scale=c("conv_w", ct * D_CONV + D_CONV - 1))
                    if n == 2:
                        act.wait_ge(s["thproj"], 2 * m)
                        last = nc.scalar.activation(hidden[0:LORA, :], bank_a[0:LORA, MT:], ACT.Tanh)
                    last.then_inc(s["xevac"], 1)

            def front_z(i, j):
                m, b = MPS * i + j, j % 2
                act.wait_ge(s["gated"], two_ago(m, halved, TPM))
                act.wait_ge(s["xskip"], m)
                for h, src in enumerate((bank_b, bank_a)):
                    act.wait_ge(s["zproj"], 2 * m + h + 1)
                    nc.scalar.activation(z_gate[b][:, 2 * h:2 * h + 2, :], src.rearrange("p (n t) -> p n t", n=2), ACT.Silu).then_inc(s["zevac"], 1)

            def front_lambda(i, j):
                m = MPS * i + j
                act.wait_ge(s["clipped"], 2 * m + 2)
                act.wait_ge(s["rsum"], 4 * m)
                act.wait_ge(s["cquad"], m)
                act.wait_ge(s["cown"], m)
                nc.scalar.activation(lam, theta, ACT.Square, scale=TWO_PI).then_inc(s["lamsq"], 1)
                act.wait_ge(s["lamsq"], m + 1)
                for q in range(PAIRS):
                    last = nc.scalar.activation(lam[:, q, :], lam[:, q, :], ACT.Identity, bias=c("lb", q), scale=c("eta", q))
                last.then_inc(s["lamd"], 1)

            def front_silu(i, j):
                m = MPS * i + j
                act.wait_ge(s["convd"], 15 * (m + 1))
                act.wait_ge(s["xturned"], TPM * m)
                act.wait_ge(s["xd"], m)
                act.wait_ge(s["repd"], 16 * REPS * m)
                nc.scalar.activation(xbc, conv, ACT.Silu).then_inc(s["silu"], 1)

            def front_trig(i, j):
                m = MPS * i + j
                act.wait_ge(s["fracd"], m + 1)
                act.wait_ge(s["grown"], m)
                act.wait_ge(s["wavedec"], m)
                act.wait_ge(s["quadgrow"], m)
                act.wait_ge(s["quaddec"], m)
                if halved:
                    act.wait_ge(s["dwave"], m)
                    act.wait_ge(s["cown"], m)
                    act.wait_ge(s["lscored"], 2 * (LEVELS + 1) * TPM * m)
                nc.scalar.activation(quad, frac, ACT.Abs).then_inc(s["fabs"], 1)
                nc.scalar.activation(wave, frac, ACT.Sin, scale=TRIG)
                act.wait_ge(s["fabs"], m + 1)
                nc.scalar.activation(quad, quad, ACT.Sin, scale=-TRIG, bias=k("halfpi")).then_inc(s["trig"], 1)

            def front_exp(i, j):
                m = MPS * i + j
                act.wait_ge(s["rsum"], 4 * (m + 1))
                act.wait_ge(s["wavedec"], m)
                act.wait_ge(s["quaddec"], m)
                act.wait_ge(s["cquad"], m)
                act.wait_ge(s["cin"], m)
                act.wait_ge(s["headdec"], m)
                if halved:
                    act.wait_ge(s["stated"], 2 * CPM * m)
                nc.scalar.activation(eneg, decay, ACT.Exp, scale=-1.0)
                nc.scalar.activation(end_dec[:, :, :], decay.rearrange("p q (c t) -> p c q t", c=CPM)[:, :, :, CH - 1], ACT.Exp, scale=-1.0).then_inc(s["negd"], 1)
                if halved:
                    act.wait_ge(s["tail"], m + 1)
                    nc.scalar.activation(epos, epos, ACT.Exp).then_inc(s["expd"], 1)
                else:
                    act.wait_ge(s["negd"], m + 1)
                    nc.scalar.activation(epos, decay, ACT.Exp).then_inc(s["expd"], 1)

            def back_b(i, j, ch):
                t = (MPS * i + j) * TPM + ch
                act.wait_ge(s["bturned"], t + 1)
                act.wait_ge(s["upd"], CPT * (t - 1 if ch else t))
                nc.scalar.activation(b_tok[ch].rearrange("p q s -> p (q s)"), bank_t, ACT.Copy).then_inc(s["bevac"], 1)

            def back_levels(i, j, ch):
                t = (MPS * i + j) * TPM + ch
                for level in range(LEVELS):
                    act.wait_ge(s["signed"], LEVELS * t + level + 1)
                    nc.scalar.activation(level_e[level % 2], level_e[level % 2], ACT.Exp).then_inc(s["lexpd"], 1)

            def back_square(i, j, ch):
                t = (MPS * i + j) * TPM + ch
                act.wait_ge(s["gsum"], t + 1)
                act.wait_ge(s["oproj"], t)
                nc.scalar.activation(gsq, g[ch], ACT.Square).then_inc(s["squared"], 1)

            def body(i, js, last):
                for j in js:
                    more = not (last and j == MPS - 1)
                    if more:
                        front_x(i, j + 1)
                    back_b(i, j, 0)
                    if more:
                        front_lambda(i, j + 1)
                    back_b(i, j, 1)
                    if more:
                        front_silu(i, j + 1)
                        front_z(i, j + 1)
                    back_square(i, j, 0)
                    if more:
                        front_trig(i, j + 1)
                    back_square(i, j, 1)
                    if more:
                        front_exp(i, j + 1)

            act.wait_ge(m_ready, 2)
            if halved:
                with act.Fori(0, BATCH) as i:
                    for j in range(MPS):
                        front_x(i, j)
                        front_lambda(i, j)
                        front_silu(i, j)
                        front_z(i, j)
                        front_trig(i, j)
                        front_exp(i, j)
                        for ch in range(TPM):
                            back_b(i, j, ch)
                            back_levels(i, j, ch)
                            back_square(i, j, ch)
            else:
                front_x(0, 0)
                front_lambda(0, 0)
                front_silu(0, 0)
                front_z(0, 0)
                front_trig(0, 0)
                front_exp(0, 0)
                with act.Fori(0, BATCH - 1) as i:
                    body(i, range(MPS), False)
                body(BATCH - 1, range(MPS), True)

        def vector_mixer(dve, halved):
            epos = grow[1] if halved else decay

            def parity(j):
                return 0 if halved else j % 2

            def front_halo(i, j):
                m, b = MPS * i + j, j % 2
                dst = x_pre[b][:, :, 0:D_CONV - 1]
                if j % MPS == 0:
                    nc.vector.memset(dst, 0.0).then_inc(s["halo"], 1)
                else:
                    dve.wait_ge(s["xevac"], 3 * m)
                    nc.vector.tensor_copy(dst, x_pre[1 - b][:, :, MT:]).then_inc(s["halo"], 1)

            def front_conv(i, j):
                m, b = MPS * i + j, j % 2
                dve.wait_ge(s["xevac"], 3 * m + 3)
                dve.wait_ge(s["halo"], m + 1)
                for tap in range(D_CONV - 1):
                    for ct in range(XBC_T):
                        if tap:
                            dve.wait_ge(s["convd"], 15 * m + (tap - 1) * XBC_T + ct + 1)
                        nc.vector.scalar_tensor_tensor(conv[:, ct, :], x_pre[b][:, ct, tap:tap + MT], c("conv_w", ct * D_CONV + tap),
                                                       conv[:, ct, :], ALU.mult, ALU.add).then_inc(s["convd"], 1)

            def front_clip(i, j):
                m = MPS * i + j
                dve.wait_ge(s["lamsq"], m)
                dve.wait_ge(s["psum"], 4 * m)
                dve.wait_ge(s["cwave"], m)
                dve.wait_ge(s["dwave"], m)
                for h, src in enumerate((bank_b, bank_a)):
                    dve.wait_ge(s["thproj"], 2 * m + h + 1)
                    nc.vector.tensor_scalar(theta[:, 2 * h:2 * h + 2, :], src.rearrange("p (n t) -> p n t", n=2), 0.25, -0.25,
                                            ALU.min, ALU.max).then_inc(s["clipped"], 1)

            def front_sums(i, j):
                m = MPS * i + j
                dve.wait_ge(s["lamdt"], m + 1)
                dve.wait_ge(s["expd"], m)
                dve.wait_ge(s["grown"], m)
                dve.wait_ge(s["quadgrow"], m)
                for q in range(PAIRS):
                    nc.vector.tensor_tensor_scan(decay[:, q, :], k("restart"), lam[:, q, :], 0.0, ALU.mult, ALU.add).then_inc(s["rsum"], 1)
                dve.wait_ge(s["angle"], m + 1)
                dve.wait_ge(s["fracd"], m)
                dve.wait_ge(s["bup"], 4 * m)
                for q in range(PAIRS):
                    start = k("quarter") if j % MPS == 0 else frac[:, q, MT - 1:MT]
                    nc.vector.tensor_tensor_scan(phase[:, q, :], expand(k("ones")[:, 0:1], MT), theta[:, q, :], start, ALU.mult, ALU.add).then_inc(s["psum"], 1)
                dve.wait_ge(s["psum"], 4 * (m + 1))
                dve.wait_ge(s["quadgrow"], m)
                dve.wait_ge(s["quaddec"], m)
                nc.vector.tensor_scalar(whole, phase, ROUND, -ROUND, ALU.add, ALU.add).then_inc(s["rounded"], 1)

            def front_xdt(i, j):
                m, b = MPS * i + j, j % 2
                dve.wait_ge(s["upd"], two_ago(m, halved, CPM))
                dve.wait_ge(s["yout"], two_ago(m, halved, TPM))
                for ch in range(TPM):
                    dve.wait_ge(s["xturned"], TPM * m + ch + 1)
                    dt_col = dt_tok[:, bass.ds(m * TPM + ch, 1), :].rearrange("p o h -> p (o h)")[:, :, None]
                    nc.vector.tensor_tensor(x_dt[b][:, ch, :].rearrange("p (h d) -> p h d", h=HEADS), bank_t.rearrange("p (h d) -> p h d", h=HEADS),
                                            dt_col.broadcast_to([P, HEADS, HEADDIM]), ALU.mult).then_inc(s["xdt"], 1)

            def front_bc(i, j):
                m, b = MPS * i + j, parity(j)
                both = [P, PAIRS, MT]
                if halved:
                    by_chunk = [v.rearrange("p q (c t) -> p (q c) t", c=CPM) for v in (epos, decay)]
                    dve.wait_ge(s["quadgrow"], m)
                    dve.wait_ge(s["rsum"], 4 * (m + 1))
                    nc.vector.tensor_tensor(by_chunk[0], by_chunk[1], by_chunk[1][:, :, CH - 1:CH].broadcast_to([P, PAIRS * CPM, CH]), ALU.subtract).then_inc(s["tail"], 1)
                dve.wait_ge(s["trig"], m + 1)
                dve.wait_ge(s["expd"], m + 1)
                dve.wait_ge(s["yout"], two_ago(m, halved, TPM))
                nc.vector.tensor_tensor(grow[b], wave, epos, ALU.mult).then_inc(s["grown"], 1)
                dve.wait_ge(s["psum"], 4 * (m + 1))
                nc.vector.tensor_tensor(wave_dec, wave, eneg, ALU.mult).then_inc(s["wavedec"], 1)
                dve.wait_ge(s["repd"], 16 * REPS * (m + 1))
                dve.wait_ge(s["wavedec"], m + 1)
                nc.vector.tensor_tensor(c_in[b], rep[:, 0:1, :].broadcast_to(both), wave_dec, ALU.mult).then_inc(s["cwave"], 1)
                dve.wait_ge(s["cb"], 6 * (m + 1))
                nc.vector.tensor_tensor(c_own[b], rep[:, 4:5, :].broadcast_to(both), wave if halved else wave_dec, ALU.mult).then_inc(s["dwave"], 1)
                dve.wait_ge(s["grown"], m + 1)
                dve.wait_ge(s["bquad"], m + 1)
                for c in range(CPM):
                    here = slice(c * CH, (c + 1) * CH)
                    nc.vector.scalar_tensor_tensor(b_up[b][:, :, here], grow[b][:, :, here], rep[:, 2, (c + 1) * CH - 1:(c + 1) * CH], quad_grow[:, :, here],
                                                   ALU.mult, ALU.subtract).then_inc(s["bup"], 1)
                dve.wait_ge(s["cquad"], m + 1)
                dve.wait_ge(s["cwave"], m + 1)
                nc.vector.tensor_tensor(c_in[b], c_in[b], eneg, ALU.add).then_inc(s["cin"], 1)
                dve.wait_ge(s["dquad"], m + 1)
                dve.wait_ge(s["dwave"], m + 1)
                nc.vector.tensor_tensor(c_own[b], c_own[b], quad if halved else quad_dec, ALU.add).then_inc(s["cown"], 1)

            def back_levels(i, j, ch):
                m, t = MPS * i + j, (MPS * i + j) * TPM + ch
                here = slice(ch * P, (ch + 1) * P)
                over_pairs = [P, PAIRS, P]
                dve.wait_ge(s["cown"], m + 1)

                def apart(level):
                    ln, dst = LEVELS * t + level, level_e[level % 2]
                    if level >= 2:
                        dve.wait_ge(s["lbdec"], ln - 1)
                        dve.wait_ge(s["lcdec"], ln - 1)
                    else:
                        dve.wait_ge(s["lbdec"], LEVELS * t)
                        dve.wait_ge(s["lcdec"], LEVELS * t)
                    own, ref = reference(decay, ch, level)
                    for q in range(PAIRS):
                        last = nc.vector.tensor_tensor(dst[:, q, :].rearrange("p (n w) -> p n w", w=CH >> level), own[q], ref[q], ALU.subtract)
                    last.then_inc(s["apart"], 1)
                    dve.wait_ge(s["apart"], ln + 1)
                    nc.vector.tensor_tensor(dst, dst, level_signs[:, level:level + 1, :].broadcast_to(over_pairs), ALU.mult).then_inc(s["signed"], 1)

                def add(level):
                    ln = (LEVELS + 1) * t + level
                    mask = level_masks[:, level:level + 1, :].broadcast_to(over_pairs)
                    for h in range(2):
                        dve.wait_ge(s["lscored"], 2 * ln + h + 1)
                        src, dst = bank_s[:, h, :].rearrange("p (h t) -> p h t", h=4), att[ch][:, 4 * h:4 * h + 4, :]
                        if level == 0:
                            nc.vector.tensor_tensor(dst, src, mask, ALU.mult).then_inc(s["lmasked"], 1)
                        else:
                            dve.wait_ge(s["lsum"], 2 * (LEVELS * t + level - 1) + h)
                            nc.vector.tensor_tensor(part_att, src, mask, ALU.mult).then_inc(s["lmasked"], 1)
                            dve.wait_ge(s["lmasked"], 2 * ln + h + 1)
                            last = nc.vector.tensor_tensor(dst, dst, part_att, ALU.add).then_inc(s["lsum"], 1)
                            if level == LEVELS:
                                dve.wait_ge(s["lsum"], 2 * (LEVELS * t + level - 1) + h + 1)
                                dve.sem_inc(s["masked"], 1)

                dve.wait_ge(s["yout"], t - 1 if ch else t)
                apart(0)
                for level in range(LEVELS + 1):
                    if level + 1 < LEVELS:
                        apart(level + 1)
                    if level < LEVELS:
                        dve.wait_ge(s["lexpd"], LEVELS * t + level + 1)
                        if level >= 2:
                            dve.wait_ge(s["lscored"], 2 * ((LEVELS + 1) * t + level - 1))
                        nc.vector.tensor_tensor(level_c[level % 2], c_own[0][:, :, here], level_e[level % 2], ALU.mult).then_inc(s["lcdec"], 1)
                    add(level)

            def back_mask(i, j, ch):
                t = (MPS * i + j) * TPM + ch
                dve.wait_ge(s["yout"], t - 1 if ch else t)
                for h in range(2):
                    dve.wait_ge(s["scored"], 2 * t + h + 1)
                    nc.vector.tensor_tensor(att[ch][:, 4 * h:4 * h + 4, :], bank_s[:, h, :].rearrange("p (h t) -> p h t", h=4),
                                            k("causal")[:, None, :].broadcast_to([P, 4, P]), ALU.mult).then_inc(s["masked"], 1)

            def back_state(i, j, ch, c):
                u = ((MPS * i + j) * TPM + ch) * CPT + c
                dve.wait_ge(s["upd"], u + 1)
                dve.wait_ge(s["statein"], u)
                for e in range(2):
                    part = slice(e * HEADDIM, (e + 1) * HEADDIM)
                    new = bank_u[part, :].rearrange("p (q d) -> p q d", q=PAIRS)[:, :, part]
                    if halved:
                        for q in range(PAIRS):
                            last = nc.vector.scalar_tensor_tensor(state[part, q, :], state_in[c][part, q, part], end_dec[part, ch * CPT + c, q:q + 1], new[:, q, :], ALU.mult, ALU.add)
                    else:
                        last = nc.vector.tensor_tensor(state[part, :, :], new, state_in[c][part, :, part], ALU.add)
                    last.then_inc(s["stated"], 1)

            def back_gate(i, j, ch):
                b, t = j % 2, (MPS * i + j) * TPM + ch
                here = slice(ch * P, (ch + 1) * P)
                dve.wait_ge(s["yout"], t + 1)
                dve.wait_ge(s["oproj"], t - 1 if ch else t)
                dve.wait_ge(s["squared"], t - 1 if ch else t)
                nc.vector.tensor_tensor(g[ch], bank_y.rearrange("p (q t) -> p q t", q=PAIRS), z_gate[b][:, :, here], ALU.mult).then_inc(s["gated"], 1)
                dve.wait_ge(s["gated"], t + 1)
                nc.vector.tensor_tensor(g[ch], g[ch], x_skip[b][:, :, here], ALU.add).then_inc(s["gsum"], 1)

            def back_final(i, j, ch):
                n, t = MPS * i + j, (MPS * i + j) * TPM + ch
                dve.wait_ge(x_loaded[ch], 16 * n + 16)
                dve.wait_ge(e_loaded2[ch], 16 * n + 16)
                gate_col = gate[:, bass.ds(t, 1)]
                nc.vector.scalar_tensor_tensor(x_tile[ch][:, :], e_tile[ch][:, :], gate_col, x_tile[ch][:, :], ALU.mult, ALU.add).then_inc(s["xplus"], 1)
                dve.wait_ge(s["oproj"], t + 1)
                nc.vector.tensor_scalar(ms[ch][:, :], bank_o[:, D_MODEL:D_MODEL + 1], 1.0 / D_INNER, RMS_EPS, ALU.mult, ALU.add).then_inc(s["meansq"], 1)
                dve.wait_ge(s["rmsd"], t + 1)
                dve.wait_ge(s["xplus"], t + 1)
                dve.wait_ge(o_stored[ch], 16 * n)
                nc.vector.scalar_tensor_tensor(o_tile[ch][:, :], bank_o[:, 0:D_MODEL], rms[ch][:, :], x_tile[ch][:, :], ALU.mult, ALU.add).then_inc(s["final"], 1)

            def body(i, js, last):
                for j in js:
                    more = not (last and j == MPS - 1)
                    back_mask(i, j, 0)
                    back_state(i, j, 0, 0)
                    if more:
                        front_halo(i, j + 1)
                        front_clip(i, j + 1)
                    back_state(i, j, 0, 1)
                    back_mask(i, j, 1)
                    back_state(i, j, 1, 0)
                    back_gate(i, j, 0)
                    if more:
                        front_conv(i, j + 1)
                    back_state(i, j, 1, 1)
                    if more:
                        front_sums(i, j + 1)
                    back_final(i, j, 0)
                    back_gate(i, j, 1)
                    if more:
                        front_xdt(i, j + 1)
                        front_bc(i, j + 1)
                    back_final(i, j, 1)

            nc.vector.memset(hidden[32:LORA + 1, :], 1.0).then_inc(m_ready, 1)
            nc.vector.memset(state_in[0][:, :, :], 0.0).then_inc(m_zero, 1)
            nc.vector.memset(state_in[1][:, :, :], 0.0).then_inc(m_zero, 1)
            if halved:
                dve.wait_ge(table_in, 32)
                with dve.Fori(0, BATCH) as i:
                    for j in range(MPS):
                        front_halo(i, j)
                        front_clip(i, j)
                        front_conv(i, j)
                        front_sums(i, j)
                        front_xdt(i, j)
                        front_bc(i, j)
                        for ch in range(TPM):
                            back_levels(i, j, ch)
                            for part in range(CPT):
                                back_state(i, j, ch, part)
                            back_gate(i, j, ch)
                            back_final(i, j, ch)
            else:
                front_halo(0, 0)
                front_clip(0, 0)
                front_conv(0, 0)
                front_sums(0, 0)
                front_xdt(0, 0)
                front_bc(0, 0)
                with dve.Fori(0, BATCH - 1) as i:
                    body(i, range(MPS), False)
                body(BATCH - 1, range(MPS), True)

        def gpsimd_mixer(pool, halved):
            epos = grow[1] if halved else decay

            def parity(j):
                return 0 if halved else j % 2

            def front_dt(i, j):
                m, n, b = MPS * i + j, 2 * i + j // 2, j % 2
                pool.wait_ge(dt_loaded[b], 32 * (n + 1))
                pool.wait_ge(s["lamsq"], m + 1)
                nc.gpsimd.tensor_tensor(theta, theta, dt_in[b], ALU.mult).then_inc(s["angle"], 1)
                pool.wait_ge(s["lamd"], m + 1)
                nc.gpsimd.tensor_tensor(lam, lam, dt_in[b], ALU.mult).then_inc(s["lamdt"], 1)

            def front_frac(i, j):
                m = MPS * i + j
                pool.wait_ge(s["rounded"], m + 1)
                pool.wait_ge(s["trig"], m)
                nc.gpsimd.tensor_tensor(frac, phase, whole, ALU.subtract).then_inc(s["fracd"], 1)

            def front_head(i, j):
                m, b = MPS * i + j, j % 2
                shape = [P, CPM * PAIRS, 2]
                pool.wait_ge(s["negd"], m + 1)
                nc.gpsimd.tensor_tensor(head_dec[b][:, :, :].rearrange("p c (q e) -> p (c q) e", e=2), end_dec[:, :, :].rearrange("p c q -> p (c q)")[:, :, None].broadcast_to(shape),
                                        k("ownhead")[:, None, :].broadcast_to(shape), ALU.mult).then_inc(s["headdec"], 1)

            def front_skip(i, j):
                m, b = MPS * i + j, j % 2
                pool.wait_ge(s["silu"], m + 1)
                pool.wait_ge(s["gsum"], two_ago(m, halved, TPM))
                nc.gpsimd.tensor_tensor(x_skip[b], xbc[:, 0:PAIRS, :], c("D", 0, PAIRS)[:, :, None].broadcast_to([P, PAIRS, MT]), ALU.mult).then_inc(s["xd"], 1)
                pool.wait_ge(s["zevac"], 2 * m + 2)
                pool.wait_ge(s["xd"], m + 1)
                nc.gpsimd.tensor_tensor(x_skip[b], x_skip[b], z_gate[b], ALU.mult).then_inc(s["xskip"], 1)

            def front_cb(i, j):
                m = MPS * i + j
                c_re, c_im, b_re, b_im, re, im = (rep[:, n, :] for n in range(6))
                pool.wait_ge(s["repd"], 16 * REPS * (m + 1))
                pool.wait_ge(s["dwave"], m)
                pool.wait_ge(s["dquad"], m)
                nc.gpsimd.tensor_tensor(re, c_re, b_re, ALU.mult).then_inc(s["cb"], 1)
                nc.gpsimd.tensor_tensor(im, c_re, b_im, ALU.mult).then_inc(s["cb"], 1)
                nc.gpsimd.tensor_tensor(cb_part[0], c_im, b_im, ALU.mult).then_inc(s["cb"], 1)
                nc.gpsimd.tensor_tensor(cb_part[1], c_im, b_re, ALU.mult).then_inc(s["cb"], 1)
                pool.wait_ge(s["cb"], 6 * m + 4)
                nc.gpsimd.tensor_tensor(re, re, cb_part[0], ALU.subtract).then_inc(s["cb"], 1)
                nc.gpsimd.tensor_tensor(im, im, cb_part[1], ALU.add).then_inc(s["cb"], 1)

            def front_bc(i, j):
                m = MPS * i + j
                both = [P, PAIRS, MT]
                b_ends = rep[:, 3, :].rearrange("p (c t) -> p c t", c=CPM)[:, None, :, CH - 1:CH]
                by_chunk = quad_grow.rearrange("p q (c t) -> p q c t", c=CPM)
                pool.wait_ge(s["trig"], m + 1)
                pool.wait_ge(s["expd"], m + 1)
                nc.gpsimd.tensor_tensor(quad_grow, quad, epos, ALU.mult).then_inc(s["quadgrow"], 1)
                pool.wait_ge(s["rsum"], 4 * (m + 1))
                nc.gpsimd.tensor_tensor(quad_dec, quad, eneg, ALU.mult).then_inc(s["quaddec"], 1)
                pool.wait_ge(s["quadgrow"], m + 1)
                nc.gpsimd.tensor_tensor(by_chunk, by_chunk, b_ends.broadcast_to([P, PAIRS, CPM, CH]), ALU.mult).then_inc(s["bquad"], 1)
                pool.wait_ge(s["quaddec"], m + 1)
                pool.wait_ge(s["wavedec"], m + 1)
                nc.gpsimd.tensor_tensor(eneg, rep[:, 1:2, :].broadcast_to(both), quad_dec, ALU.mult).then_inc(s["cquad"], 1)
                pool.wait_ge(s["cquad"], m + 1)
                pool.wait_ge(s["cb"], 6 * (m + 1))
                v = quad if halved else quad_dec
                nc.gpsimd.tensor_tensor(v, rep[:, 5:6, :].broadcast_to(both), v, ALU.mult).then_inc(s["dquad"], 1)

            def back_levels(i, j, ch):
                m, t = MPS * i + j, (MPS * i + j) * TPM + ch
                here = slice(ch * P, (ch + 1) * P)
                pool.wait_ge(s["cown"], m + 1)
                pool.wait_ge(s["cin"], m + 1)
                for level in range(LEVELS):
                    pool.wait_ge(s["lexpd"], LEVELS * t + level + 1)
                    pool.wait_ge(s["lscored"], 2 * ((LEVELS + 1) * t + max(level - 1, 0)))
                    nc.gpsimd.tensor_tensor(level_b[level % 2], wave[:, :, here], level_e[level % 2], ALU.mult).then_inc(s["lbdec"], 1)

            def back_state(i, j, ch, c):
                b, u = j % 2, ((MPS * i + j) * TPM + ch) * CPT + c
                pool.wait_ge(s["stated"], 2 * u + 2)
                if c:
                    pool.wait_ge(s["yout"], (MPS * i + j) * TPM + ch + 1)
                else:
                    pool.wait_ge(s["yout"], (MPS * i + j) * TPM + ch)
                shape = [P, PAIRS, 2, HEADDIM]
                dst = state_in[1 - c][:, :, :].rearrange("p q (e d) -> p q e d", e=2)
                if j == MPS - 1 and ch == TPM - 1 and c == CPT - 1:
                    by = zero_dec[:, :]
                elif halved:
                    by = None
                else:
                    by = head_dec[b][:, ch * CPT + c, :]
                own = k("ownhead")[:, None, :, None] if by is None else by.rearrange("p (q e) -> p q e", e=2)[:, :, :, None]
                nc.gpsimd.tensor_tensor(dst, state[:, :, None, :].broadcast_to(shape), own.broadcast_to(shape), ALU.mult).then_inc(s["statein"], 1)

            def back_gather(i, j, ch):
                n, t = MPS * i + j, (MPS * i + j) * TPM + ch
                pool.wait_ge(s["xplus"], TPM * n)
                pool.wait_ge(e_loaded2[ch], 16 * n)
                pool.sem_inc(passed, 1)
                nc.gpsimd.tensor_copy(e_index[ch][:, :], slot_of[:, bass.ds(t, 1)]).then_inc(s["eidx"], 1)
                pool.wait_ge(s["eidx"], t + 1)
                pool.sem_inc(passed, 1)
                pool.indirect_dma_start(e_tile[ch][:, :], None, expert_d, bass.IndirectOffsetOnAxis(ap=e_index[ch][:, :], axis=0)).then_inc(e_loaded2[ch], 16)

            def back_rms(i, j, ch):
                t = (MPS * i + j) * TPM + ch
                pool.wait_ge(s["meansq"], t + 1)
                pool.wait_ge(s["final"], t)
                nc.gpsimd.tensor_tensor(rms[ch][:, :], ms[ch][:, :], k("minushalf")[:, 0:1], ALU.pow).then_inc(s["rmsd"], 1)

            def body(i, js, last):
                for j in js:
                    more = not (last and j == MPS - 1)
                    for ch in range(TPM):
                        back_gather(i, j, ch)
                    back_state(i, j, 0, 0)
                    if more:
                        front_dt(i, j + 1)
                    back_state(i, j, 0, 1)
                    back_state(i, j, 1, 0)
                    if more:
                        front_cb(i, j + 1)
                        front_frac(i, j + 1)
                    back_state(i, j, 1, 1)
                    back_rms(i, j, 0)
                    if more:
                        front_skip(i, j + 1)
                        front_head(i, j + 1)
                        front_bc(i, j + 1)
                    back_rms(i, j, 1)

            pool.wait_ge(m_zero, 2)
            nc.gpsimd.memset(zero_dec[:, :], 0.0).then_inc(m_ready, 1)
            pool.wait_ge(m_ready, 2)
            if halved:
                with pool.Fori(0, BATCH) as i:
                    for j in range(MPS):
                        front_dt(i, j)
                        front_cb(i, j)
                        front_frac(i, j)
                        front_skip(i, j)
                        front_head(i, j)
                        front_bc(i, j)
                        for ch in range(TPM):
                            back_gather(i, j, ch)
                            back_levels(i, j, ch)
                            for part in range(CPT):
                                back_state(i, j, ch, part)
                            back_rms(i, j, ch)
            else:
                front_dt(0, 0)
                front_cb(0, 0)
                front_frac(0, 0)
                front_skip(0, 0)
                front_head(0, 0)
                front_bc(0, 0)
                with pool.Fori(0, BATCH - 1) as i:
                    body(i, range(MPS), False)
                body(BATCH - 1, range(MPS), True)

        with nc.Block() as block:
            @block.sync
            def _(sp):
                chunks_halved = sp.value_load(halve[0:1, 0:1], min_val=0, max_val=1)
                with sp.If(chunks_halved == 0):
                    sync_mixer(sp, False)
                with sp.If(chunks_halved != 0):
                    sync_mixer(sp, True)

            @block.tensor
            def _(pe):
                chunks_halved = pe.value_load(halve[0:1, 0:1], min_val=0, max_val=1)
                with pe.If(chunks_halved == 0):
                    tensor_mixer(pe, False)
                with pe.If(chunks_halved != 0):
                    tensor_mixer(pe, True)

            @block.scalar
            def _(act):
                chunks_halved = act.value_load(halve[0:1, 0:1], min_val=0, max_val=1)
                with act.If(chunks_halved == 0):
                    scalar_mixer(act, False)
                with act.If(chunks_halved != 0):
                    scalar_mixer(act, True)

            @block.vector
            def _(dve):
                chunks_halved = dve.value_load(halve[0:1, 0:1], min_val=0, max_val=1)
                with dve.If(chunks_halved == 0):
                    vector_mixer(dve, False)
                with dve.If(chunks_halved != 0):
                    vector_mixer(dve, True)

            @block.gpsimd
            def _(pool):
                chunks_halved = pool.value_load(halve[0:1, 0:1], min_val=0, max_val=1)
                with pool.If(chunks_halved == 0):
                    gpsimd_mixer(pool, False)
                with pool.If(chunks_halved != 0):
                    gpsimd_mixer(pool, True)


_OUT = (BATCH, SEQ, D_MODEL)


def kernel(**inputs):
    import numpy as np
    import concourse.bacc as bacc
    from concourse.bass_utils import run_bass_kernel_spmd

    a = {n.replace("L0_", ""): np.asarray(v) for n, v in inputs.items()}

    const = np.zeros((P, CONST_W), np.float32)

    def put(name, v):
        const[:, CONST[name][0]:CONST[name][0] + CONST[name][1]] = v
    row, colm = np.arange(P)[:, None], np.arange(P)[None, :]
    put("ident", row == colm)
    put("causal", (row <= colm) & (row // CH == colm // CH))
    put("before", row < colm)
    put("ones", 1.0)
    put("restart", (np.arange(MT) % CH != 0)[None, :])
    put("tilestart", (np.arange(TILES * EXPERTS) % TILES != 0)[None, :])
    put("first", (EXPERTS - np.arange(EXPERTS))[None, :])
    put("slot", np.arange(SLOT_TILES)[None, :])
    real = (row // NBLK) % 2 == 0
    put("quarter", np.where(real, 0.25, 0.0))
    put("halfpi", math.pi / 2)
    put("minushalf", -0.5)
    put("ownhead", row // (2 * NBLK) == np.arange(2)[None, :])

    halvings = np.zeros((P, 2 * LEVELS + 1, P), np.float32)
    for level in range(LEVELS):
        half = CH >> (level + 1)
        first = np.arange(P) % (2 * half) < half
        halvings[:, level] = np.where(first, 1.0, -1.0)
        halvings[:, LEVELS + level] = (row // (2 * half) == colm // (2 * half)) & first[:, None] & ~first[None, :]
    halvings[:, 2 * LEVELS] = row == colm

    def by_tile(v):
        return np.moveaxis(v.reshape(-1, P, *v.shape[1:]), 0, 1)

    bc = D_INNER + np.concatenate([np.arange(h, h + 2 * NBLK, 2) for h in (0, 1, 2 * NBLK, 2 * NBLK + 1)])
    xbc = np.concatenate([np.arange(D_INNER), bc])
    w = a["attn_in_proj_w"]
    w_in = np.concatenate([w[D_INNER:][xbc], w[:D_INNER]]).T
    w_small = np.concatenate([w[-HEADS:].T, a["ffn_router_w"]], axis=1)

    def spread(v):
        return np.broadcast_to(v.reshape(PAIRS, 2, 1, NBLK), (PAIRS, 2, 2, NBLK)).reshape(PAIRS, P).T

    lora2 = np.concatenate([a["attn_theta_w2"], a["attn_theta_base"].reshape(1, -1)])
    lora2 = np.broadcast_to(lora2.reshape(LORA + 1, PAIRS, 2, 1, NBLK), (LORA + 1, PAIRS, 2, 2, NBLK)).reshape(LORA + 1, PAIRS * P)
    cols = np.concatenate([
        by_tile(a["attn_conv_w"][xbc]).reshape(P, -1), by_tile(a["attn_conv_b"][xbc]).reshape(P, -1),
        by_tile(np.repeat(a["attn_D"], HEADDIM)), by_tile(a["attn_norm_w"]),
        spread(a["attn_lambda_base"]), spread(a["attn_viscosity_eta"])], axis=1)
    arrays = {
        "x": a["attn_x"].reshape(TOKENS, D_MODEL), "const": const, "halvings": halvings, "cols": cols, "w_in": by_tile(w_in), "w_small": by_tile(w_small),
        "w_lora1": by_tile(a["attn_theta_w1"]), "w_lora2": lora2, "w_out": by_tile(a["attn_out_proj_w"].T),
        "rows": np.concatenate([a[n].reshape(-1) for n in ("attn_dt_bias", "ffn_router_b", "attn_lambda_base", "attn_viscosity_eta")])[None, :],
        "w_exp": by_tile(np.moveaxis(a["ffn_expert_w"], 0, 1)).reshape(P, KT * EXPERTS, D_MODEL),
        "b_exp": a["ffn_expert_b"],
    }
    nc = bacc.Bacc("TRN2", target_bir_lowering=False, num_devices=1)
    arrays = {n: np.ascontiguousarray(v) for n, v in arrays.items()}
    aps = [nc.dram_tensor(n, v.shape, mybir.dt.from_np(v.dtype), kind="ExternalInput").ap() for n, v in arrays.items()]
    out = nc.dram_tensor("out", (TOKENS, D_MODEL), F32, kind="ExternalOutput").ap()
    mixer_and_experts(nc, *aps, out)
    r = run_bass_kernel_spmd(nc, [arrays], core_ids=[0])
    return r.results[0]["out"].reshape(_OUT)
```

```python
import concourse.bass as bass
from concourse import mybir
from contextlib import ExitStack
import math

F32 = mybir.dt.float32
I32 = mybir.dt.int32
ALU = mybir.AluOpType
ACT = mybir.ActivationFunctionType
AX_X = mybir.AxisListType.X

P = 128
BATCH, SEQ, D_MODEL = 8, 1024, 256
TOKENS = BATCH * SEQ
KT = D_MODEL // P
D_INNER, HEADS, HEADDIM, NBLK, LORA, D_CONV = 512, 8, 64, 32, 48, 4
PAIRS = HEADS // 2
TILES = TOKENS // P
EXPERTS = 8
SLOT_TILES = TILES + EXPERTS
SLOTS = SLOT_TILES * P
MT = 256
TPM = MT // P
CH = 64
CPT, CPM = P // CH, MT // CH
MPS = SEQ // MT
MACROS = TOKENS // MT
XBC_T = 5
GROUP = 4
LN_EPS, RMS_EPS = 1e-5, 1e-5
ROUND = 1.5 * 2.0 ** 23
TWO_PI = 2.0 * math.pi
MAX_DECAY = 60.0
LEVELS = int(math.log2(CH))
TRIG = TWO_PI * (1.0 - 2.0 ** -22)

CONST, _at = {}, 0
for _n, _w in (("ident", P), ("causal", P), ("before", P), ("ones", P), ("restart", MT), ("tilestart", TILES * EXPERTS),
               ("first", EXPERTS), ("slot", SLOT_TILES), ("quarter", 1), ("halfpi", 1), ("minushalf", 8), ("ownhead", 2)):
    CONST[_n] = (_at, _w)
    _at += _w
CONST_W = _at
COLS, _at = {}, 0
for _n, _w in (("conv_w", XBC_T * D_CONV), ("conv_b", XBC_T), ("D", PAIRS), ("norm_w", PAIRS), ("lb", PAIRS), ("eta", PAIRS)):
    COLS[_n] = (_at, _w)
    _at += _w
COLS_W = _at


def mixer_and_experts(nc, x, const, halvings, cols, w_in, w_small, w_lora1, w_lora2, w_out, rows, w_exp, b_exp, out):
    ctx = ExitStack()
    with ctx:
        def sb(name, shape, dt=F32):
            return ctx.enter_context(nc.sbuf_tensor(name, shape, dt))

        def sem(name):
            return ctx.enter_context(nc.semaphore(name))

        def scratch(name, shape):
            return nc.dram_tensor(name, shape, F32, kind="Internal").ap()

        xnT_d = scratch("xnT_d", (P, KT, TOKENS))
        dtT_d = scratch("dtT_d", (HEADS, TOKENS))
        table_d = scratch("table_d", (SLOTS, D_MODEL))
        expert_d = scratch("expert_d", (SLOTS, D_MODEL))
        bc_d = scratch("bc_d", (P, MT))

        cst = sb("cst", [P, CONST_W])
        col = sb("col", [P, COLS_W])
        win = sb("win", [P, KT, (XBC_T + PAIRS) * P])
        wsm = sb("wsm", [P, KT, 2 * HEADS])
        wl1 = sb("wl1", [P, KT, LORA])
        wl2 = sb("wl2", [LORA + 1, PAIRS * P])
        wout = sb("wout", [P, PAIRS, D_MODEL])
        rowc = sb("rowc", [P, 2 * HEADS])
        eta2 = sb("eta2", [P, PAIRS])
        dt_tok = sb("dt_tok", [P, TILES, HEADS])
        gate = sb("gate", [P, TILES])
        slot_of = sb("slot_of", [P, TILES], I32)
        tile_expert = sb("tile_expert", [P, SLOT_TILES], I32)
        halve = sb("halve", [P, 1], I32)

        class Region:

            def __init__(self, name, width):
                self.t, self.width, self.at = sb(name, [P, width]), width, 0

            def again(self):
                self.at = 0

            def take(self, *dims):
                n = math.prod(dims)
                assert self.at + n <= self.width
                v = self.t[:, self.at:self.at + n]
                self.at += n
                if len(dims) == 2:
                    v = v.rearrange("p (a b) -> p a b", a=dims[0])
                if len(dims) == 3:
                    v = v.rearrange("p (a b c) -> p a b c", a=dims[0], b=dims[1])
                return v

        r_tokens, r_route = Region("r_tokens", TILES * D_MODEL), Region("r_route", 6144)
        r_tiles, r_expw = Region("r_tiles", 6144), Region("r_expw", 6144)
        r_mixer = Region("r_mixer", 5200)

        pst = [ctx.enter_context(nc.psum_tensor(f"ps{n}", [P, 2, 512], F32)) for n in range(4)]

        def bank(n):
            return pst[n // 2][:, n % 2, :]

        def k(name):
            a, w = CONST[name]
            return cst[:, a:a + w]

        def c(name, n=0, w=1):
            a = COLS[name][0] + n
            return col[:, a:a + w]

        ident = k("ident")

        xn_all = r_tokens.take(TILES, D_MODEL)
        logits = r_route.take(TILES, EXPERTS)
        zeros = r_expw.take(8, D_MODEL)
        a_in = [r.take(GROUP, D_MODEL) for r in (r_tiles, r_tiles, r_expw, r_expw)]
        a_xn = [r_tiles.take(GROUP, D_MODEL) for _ in range(2)]
        a_xT = [r_tiles.take(KT, GROUP * P) for _ in range(2)]
        AHEAD = len(a_in)
        stats = sb("stats", [P, GROUP, nc.vector.BN_STATS_DIM])
        mv = [sb(f"mv{b}", [P, GROUP, nc.vector.BN_AGGR_DIM]) for b in range(2)]
        veps = sb("veps", [P, GROUP])
        rstd = [sb(f"rstd{b}", [P, GROUP]) for b in range(2)]
        shift = [sb(f"shift{b}", [P, GROUP]) for b in range(2)]

        weights_in = sem("weights_in")
        N_WEIGHTS = 9
        a_loaded = [sem(f"a_loaded{b}") for b in range(AHEAD)]
        a_stats, a_mv = sem("a_stats"), sem("a_mv")
        a_veps, a_rstd, a_shift, a_norm, a_kept, a_turned, a_evac, a_small = (sem(n) for n in (
            "a_veps", "a_rstd", "a_shift", "a_norm", "a_kept", "a_turned", "a_evac", "a_small"))
        a_read = sem("a_read")
        a_stored = [sem(f"a_stored{b}") for b in range(2)]
        passed = sem("passed")
        pads_zero, zeroed = sem("pads_zero"), sem("zeroed")

        GROUPS = TILES // GROUP
        QUADS = GROUPS // AHEAD
        GT = GROUP * P
        a_T = [pst[0], pst[1]]
        a_S = [bank(4), bank(5)]

        def after(eng, signal, count):
            if not isinstance(count, int) or count > 0:
                eng.wait_ge(signal, count)

        def quads(eng, quad):
            quad(0)
            with eng.Fori(1, QUADS - 1) as i:
                quad(i)
            quad(QUADS - 1)

        with nc.Block() as block:
            @block.sync
            def _(sp):
                for dst, src in ((cst[:, :], const), (col[:, :], cols), (win[:, :, :], w_in), (wsm[:, :, :], w_small),
                                 (wl1[:, :, :], w_lora1), (wl2[:, :], w_lora2), (wout[:, :, :], w_out),
                                 (rowc[:, 0:HEADS], rows[0:1, 0:HEADS].broadcast_to([P, HEADS])),
                                 (rowc[:, HEADS:], rows[0:1, HEADS:2 * HEADS].broadcast_to([P, HEADS]))):
                    sp.dma_start(dst, src).then_inc(weights_in, 16)

                def quad(i):
                    for b in range(AHEAD):
                        g = AHEAD * i + b
                        after(sp, a_norm, g - AHEAD + 1)
                        after(sp, a_kept, g - AHEAD + 1)
                        sp.dma_start(a_in[b], x[bass.ds(g * GT, GT), :].rearrange("(t p) d -> p t d", p=P)).then_inc(a_loaded[b], 16)

                quads(sp, quad)

            @block.vector
            def _(dve):
                def moments(g, b, n):
                    dve.wait_ge(a_loaded[b], 16 * n + 16)
                    for t in range(GROUP):
                        nc.vector.bn_stats(stats[:, t, :], a_in[b][:, t, :]).then_inc(a_stats, 1)
                    for t in range(GROUP):
                        if t == 0:
                            dve.wait_ge(a_stats, GROUP * (g + 1))
                            dve.sem_inc(passed, 1)
                        nc.vector.bn_aggr(mv[b % 2][:, t, :], stats[:, t, :]).then_inc(a_mv, 1)
                    dve.wait_ge(a_mv, GROUP * (g + 1))
                    after(dve, a_rstd, g)
                    nc.vector.tensor_scalar(veps[:, :], mv[b % 2][:, :, 1], LN_EPS, None, ALU.add).then_inc(a_veps, 1)

                def normalise(g, b):
                    h = b % 2
                    dve.wait_ge(a_rstd, g + 1)
                    after(dve, a_kept, g - 1)
                    nc.vector.scalar_tensor_tensor(shift[h][:, :], mv[h][:, :, 0], -1.0, rstd[h][:, :], ALU.mult, ALU.mult).then_inc(a_shift, 1)
                    dve.wait_ge(a_shift, g + 1)
                    after(dve, a_turned, g - 1)
                    for t in range(GROUP):
                        last = nc.vector.tensor_scalar(a_xn[h][:, t, :], a_in[b][:, t, :], rstd[h][:, t:t + 1], shift[h][:, t:t + 1], ALU.mult, ALU.add)
                    last.then_inc(a_norm, 1)

                def read(g, b):
                    dve.wait_ge(a_small, g + 1)
                    small = a_S[b % 2][:, 0:GROUP * 2 * HEADS].rearrange("p (t e) -> p t e", t=GROUP)
                    nc.vector.tensor_tensor(dt_tok[:, bass.ds(g * GROUP, GROUP), :], small[:, :, 0:HEADS],
                                            rowc[:, None, 0:HEADS].broadcast_to([P, GROUP, HEADS]), ALU.add).then_inc(a_read, 1)
                    nc.vector.tensor_tensor(logits[:, bass.ds(g * GROUP, GROUP), :], small[:, :, HEADS:],
                                            rowc[:, None, HEADS:].broadcast_to([P, GROUP, HEADS]), ALU.add).then_inc(a_read, 1)

                def quad(i):
                    for b in range(AHEAD):
                        g = AHEAD * i + b
                        if not (isinstance(i, int) and g == GROUPS - 1):
                            moments(g + 1, (b + 1) % AHEAD, i + (b + 1) // AHEAD)
                        normalise(g, b)
                        if not (isinstance(i, int) and g < 2):
                            read(g - 2, (b - 2) % AHEAD)

                moments(0, 0, 0)
                dve.wait_ge(weights_in, 16 * N_WEIGHTS)
                quads(dve, quad)
                read(GROUPS - 2, AHEAD - 2)
                read(GROUPS - 1, AHEAD - 1)

            @block.gpsimd
            def _(pool):
                pool.memset(zeros, 0.0).then_inc(zeroed, 1)
                pool.wait_ge(weights_in, 16 * N_WEIGHTS)

                def quad(i):
                    for b in range(AHEAD):
                        g = AHEAD * i + b
                        pool.wait_ge(a_veps, g + 1)
                        after(pool, a_norm, g - 1)
                        after(pool, a_kept, g - 1)
                        nc.gpsimd.tensor_tensor(rstd[b % 2][:, :], veps[:, :], k("minushalf")[:, 0:GROUP], ALU.pow).then_inc(a_rstd, 1)

                quads(pool, quad)

            @block.scalar
            def _(act):
                act.wait_ge(zeroed, 1)
                for n in range(SLOT_TILES // 8):
                    act.dma_start(table_d[n * 8 * P:(n + 1) * 8 * P, :].rearrange("(t p) d -> p t d", p=P), zeros).then_inc(pads_zero, 16)
                act.wait_ge(weights_in, 16 * N_WEIGHTS)

                def keep(g, b):
                    act.wait_ge(a_shift, g + 1)
                    act.sem_inc(passed, 1)
                    for t in range(GROUP):
                        last = nc.scalar.activation(xn_all[:, bass.ds(g * GROUP + t, 1), :], a_in[b][:, t:t + 1, :], ACT.Identity,
                                                    bias=shift[b % 2][:, t:t + 1], scale=rstd[b % 2][:, t:t + 1])
                    last.then_inc(a_kept, 1)

                def store(g, b, n):
                    h = b % 2
                    act.wait_ge(a_turned, g + 1)
                    after(act, a_stored[h], 16 * n)
                    after(act, a_small, g - 1)
                    nc.scalar.activation(a_xT[h], a_T[h][:, :, :], ACT.Copy).then_inc(a_evac, 1)
                    act.wait_ge(a_evac, g + 1)
                    act.dma_start(xnT_d[:, :, bass.ds(g * GT, GT)], a_xT[h]).then_inc(a_stored[h], 16)

                def quad(i):
                    for b in range(AHEAD):
                        g = AHEAD * i + b
                        keep(g, b)
                        if not (isinstance(i, int) and g == 0):
                            store(g - 1, (b - 1) % AHEAD, 2 * i + (b + 1) // 2 - 1)

                quads(act, quad)
                store(GROUPS - 1, AHEAD - 1, GROUPS // 2 - 1)
                for b in range(2):
                    act.wait_ge(a_stored[b], 16 * (GROUPS // 2))
                act.wait_ge(pads_zero, 16 * (SLOT_TILES // 8))

            @block.tensor
            def _(pe):
                pe.wait_ge(weights_in, 16 * N_WEIGHTS)

                def turn(g, b):
                    h = b % 2
                    pe.wait_ge(a_norm, g + 1)
                    after(pe, a_evac, g - 1)
                    for kt in range(KT):
                        for t in range(GROUP):
                            last = nc.tensor.transpose(a_T[h][:, kt, t * P:(t + 1) * P], a_xn[h][:, t, kt * P:(kt + 1) * P], ident)
                    last.then_inc(a_turned, 1)

                def small(g, b):
                    h = b % 2
                    pe.wait_ge(a_evac, g + 1)
                    after(pe, a_read, 2 * (g - 1))
                    for t in range(GROUP):
                        for kt in range(KT):
                            last = nc.tensor.matmul(a_S[h][:, t * 2 * HEADS:(t + 1) * 2 * HEADS], a_xT[h][:, kt, t * P:(t + 1) * P],
                                                    wsm[:, kt, :], start=(kt == 0), stop=(kt == KT - 1))
                    last.then_inc(a_small, 1)

                def quad(i):
                    for b in range(AHEAD):
                        g = AHEAD * i + b
                        turn(g, b)
                        if not (isinstance(i, int) and g == 0):
                            small(g - 1, (b - 1) % AHEAD)

                quads(pe, quad)
                small(GROUPS - 1, AHEAD - 1)

        TE = TILES * EXPERTS
        r_route.again(), r_expw.again()
        logits = r_route.take(TILES, EXPERTS)
        f1, f2, f3, f4, f5, onehot = (r_route.take(TILES, EXPERTS) for _ in range(6))
        incl = r_route.take(EXPERTS, TILES)
        dtT = r_route.take(4, P)
        t64 = [r_route.take(TILES) for _ in range(4)]
        e8 = [r_route.take(EXPERTS) for _ in range(6)]
        ge = r_route.take(SLOT_TILES, EXPERTS)
        ends = r_route.take(SLOT_TILES)
        most = r_route.take(EXPERTS)
        lam_rows = r_tiles.t[:, 0:2 * HEADS * NBLK].rearrange("p (n h k) -> p n h k", n=2, h=HEADS)
        e8i = sb("e8i", [P, EXPERTS], I32)
        rv, ra, rp, scattered, dt_stored, r_ew = (sem(n) for n in ("rv", "ra", "rp", "scattered", "dt_stored", "r_ew"))
        w8 = r_expw.take(KT * EXPERTS, D_MODEL)
        b8 = r_expw.take(EXPERTS, D_MODEL)

        def over(v, *shape):
            return v.broadcast_to([P, *shape])

        with nc.Block() as block:
            @block.sync
            def _(sp):
                sp.dma_start(w8, w_exp).then_inc(r_ew, 16)
                sp.dma_start(b8, b_exp.rearrange("e d -> (e d)")[None, :].broadcast_to([P, EXPERTS * D_MODEL]).rearrange("p (e d) -> p e d", e=EXPERTS)).then_inc(r_ew, 16)
                sp.dma_start(r_tiles.t[:, 0:2 * HEADS * NBLK], rows[0:1, 2 * HEADS:].broadcast_to([P, 2 * HEADS * NBLK])).then_inc(r_ew, 16)
                sp.wait_ge(ra, 3)
                for n in range(4):
                    sp.dma_start(dtT_d[:, n * 16 * P:(n + 1) * 16 * P].rearrange("h (t s) -> t h s", s=P),
                                 dtT[:, n, :]).then_inc(dt_stored, 16)
                sp.wait_ge(dt_stored, 64)
                sp.wait_ge(r_ew, 48)

            @block.vector
            def _(dve):
                done = [0]

                def step(ins):
                    done[0] += 1
                    ins.then_inc(rv, 1)
                    dve.wait_ge(rv, done[0])

                u = dt_tok[:, :, :]
                step(nc.vector.scalar_tensor_tensor(f1, u, -1.0, u, ALU.mult, ALU.max))
                step(nc.vector.tensor_reduce(t64[0], logits, AX_X, ALU.max))
                step(nc.vector.tensor_tensor(f2, logits, over(t64[0][:, :, None], TILES, EXPERTS), ALU.subtract))
                dve.wait_ge(ra, 1)
                step(nc.vector.tensor_scalar(f4, f3, 1.0, None, ALU.add))
                step(nc.vector.tensor_scalar(f5, f4, -1.0, 2.0 ** -24, ALU.add, ALU.max))
                step(nc.vector.reciprocal(f5, f5))
                step(nc.vector.tensor_tensor(f5, f5, f3, ALU.mult))
                step(nc.vector.tensor_scalar(f1, f4, 1.0, None, ALU.is_equal))
                dve.wait_ge(ra, 2)
                step(nc.vector.tensor_tensor(f4, f4, f5, ALU.mult))
                step(nc.vector.tensor_tensor(f1, f1, f3, ALU.mult))
                step(nc.vector.tensor_tensor(f4, f4, f1, ALU.max))
                step(nc.vector.scalar_tensor_tensor(u, u, 0.0, f4, ALU.max, ALU.add))
                step(nc.vector.tensor_reduce(t64[1], onehot, AX_X, ALU.add))
                step(nc.vector.reciprocal(gate[:, :], t64[1]))
                step(nc.vector.tensor_tensor(f1, logits, over(t64[0][:, :, None], TILES, EXPERTS), ALU.is_equal))
                step(nc.vector.tensor_tensor(f1, f1, over(k("first")[:, None, :], TILES, EXPERTS), ALU.mult))
                step(nc.vector.tensor_reduce(t64[2], f1, AX_X, ALU.max))
                step(nc.vector.tensor_tensor(onehot, f1, over(t64[2][:, :, None], TILES, EXPERTS), ALU.is_equal))
                assert done[0] == 18
                dve.wait_ge(rp, 2)
                step(nc.vector.tensor_copy(f2.rearrange("p t e -> p (t e)"), bank(3)))
                by_expert = bank(2).rearrange("p (t e) -> p e t", t=TILES)
                step(nc.vector.tensor_copy(f3.rearrange("p a b -> p (a b)").rearrange("p (e t) -> p e t", e=EXPERTS), by_expert))
                counts = f3.rearrange("p a b -> p (a b)")
                step(nc.vector.tensor_tensor_scan(incl.rearrange("p e t -> p (e t)"), k("tilestart"), counts, 0.0, ALU.mult, ALU.add))
                step(nc.vector.tensor_scalar(e8[0], incl[:, :, TILES - 1], float(P - 1), None, ALU.add))
                step(nc.vector.tensor_copy(e8i[:, :], e8[0]))
                step(nc.vector.tensor_scalar(e8i[:, :], e8i[:, :], int(math.log2(P)), None, ALU.logical_shift_right))
                step(nc.vector.tensor_copy(e8[1], e8i[:, :]))
                step(nc.vector.tensor_tensor_scan(e8[2], k("ones")[:, 0:EXPERTS], e8[1], 0.0, ALU.mult, ALU.add))
                step(nc.vector.tensor_tensor(e8[3], e8[2], e8[1], ALU.subtract))
                step(nc.vector.tensor_scalar(e8[3], e8[3], float(P), None, ALU.mult))
                step(nc.vector.tensor_tensor(f4.rearrange("p a b -> p (a b)"), incl.rearrange("p e t -> p (e t)"), counts, ALU.subtract))
                earlier = f4.rearrange("p a b -> p (a b)").rearrange("p (e t) -> p t e", e=EXPERTS)
                step(nc.vector.tensor_tensor(f2, f2, earlier, ALU.add))
                step(nc.vector.tensor_tensor(f2, f2, over(e8[3][:, None, :], TILES, EXPERTS), ALU.add))
                step(nc.vector.tensor_tensor(f2, f2, onehot, ALU.mult))
                step(nc.vector.tensor_reduce(t64[3], f2, AX_X, ALU.add))
                step(nc.vector.tensor_copy(slot_of[:, :], t64[3]))
                assert done[0] == 34
                step(nc.vector.tensor_tensor(ge, over(k("slot")[:, :, None], SLOT_TILES, EXPERTS), over(e8[2][:, None, :], SLOT_TILES, EXPERTS), ALU.is_ge))
                step(nc.vector.tensor_reduce(ends, ge, AX_X, ALU.add))
                step(nc.vector.tensor_scalar(ends, ends, float(EXPERTS - 1), None, ALU.min))
                step(nc.vector.tensor_copy(tile_expert[:, :], ends))
                dve.wait_ge(r_ew, 48)
                for n in range(2):
                    step(nc.vector.scalar_tensor_tensor(lam_rows[:, n], lam_rows[:, n], -1.0, lam_rows[:, n], ALU.mult, ALU.max))
                step(nc.vector.scalar_tensor_tensor(lam_rows[:, 0], lam_rows[:, 1], (math.pi / 2) ** 2, lam_rows[:, 0], ALU.mult, ALU.add))
                step(nc.vector.tensor_reduce(most, lam_rows[:, 0], AX_X, ALU.max))
                dve.wait_ge(rp, 4)
                step(nc.vector.tensor_tensor(f1, bank(5).rearrange("p (t h) -> p t h", t=TILES), over(most[:, None, :], TILES, HEADS), ALU.mult))
                step(nc.vector.tensor_reduce(t64[0][:, 0:1], f1.rearrange("p t h -> p (t h)"), AX_X, ALU.max))
                step(nc.vector.tensor_scalar(t64[0][:, 0:1], t64[0][:, 0:1], MAX_DECAY, None, ALU.is_gt))
                step(nc.vector.tensor_copy(halve[:, :], t64[0][:, 0:1]))
                step(nc.vector.tensor_scalar(wl2[:, :], wl2[:, :], 1.0 / TWO_PI, None, ALU.mult))
                for q in range(PAIRS):
                    step(nc.vector.tensor_scalar(wout[:, q, :], wout[:, q, :], c("norm_w", q), None, ALU.mult))

            @block.scalar
            def _(act):
                act.wait_ge(rv, 1)
                nc.scalar.activation(f3, f1, ACT.Exp, scale=-1.0).then_inc(ra, 1)
                act.wait_ge(rv, 8)
                nc.scalar.activation(onehot, f2, ACT.Exp)
                nc.scalar.activation(f4, f4, ACT.Ln).then_inc(ra, 1)
                act.wait_ge(rp, 3)
                nc.scalar.activation(dtT.rearrange("p n s -> p (n s)"), bank(4), ACT.Copy).then_inc(ra, 1)

            @block.tensor
            def _(pe):
                pe.wait_ge(rv, 18)
                flat = onehot.rearrange("p t e -> p (t e)")
                nc.tensor.matmul(bank(3), k("before"), flat, start=True, stop=True).then_inc(rp, 1)
                nc.tensor.matmul(bank(2), k("ones"), flat, start=True, stop=True).then_inc(rp, 1)
                dt_flat = dt_tok[:, :, :].rearrange("p t h -> p (t h)")
                for n in range(4):
                    last = nc.tensor.transpose(bank(4)[:, n * P:(n + 1) * P], dt_flat[:, n * P:(n + 1) * P], ident)
                last.then_inc(rp, 1)
                nc.tensor.matmul(bank(5), k("ones"), dt_flat, start=True, stop=True).then_inc(rp, 1)

            @block.gpsimd
            def _(pool):
                pool.wait_ge(rv, 34)
                for t in range(TILES):
                    pool.indirect_dma_start(table_d, bass.IndirectOffsetOnAxis(ap=slot_of[:, t:t + 1], axis=0), xn_all[:, t, :], None).then_inc(scattered, 16)
                pool.wait_ge(scattered, 16 * TILES)

        r_tiles.again()
        e_in = [r_tiles.take(GROUP, D_MODEL) for _ in range(2)]
        e_xT = [r_tiles.take(KT, GROUP * P) for _ in range(2)]
        e_out = [r_tiles.take(GROUP, D_MODEL) for _ in range(2)]
        e_loaded, e_turned, e_evac, e_mm, e_added, e_stored = ([sem(f"{n}{b}") for b in range(2)] for n in (
            "e_loaded", "e_turned", "e_evac", "e_mm", "e_added", "e_stored"))
        E_HALF = SLOT_TILES // GROUP // 2
        e_T = [pst[0], pst[1]]
        e_Y = [pst[2], pst[3]]

        with nc.Block() as block:
            @block.sync
            def _(sp):
                with sp.Fori(0, E_HALF) as i:
                    for b in range(2):
                        sp.wait_ge(e_turned[b], i)
                        sp.dma_start(e_in[b], table_d[bass.ds((2 * i + b) * GT, GT), :].rearrange("(t p) d -> p t d", p=P)).then_inc(e_loaded[b], 16)

            @block.tensor
            def _(pe):
                def turn(i, b):
                    pe.wait_ge(e_loaded[b], 16 * i + 16)
                    pe.wait_ge(e_evac[b], i)
                    for t in range(GROUP):
                        for kt in range(KT):
                            last = nc.tensor.transpose(e_T[b][:, kt, t * P:(t + 1) * P], e_in[b][:, t, kt * P:(kt + 1) * P], ident)
                    last.then_inc(e_turned[b], 1)

                def products(i, b):
                    pe.wait_ge(e_evac[b], i + 1)
                    pe.wait_ge(e_added[b], GROUP * i)
                    for t in range(GROUP):
                        e = pe.value_load(tile_expert[0:1, bass.ds((2 * i + b) * GROUP + t, 1)], min_val=0, max_val=EXPERTS - 1)
                        for kt in range(KT):
                            last = nc.tensor.matmul(e_Y[b][:, t // 2, (t % 2) * D_MODEL:(t % 2 + 1) * D_MODEL],
                                                    e_xT[b][:, kt, t * P:(t + 1) * P],
                                                    w8[:, bass.ds(e + kt * EXPERTS, 1), :].rearrange("p o d -> p (o d)"),
                                                    start=(kt == 0), stop=(kt == KT - 1))
                    last.then_inc(e_mm[b], 1)

                turn(0, 0)
                with pe.Fori(0, E_HALF - 1) as i:
                    turn(i, 1)
                    products(i, 0)
                    turn(i + 1, 0)
                    products(i, 1)
                turn(E_HALF - 1, 1)
                products(E_HALF - 1, 0)
                products(E_HALF - 1, 1)

            @block.scalar
            def _(act):
                def evacuate(i, b):
                    act.wait_ge(e_turned[b], i + 1)
                    act.wait_ge(e_mm[b], i)
                    nc.scalar.activation(e_xT[b], e_T[b][:, :, :], ACT.Copy).then_inc(e_evac[b], 1)

                def store(i, b):
                    act.wait_ge(e_added[b], GROUP * (i + 1))
                    act.dma_start(expert_d[bass.ds((2 * i + b) * GT, GT), :].rearrange("(t p) d -> p t d", p=P), e_out[b]).then_inc(e_stored[b], 16)

                evacuate(0, 0)
                evacuate(0, 1)
                with act.Fori(0, E_HALF - 1) as i:
                    for b in range(2):
                        evacuate(i + 1, b)
                        store(i, b)
                for b in range(2):
                    store(E_HALF - 1, b)
                for b in range(2):
                    act.wait_ge(e_stored[b], 16 * E_HALF)

            @block.vector
            def _(dve):
                with dve.Fori(0, E_HALF) as i:
                    for b in range(2):
                        dve.wait_ge(e_mm[b], i + 1)
                        dve.wait_ge(e_stored[b], 16 * i)
                        for t in range(GROUP):
                            e = dve.value_load(tile_expert[0:1, bass.ds((2 * i + b) * GROUP + t, 1)], min_val=0, max_val=EXPERTS - 1)
                            nc.vector.tensor_tensor(e_out[b][:, t, :], e_Y[b][:, t // 2, (t % 2) * D_MODEL:(t % 2 + 1) * D_MODEL],
                                                    b8[:, bass.ds(e, 1), :].rearrange("p o d -> p (o d)"), ALU.add).then_inc(e_added[b], 1)

        r_tokens.again(), r_route.again(), r_tiles.again(), r_expw.again()
        theta, lam, decay, phase, frac, wave, quad, eneg = (r_tokens.take(PAIRS, MT) for _ in range(8))
        epos = sb("epos", [P, PAIRS, MT])[:, :, :]
        quad_grow = sb("quad_grow", [P, PAIRS, MT])[:, :, :]
        rep = r_expw.take(6, MT)
        c_in = [r_tokens.take(PAIRS, MT) for _ in range(2)]
        c_own = [r_tokens.take(PAIRS, MT) for _ in range(2)]
        grow = [r_tokens.take(PAIRS, MT) for _ in range(2)]
        b_up = [r_tokens.take(PAIRS, MT) for _ in range(2)]
        z_gate = [r_route.take(PAIRS, MT) for _ in range(2)]
        x_skip = [r_route.take(PAIRS, MT) for _ in range(2)]
        x_dt = [r_route.take(TPM, D_INNER) for _ in range(2)]
        end_dec = sb("end_dec", [P, CPM, PAIRS])
        head_dec = [sb(f"head_dec{b}", [P, CPM, PAIRS * 2]) for b in range(2)]
        x_pre = [r_expw.take(XBC_T, MT + D_CONV - 1) for _ in range(2)]
        conv = r_expw.take(XBC_T, MT)
        xbc = r_mixer.take(XBC_T, MT)
        xn_in = [r_mixer.take(KT, MT) for _ in range(2)]
        dt_in = [r_mixer.take(PAIRS, MT) for _ in range(2)]
        zero_dec = sb("zero_dec", [P, PAIRS * 2])
        cb_part = sb("cb_part", [P, 2, MT])[:, :, :]
        hidden = sb("hidden", [LORA + 1, MT])
        b_tok = [r_tiles.take(PAIRS, P) for _ in range(2)]
        att = [r_tiles.take(HEADS, P) for _ in range(2)]
        g = [r_tiles.take(PAIRS, P) for _ in range(2)]
        gsq = r_tiles.take(PAIRS, P)
        state_in = [sb(f"state_in{b}", [P, PAIRS, P]) for b in range(CPM)]
        state = sb("state", [P, PAIRS, HEADDIM])
        level_signs, level_masks = r_mixer.take(LEVELS, P), r_tiles.take(LEVELS + 1, P)
        part_att = conv[:, 0:2, :].rearrange("p n (a t) -> p (n a) t", a=2)
        level_e, level_b, level_c = ([v[1][:, :, n * P:(n + 1) * P] for n in range(2)] for v in (b_up, c_in, c_own))
        x_tile = [sb(f"x_tile{b}", [P, D_MODEL]) for b in range(2)]
        e_tile = [sb(f"e_tile{b}", [P, D_MODEL]) for b in range(2)]
        o_tile = [sb(f"o_tile{b}", [P, D_MODEL]) for b in range(2)]
        e_index = [sb(f"e_index{b}", [P, 1], I32) for b in range(2)]
        ms = [sb(f"ms{b}", [P, 1]) for b in range(2)]
        rms = [sb(f"rms{b}", [P, 1]) for b in range(2)]

        bank_a, bank_b, bank_t, bank_u = bank(0), bank(1), bank(2), bank(3)
        bank_s, bank_y, bank_o = pst[2], bank(6), bank(7)

        made = {n: sem(n) for n in (
            "xproj", "zproj", "thproj",
            "xturned",
            "bturned", "scored", "yout", "oproj",
            "upd",
            "xevac", "zevac",
            "lamsq", "lamd",
            "silu", "xd", "shifted", "rounded",
            "trig", "negd", "expd",
            "bevac", "squared",
            "fabs",
            "halo", "convd",
            "clipped", "rsum", "psum", "fracd",
            "xdt",
            "grown", "bup", "wavedec", "cwave", "cin", "dwave", "cown",
            "masked", "gated", "meansq", "xplus", "final",
            "stated",
            "angle", "lamdt", "headdec",
            "cb",
            "quadgrow", "bquad", "quaddec", "cquad", "dquad",
            "rmsd", "eidx",
            "statein",
            "repd",
            "tail",
            "apart", "signed", "lcdec", "lmasked",
            "lsum",
            "lexpd",
            "lbdec",
            "lscored",
        )}
        s = made
        xn_loaded, dt_loaded = [sem(f"xn_loaded{b}") for b in range(2)], [sem(f"dt_loaded{b}") for b in range(2)]
        x_loaded, e_loaded2, o_stored = ([sem(f"{n}{b}") for b in range(2)] for n in ("x_loaded", "e_gathered", "o_stored"))
        m_ready, m_zero, table_in, bc_out = sem("m_ready"), sem("m_zero"), sem("table_in"), sem("bc_out")

        REPS = 4

        def expand(v, *shape):
            return v.broadcast_to([v.shape[0], *shape])



        def two_ago(m, halved, per):
            if halved:
                return per * m
            return per * (m - 1) if not (isinstance(m, int) and m == 0) else 0

        def reference(v, ch, level):
            half = CH >> (level + 1)
            blocks = v[:, :, ch * P:(ch + 1) * P].rearrange("p q (n w) -> p q n w", w=2 * half)
            return [blocks[:, q] for q in range(PAIRS)], [blocks[:, q, :, half - 1:half].broadcast_to([P, P // (2 * half), 2 * half]) for q in range(PAIRS)]

        def sync_mixer(sp, halved):
            def load(i, j, first=False):
                m, b = MPS * i + j, j % 2
                if not first:
                    sp.wait_ge(s["zproj"], two_ago(m, halved, 2))
                    sp.wait_ge(s["lamdt"], two_ago(m, halved, 1))
                    sp.wait_ge(s["angle"], two_ago(m, halved, 1))
                    sp.sem_inc(passed, 1)
                sp.dma_start(xn_in[b], xnT_d[:, :, bass.ds(m * MT, MT)]).then_inc(xn_loaded[b], 16)
                for e in range(2):
                    src = dtT_d.rearrange("(q e) t -> e q t", e=2)[e:e + 1, :, bass.ds(m * MT, MT)]
                    sp.dma_start(dt_in[b][e * HEADDIM:(e + 1) * HEADDIM, :, :],
                                 src.broadcast_to([HEADDIM, PAIRS, MT])).then_inc(dt_loaded[b], 16)

            def replicate(i, j):
                m = MPS * i + j
                sp.wait_ge(s["cown"], m)
                sp.sem_inc(passed, 1)
                sp.wait_ge(s["silu"], m + 1)
                sp.dma_start(bc_d, xbc[:, XBC_T - 1, :]).then_inc(bc_out, 16)
                sp.wait_ge(bc_out, 16 * m + 16)
                for at in range(0, P, NBLK):
                    sp.dma_start(rep[at:at + NBLK, 0:4, :], bc_d.rearrange("(n k) t -> k n t", n=4)).then_inc(s["repd"], 16)

            def load_x(i, j, ch):
                t = (MPS * i + j) * TPM + ch
                n = MPS * i + j
                sp.wait_ge(s["xplus"], TPM * n)
                sp.dma_start(x_tile[ch][:, :], x[bass.ds(t * P, P), :]).then_inc(x_loaded[ch], 16)

            def store(i, j, ch):
                t = (MPS * i + j) * TPM + ch
                sp.wait_ge(s["final"], t + 1)
                sp.dma_start(out[bass.ds(t * P, P), :], o_tile[ch][:, :]).then_inc(o_stored[ch], 16)

            def body(i, js, last):
                for j in js:
                    left = MPS - 1 - j if last else MPS
                    load_x(i, j, 0)
                    load_x(i, j, 1)
                    if left >= 2:
                        replicate(i, j + 2)
                    store(i, j, 0)
                    if left >= 4:
                        load(i, j + 4)
                    store(i, j, 1)

            if halved:
                sp.dma_start(level_signs, halvings[:, 0:LEVELS, :]).then_inc(table_in, 16)
                sp.dma_start(level_masks, halvings[:, LEVELS:, :]).then_inc(table_in, 16)
                sp.wait_ge(table_in, 32)
                with sp.Fori(0, BATCH) as i:
                    for j in range(MPS):
                        load(i, j)
                        replicate(i, j)
                        for ch in range(TPM):
                            load_x(i, j, ch)
                        for ch in range(TPM):
                            store(i, j, ch)
            else:
                load(0, 0, True)
                load(0, 1, True)
                replicate(0, 0)
                load(0, 2)
                replicate(0, 1)
                load(0, 3)
                with sp.Fori(0, BATCH - 1) as i:
                    body(i, range(MPS), False)
                body(BATCH - 1, range(MPS), True)
            for ch in range(TPM):
                sp.wait_ge(o_stored[ch], 16 * MACROS)

        def tensor_mixer(pe, halved):

            def parity(j):
                return 0 if halved else j % 2

            def project(dst, n, b):
                for kt in range(KT):
                    last = nc.tensor.matmul(dst, win[:, kt, n * P:(n + 1) * P], xn_in[b][:, kt, :], start=(kt == 0), stop=(kt == KT - 1))
                return last

            def front_x(i, j):
                m, n, b = MPS * i + j, 2 * i + j // 2, j % 2
                pe.wait_ge(xn_loaded[b], 16 * n + 16)
                if not (isinstance(m, int) and m < 2):
                    pe.wait_ge(s["zevac"], two_ago(m, halved, 2))
                elif m == 1:
                    pe.wait_ge(s["clipped"], 2)
                project(bank_a[:, 0:MT], 0, b)
                project(bank_a[:, MT:], 1, b).then_inc(s["xproj"], 1)
                project(bank_b[:, 0:MT], 2, b)
                project(bank_b[:, MT:], 3, b).then_inc(s["xproj"], 1)
                pe.wait_ge(s["xevac"], 3 * m + 1)
                project(bank_a[:, 0:MT], 4, b)
                for kt in range(KT):
                    last = nc.tensor.matmul(bank_a[0:LORA, MT:], wl1[:, kt, :], xn_in[b][:, kt, :], start=(kt == 0), stop=(kt == KT - 1))
                last.then_inc(s["xproj"], 1)

            def front_theta(i, j):
                m = MPS * i + j
                pe.wait_ge(s["xevac"], 3 * m + 3)
                for q in range(PAIRS):
                    dst = (bank_b, bank_a)[q // 2][:, (q % 2) * MT:(q % 2 + 1) * MT]
                    last = nc.tensor.matmul(dst, wl2[:, q * P:(q + 1) * P], hidden[:, :], start=True, stop=True)
                    if q % 2:
                        last.then_inc(s["thproj"], 1)

            def front_z(i, j, ahead=0):
                m, b = MPS * i + j, j % 2
                for h, dst in enumerate((bank_b, bank_a)):
                    pe.wait_ge(s["clipped"], 2 * (m + ahead) + h + 1)
                    project(dst[:, 0:MT], XBC_T + 2 * h, b)
                    project(dst[:, MT:], XBC_T + 2 * h + 1, b).then_inc(s["zproj"], 1)

            def front_turn(i, j):
                m = MPS * i + j
                pe.wait_ge(s["silu"], m + 1)
                pe.wait_ge(s["bevac"], TPM * m)
                for ch in range(TPM):
                    pe.wait_ge(s["xdt"], TPM * m + ch)
                    for q in range(PAIRS):
                        last = nc.tensor.transpose(bank_t[:, q * P:(q + 1) * P], xbc[:, q, ch * P:(ch + 1) * P], ident)
                    last.then_inc(s["xturned"], 1)

            def back_turn(i, j, ch):
                m, b, t = MPS * i + j, parity(j), (MPS * i + j) * TPM + ch
                pe.wait_ge(s["bup"], 4 * (m + 1))
                pe.wait_ge(s["xdt"], TPM * (m + 1))
                pe.wait_ge(s["bevac"], t)
                for q in range(PAIRS):
                    last = nc.tensor.transpose(bank_t[:, q * P:(q + 1) * P], b_up[b][:, q, ch * P:(ch + 1) * P], ident)
                last.then_inc(s["bturned"], 1)

            def back_scores(i, j, ch):
                m, b, t = MPS * i + j, parity(j), (MPS * i + j) * TPM + ch
                here = slice(ch * P, (ch + 1) * P)
                pe.wait_ge(s["cown"], m + 1)
                if halved:
                    for level in range(LEVELS + 1):
                        ln, lb = LEVELS * t + level, level % 2
                        pe.wait_ge(s["lmasked"], 2 * ((LEVELS + 1) * t + level))
                        if level < LEVELS:
                            pe.wait_ge(s["lbdec"], ln + 1)
                            pe.wait_ge(s["lcdec"], ln + 1)
                        for e in range(2):
                            part = slice(e * HEADDIM, (e + 1) * HEADDIM)
                            for q in range(PAIRS):
                                lhs, rhs = (level_b[lb][part, q, :], level_c[lb][part, q, :]) if level < LEVELS else (wave[part, q, here], c_own[b][part, q, here])
                                last = nc.tensor.matmul(bank_s[:, e, q * P:(q + 1) * P], lhs, rhs, start=True, stop=True)
                            last.then_inc(s["lscored"], 1)
                    return
                pe.wait_ge(s["grown"], m + 1)
                pe.wait_ge(s["masked"], 2 * t)
                for q in range(PAIRS):
                    for e in range(2):
                        part = slice(e * HEADDIM, (e + 1) * HEADDIM)
                        last = nc.tensor.matmul(bank_s[:, e, q * P:(q + 1) * P], grow[b][part, q, here], c_own[b][part, q, here], start=True, stop=True)
                        if q == PAIRS - 1:
                            last.then_inc(s["scored"], 1)

            def back_update(i, j, ch, c):
                b, t = parity(j), (MPS * i + j) * TPM + ch
                u, rows_c = CPT * t + c, slice(c * CH, (c + 1) * CH)
                pe.wait_ge(s["bevac"], t + 1)
                pe.wait_ge(s["stated"], 2 * u)
                for q in range(PAIRS):
                    last = nc.tensor.matmul(bank_u[:, q * P:(q + 1) * P], b_tok[ch][rows_c, q, :], x_dt[j % 2][rows_c, ch, q * P:(q + 1) * P], start=True, stop=True)
                last.then_inc(s["upd"], 1)

            def back_y(i, j, ch):
                b, t = parity(j), (MPS * i + j) * TPM + ch
                pe.wait_ge(s["masked"], 2 * t + 2)
                pe.wait_ge(s["cin"], MPS * i + j + 1)
                pe.wait_ge(s["gated"], t)
                pe.wait_ge(s["statein"], CPT * t + 1)
                pe.wait_ge(s["xd"], MPS * i + j + 1)
                for q in range(PAIRS):
                    dst = bank_y[:, q * P:(q + 1) * P]
                    for e in range(2):
                        nc.tensor.matmul(dst[e * HEADDIM:(e + 1) * HEADDIM, :], x_dt[j % 2][:, ch, q * P + e * HEADDIM:q * P + (e + 1) * HEADDIM],
                                         att[ch][:, e * PAIRS + q, :], start=True, stop=False, skip_group_check=True)
                    nc.tensor.matmul(dst, ident, x_skip[j % 2][:, q, ch * P:(ch + 1) * P], start=False, stop=False, skip_group_check=True)
                    for n in range(CPT):
                        here = slice(n * CH, (n + 1) * CH)
                        last = nc.tensor.matmul(dst[:, here], state_in[ch * CPT + n][:, q, :], c_in[b][:, q, ch * P + n * CH:ch * P + (n + 1) * CH],
                                                start=False, stop=True, skip_group_check=True)
                last.then_inc(s["yout"], 1)

            def back_out(i, j, ch):
                t = (MPS * i + j) * TPM + ch
                pe.wait_ge(s["gated"], t + 1)
                pe.wait_ge(s["final"], t)
                for q in range(PAIRS):
                    nc.tensor.matmul(bank_o[:, 0:D_MODEL], g[ch][:, q, :], wout[:, q, :], start=(q == 0), stop=(q == PAIRS - 1))
                pe.wait_ge(s["squared"], t + 1)
                for q in range(PAIRS):
                    last = nc.tensor.matmul(bank_o[:, D_MODEL:D_MODEL + 1], gsq[:, q, :], k("ones")[:, 0:1], start=(q == 0), stop=(q == PAIRS - 1))
                last.then_inc(s["oproj"], 1)

            def body(i, js, last):
                for j in js:
                    left = MPS - 1 - j if last else MPS
                    back_turn(i, j, 0)
                    back_scores(i, j, 0)
                    back_update(i, j, 0, 0)
                    back_turn(i, j, 1)
                    back_update(i, j, 0, 1)
                    if left >= 1:
                        front_z(i, j + 1, min(left - 1, 1))
                    back_update(i, j, 1, 0)
                    back_y(i, j, 0)
                    back_scores(i, j, 1)
                    back_out(i, j, 0)
                    if left >= 1:
                        front_turn(i, j + 1)
                    back_update(i, j, 1, 1)
                    back_y(i, j, 1)
                    if left >= 3:
                        front_x(i, j + 3)
                    back_out(i, j, 1)
                    if left >= 3:
                        front_theta(i, j + 3)

            pe.wait_ge(m_ready, 2)
            if halved:
                with pe.Fori(0, BATCH) as i:
                    for j in range(MPS):
                        front_x(i, j)
                        front_theta(i, j)
                        front_z(i, j)
                        front_turn(i, j)
                        for ch in range(TPM):
                            back_turn(i, j, ch)
                            back_scores(i, j, ch)
                            for part in range(CPT):
                                back_update(i, j, ch, part)
                            back_y(i, j, ch)
                            back_out(i, j, ch)
            else:
                front_x(0, 0)
                front_theta(0, 0)
                front_x(0, 1)
                front_theta(0, 1)
                front_z(0, 0, 1)
                front_turn(0, 0)
                front_x(0, 2)
                front_theta(0, 2)
                with pe.Fori(0, BATCH - 1) as i:
                    body(i, range(MPS), False)
                body(BATCH - 1, range(MPS), True)

        def scalar_mixer(act, halved):

            def parity(j):
                return 0 if halved else j % 2

            def front_x(i, j):
                m, b = MPS * i + j, j % 2
                act.wait_ge(s["convd"], 15 * m)
                act.wait_ge(s["halo"], m)
                act.wait_ge(s["silu"], m)
                for n, (dst, w) in enumerate(((bank_a, 2), (bank_b, 2), (bank_a, 1))):
                    act.wait_ge(s["xproj"], 3 * m + n + 1)
                    src = dst[:, 0:w * MT].rearrange("p (n t) -> p n t", n=w)
                    nc.scalar.activation(x_pre[b][:, 2 * n:2 * n + w, D_CONV - 1:], src, ACT.Copy)
                    for d in range(w):
                        ct = 2 * n + d
                        last = nc.scalar.activation(conv[:, ct, :], src[:, d, :], ACT.Identity, bias=c("conv_b", ct),
                                                    scale=c("conv_w", ct * D_CONV + D_CONV - 1))
                    if n == 2:
                        act.wait_ge(s["thproj"], 2 * m)
                        last = nc.scalar.activation(hidden[0:LORA, :], bank_a[0:LORA, MT:], ACT.Tanh)
                    last.then_inc(s["xevac"], 1)

            def front_z(i, j):
                m, b = MPS * i + j, j % 2
                act.wait_ge(s["gated"], two_ago(m, halved, TPM))
                for h, src in enumerate((bank_b, bank_a)):
                    act.wait_ge(s["zproj"], 2 * m + h + 1)
                    nc.scalar.activation(z_gate[b][:, 2 * h:2 * h + 2, :], src.rearrange("p (n t) -> p n t", n=2), ACT.Silu).then_inc(s["zevac"], 1)

            def front_lambda(i, j):
                m = MPS * i + j
                act.wait_ge(s["clipped"], 2 * m + 2)
                act.wait_ge(s["rsum"], 4 * m)
                if halved:
                    act.wait_ge(s["cquad"], m)
                nc.scalar.activation(lam, theta, ACT.Square, scale=TWO_PI).then_inc(s["lamsq"], 1)
                act.wait_ge(s["lamsq"], m + 1)
                for q in range(PAIRS):
                    last = nc.scalar.activation(lam[:, q, :], lam[:, q, :], ACT.Identity, bias=c("lb", q), scale=c("eta", q))
                last.then_inc(s["lamd"], 1)

            def front_silu(i, j):
                m = MPS * i + j
                act.wait_ge(s["convd"], 15 * (m + 1))
                act.wait_ge(s["xturned"], TPM * m)
                act.wait_ge(s["xd"], m)
                act.wait_ge(s["repd"], 16 * REPS * m)
                nc.scalar.activation(xbc, conv, ACT.Silu).then_inc(s["silu"], 1)

            def front_skip(i, j):
                m, b = MPS * i + j, j % 2
                act.wait_ge(s["silu"], m + 1)
                act.wait_ge(s["yout"], two_ago(m, halved, TPM))
                for q in range(PAIRS):
                    last = nc.scalar.activation(x_skip[b][:, q, :], xbc[:, q, :], ACT.Copy, scale=c("D", q))
                last.then_inc(s["xd"], 1)

            def front_round(i, j):
                m = MPS * i + j
                act.wait_ge(s["psum"], 4 * (m + 1))
                act.wait_ge(s["trig"], m)
                nc.scalar.activation(frac, phase, ACT.Copy, bias=ROUND).then_inc(s["shifted"], 1)
                act.wait_ge(s["shifted"], m + 1)
                nc.scalar.activation(frac, frac, ACT.Copy, bias=-ROUND).then_inc(s["rounded"], 1)

            def front_trig(i, j):
                m = MPS * i + j
                act.wait_ge(s["fracd"], m + 1)
                act.wait_ge(s["cown"], m)
                if halved:
                    act.wait_ge(s["lscored"], 2 * (LEVELS + 1) * TPM * m)
                nc.scalar.activation(quad, frac, ACT.Abs).then_inc(s["fabs"], 1)
                nc.scalar.activation(wave, frac, ACT.Sin, scale=TRIG)
                act.wait_ge(s["fabs"], m + 1)
                nc.scalar.activation(quad, quad, ACT.Sin, scale=-TRIG, bias=k("halfpi")).then_inc(s["trig"], 1)

            def front_exp(i, j):
                m = MPS * i + j
                act.wait_ge(s["rsum"], 4 * (m + 1))
                act.wait_ge(s["cown"], m)
                act.wait_ge(s["headdec"], m)
                if halved:
                    act.wait_ge(s["stated"], 2 * CPM * m)
                nc.scalar.activation(eneg, decay, ACT.Exp, scale=-1.0)
                nc.scalar.activation(end_dec[:, :, :], decay.rearrange("p q (c t) -> p c q t", c=CPM)[:, :, :, CH - 1], ACT.Exp, scale=-1.0).then_inc(s["negd"], 1)
                if halved:
                    act.wait_ge(s["tail"], m + 1)
                    nc.scalar.activation(epos, epos, ACT.Exp).then_inc(s["expd"], 1)
                else:
                    nc.scalar.activation(epos, decay, ACT.Exp).then_inc(s["expd"], 1)

            def back_b(i, j, ch):
                t = (MPS * i + j) * TPM + ch
                act.wait_ge(s["bturned"], t + 1)
                act.wait_ge(s["upd"], CPT * (t - 1 if ch else t))
                nc.scalar.activation(b_tok[ch].rearrange("p q s -> p (q s)"), bank_t, ACT.Copy).then_inc(s["bevac"], 1)

            def back_levels(i, j, ch):
                t = (MPS * i + j) * TPM + ch
                for level in range(LEVELS):
                    act.wait_ge(s["signed"], LEVELS * t + level + 1)
                    nc.scalar.activation(level_e[level % 2], level_e[level % 2], ACT.Exp).then_inc(s["lexpd"], 1)

            def back_square(i, j, ch):
                t = (MPS * i + j) * TPM + ch
                act.wait_ge(s["gated"], t + 1)
                act.wait_ge(s["oproj"], t)
                nc.scalar.activation(gsq, g[ch], ACT.Square).then_inc(s["squared"], 1)

            def body(i, js, last):
                for j in js:
                    left = MPS - 1 - j if last else MPS
                    if left >= 2:
                        front_x(i, j + 2)
                    back_b(i, j, 0)
                    if left >= 1:
                        front_skip(i, j + 1)
                    back_b(i, j, 1)
                    if left >= 2:
                        front_lambda(i, j + 2)
                    if left >= 1:
                        front_exp(i, j + 1)
                        front_round(i, j + 1)
                    back_square(i, j, 0)
                    if left >= 1:
                        front_trig(i, j + 1)
                        front_z(i, j + 1)
                    if left >= 2:
                        front_silu(i, j + 2)
                    back_square(i, j, 1)

            act.wait_ge(m_ready, 2)
            if halved:
                with act.Fori(0, BATCH) as i:
                    for j in range(MPS):
                        front_x(i, j)
                        front_lambda(i, j)
                        front_silu(i, j)
                        front_z(i, j)
                        front_round(i, j)
                        front_trig(i, j)
                        front_skip(i, j)
                        front_exp(i, j)
                        for ch in range(TPM):
                            back_b(i, j, ch)
                            back_levels(i, j, ch)
                            back_square(i, j, ch)
            else:
                front_x(0, 0)
                front_lambda(0, 0)
                front_silu(0, 0)
                front_x(0, 1)
                front_skip(0, 0)
                front_lambda(0, 1)
                front_exp(0, 0)
                front_round(0, 0)
                front_trig(0, 0)
                front_z(0, 0)
                front_silu(0, 1)
                with act.Fori(0, BATCH - 1) as i:
                    body(i, range(MPS), False)
                body(BATCH - 1, range(MPS), True)

        def vector_mixer(dve, halved):
            wave_dec, quad_dec = (theta, lam) if halved else (wave, quad)

            def parity(j):
                return 0 if halved else j % 2

            def front_halo(i, j):
                m, b = MPS * i + j, j % 2
                dst = x_pre[b][:, :, 0:D_CONV - 1]
                if j % MPS == 0:
                    nc.vector.memset(dst, 0.0).then_inc(s["halo"], 1)
                else:
                    dve.wait_ge(s["xevac"], 3 * m)
                    nc.vector.tensor_copy(dst, x_pre[1 - b][:, :, MT:]).then_inc(s["halo"], 1)

            def front_conv(i, j):
                m, b = MPS * i + j, j % 2
                dve.wait_ge(s["xevac"], 3 * m + 3)
                dve.wait_ge(s["halo"], m + 1)
                for tap in range(D_CONV - 1):
                    for ct in range(XBC_T):
                        if tap:
                            dve.wait_ge(s["convd"], 15 * m + (tap - 1) * XBC_T + ct + 1)
                        nc.vector.scalar_tensor_tensor(conv[:, ct, :], x_pre[b][:, ct, tap:tap + MT], c("conv_w", ct * D_CONV + tap),
                                                       conv[:, ct, :], ALU.mult, ALU.add).then_inc(s["convd"], 1)

            def front_clip(i, j):
                m = MPS * i + j
                dve.wait_ge(s["lamsq"], m)
                dve.wait_ge(s["psum"], 4 * m)
                if halved:
                    dve.wait_ge(s["dwave"], m)
                for h, src in enumerate((bank_b, bank_a)):
                    dve.wait_ge(s["thproj"], 2 * m + h + 1)
                    nc.vector.tensor_scalar(theta[:, 2 * h:2 * h + 2, :], src.rearrange("p (n t) -> p n t", n=2), 0.25, -0.25,
                                            ALU.min, ALU.max).then_inc(s["clipped"], 1)

            def front_sums(i, j):
                m = MPS * i + j
                dve.wait_ge(s["lamdt"], m + 1)
                dve.wait_ge(s["expd"], m)
                for q in range(PAIRS):
                    nc.vector.tensor_tensor_scan(decay[:, q, :], k("restart"), lam[:, q, :], 0.0, ALU.mult, ALU.add).then_inc(s["rsum"], 1)
                dve.wait_ge(s["angle"], m + 1)
                dve.wait_ge(s["fracd"], m)
                for q in range(PAIRS):
                    start = k("quarter") if j % MPS == 0 else frac[:, q, MT - 1:MT]
                    nc.vector.tensor_tensor_scan(phase[:, q, :], expand(k("ones")[:, 0:1], MT), theta[:, q, :], start, ALU.mult, ALU.add).then_inc(s["psum"], 1)

            def front_frac(i, j):
                m = MPS * i + j
                dve.wait_ge(s["rounded"], m + 1)
                nc.vector.tensor_tensor(frac, phase, frac, ALU.subtract).then_inc(s["fracd"], 1)

            def front_xdt(i, j):
                m, b = MPS * i + j, j % 2
                dve.wait_ge(s["upd"], two_ago(m, halved, CPM))
                dve.wait_ge(s["yout"], two_ago(m, halved, TPM))
                for ch in range(TPM):
                    dve.wait_ge(s["xturned"], TPM * m + ch + 1)
                    dt_col = dt_tok[:, bass.ds(m * TPM + ch, 1), :].rearrange("p o h -> p (o h)")[:, :, None]
                    nc.vector.tensor_tensor(x_dt[b][:, ch, :].rearrange("p (h d) -> p h d", h=HEADS), bank_t.rearrange("p (h d) -> p h d", h=HEADS),
                                            dt_col.broadcast_to([P, HEADS, HEADDIM]), ALU.mult).then_inc(s["xdt"], 1)

            def front_bc(i, j):
                m, b = MPS * i + j, parity(j)
                both = [P, PAIRS, MT]
                if halved:
                    by_chunk = [v.rearrange("p q (c t) -> p (q c) t", c=CPM) for v in (epos, decay)]
                    dve.wait_ge(s["quadgrow"], m)
                    dve.wait_ge(s["rsum"], 4 * (m + 1))
                    nc.vector.tensor_tensor(by_chunk[0], by_chunk[1], by_chunk[1][:, :, CH - 1:CH].broadcast_to([P, PAIRS * CPM, CH]), ALU.subtract).then_inc(s["tail"], 1)
                dve.wait_ge(s["trig"], m + 1)
                dve.wait_ge(s["expd"], m + 1)
                dve.wait_ge(s["yout"], two_ago(m, halved, TPM))
                nc.vector.tensor_tensor(grow[b], wave, epos, ALU.mult).then_inc(s["grown"], 1)
                dve.wait_ge(s["psum"], 4 * (m + 1))
                nc.vector.tensor_tensor(wave_dec, wave, eneg, ALU.mult).then_inc(s["wavedec"], 1)
                dve.wait_ge(s["repd"], 16 * REPS * (m + 1))
                dve.wait_ge(s["wavedec"], m + 1)
                nc.vector.tensor_tensor(c_in[b], rep[:, 2:3, :].broadcast_to(both), wave_dec, ALU.mult).then_inc(s["cwave"], 1)

            def front_sum(i, j):
                m, b = MPS * i + j, parity(j)
                dve.wait_ge(s["cb"], 4 * (m + 1))
                dve.wait_ge(s["wavedec"], m + 1)
                nc.vector.tensor_tensor(c_own[b], rep[:, 4:5, :].broadcast_to([P, PAIRS, MT]), wave if halved else wave_dec, ALU.mult).then_inc(s["dwave"], 1)
                dve.wait_ge(s["grown"], m + 1)
                dve.wait_ge(s["bquad"], m + 1)
                for c in range(CPM):
                    here = slice(c * CH, (c + 1) * CH)
                    nc.vector.scalar_tensor_tensor(b_up[b][:, :, here], grow[b][:, :, here], rep[:, 0, (c + 1) * CH - 1:(c + 1) * CH], quad_grow[:, :, here],
                                                   ALU.mult, ALU.subtract).then_inc(s["bup"], 1)
                dve.wait_ge(s["cquad"], m + 1)
                dve.wait_ge(s["cwave"], m + 1)
                nc.vector.tensor_tensor(c_in[b], c_in[b], eneg, ALU.add).then_inc(s["cin"], 1)
                dve.wait_ge(s["dquad"], m + 1)
                dve.wait_ge(s["dwave"], m + 1)
                nc.vector.tensor_tensor(c_own[b], c_own[b], quad if halved else quad_dec, ALU.add).then_inc(s["cown"], 1)

            def back_levels(i, j, ch):
                m, t = MPS * i + j, (MPS * i + j) * TPM + ch
                here = slice(ch * P, (ch + 1) * P)
                over_pairs = [P, PAIRS, P]
                dve.wait_ge(s["cown"], m + 1)

                def apart(level):
                    ln, dst = LEVELS * t + level, level_e[level % 2]
                    if level >= 2:
                        dve.wait_ge(s["lbdec"], ln - 1)
                        dve.wait_ge(s["lcdec"], ln - 1)
                    else:
                        dve.wait_ge(s["lbdec"], LEVELS * t)
                        dve.wait_ge(s["lcdec"], LEVELS * t)
                    own, ref = reference(decay, ch, level)
                    for q in range(PAIRS):
                        last = nc.vector.tensor_tensor(dst[:, q, :].rearrange("p (n w) -> p n w", w=CH >> level), own[q], ref[q], ALU.subtract)
                    last.then_inc(s["apart"], 1)
                    dve.wait_ge(s["apart"], ln + 1)
                    nc.vector.tensor_tensor(dst, dst, level_signs[:, level:level + 1, :].broadcast_to(over_pairs), ALU.mult).then_inc(s["signed"], 1)

                def add(level):
                    ln = (LEVELS + 1) * t + level
                    mask = level_masks[:, level:level + 1, :].broadcast_to(over_pairs)
                    for h in range(2):
                        dve.wait_ge(s["lscored"], 2 * ln + h + 1)
                        src, dst = bank_s[:, h, :].rearrange("p (h t) -> p h t", h=4), att[ch][:, 4 * h:4 * h + 4, :]
                        if level == 0:
                            nc.vector.tensor_tensor(dst, src, mask, ALU.mult).then_inc(s["lmasked"], 1)
                        else:
                            dve.wait_ge(s["lsum"], 2 * (LEVELS * t + level - 1) + h)
                            nc.vector.tensor_tensor(part_att, src, mask, ALU.mult).then_inc(s["lmasked"], 1)
                            dve.wait_ge(s["lmasked"], 2 * ln + h + 1)
                            last = nc.vector.tensor_tensor(dst, dst, part_att, ALU.add).then_inc(s["lsum"], 1)
                            if level == LEVELS:
                                dve.wait_ge(s["lsum"], 2 * (LEVELS * t + level - 1) + h + 1)
                                dve.sem_inc(s["masked"], 1)

                dve.wait_ge(s["yout"], t - 1 if ch else t)
                apart(0)
                for level in range(LEVELS + 1):
                    if level + 1 < LEVELS:
                        apart(level + 1)
                    if level < LEVELS:
                        dve.wait_ge(s["lexpd"], LEVELS * t + level + 1)
                        if level >= 2:
                            dve.wait_ge(s["lscored"], 2 * ((LEVELS + 1) * t + level - 1))
                        nc.vector.tensor_tensor(level_c[level % 2], c_own[0][:, :, here], level_e[level % 2], ALU.mult).then_inc(s["lcdec"], 1)
                    add(level)

            def back_mask(i, j, ch):
                t = (MPS * i + j) * TPM + ch
                dve.wait_ge(s["yout"], t - 1 if ch else t)
                for h in range(2):
                    dve.wait_ge(s["scored"], 2 * t + h + 1)
                    nc.vector.tensor_tensor(att[ch][:, 4 * h:4 * h + 4, :], bank_s[:, h, :].rearrange("p (h t) -> p h t", h=4),
                                            k("causal")[:, None, :].broadcast_to([P, 4, P]), ALU.mult).then_inc(s["masked"], 1)

            def back_state(i, j, ch, c):
                u = ((MPS * i + j) * TPM + ch) * CPT + c
                dve.wait_ge(s["upd"], u + 1)
                dve.wait_ge(s["statein"], u)
                for e in range(2):
                    part = slice(e * HEADDIM, (e + 1) * HEADDIM)
                    new = bank_u[part, :].rearrange("p (q d) -> p q d", q=PAIRS)[:, :, part]
                    if halved:
                        for q in range(PAIRS):
                            last = nc.vector.scalar_tensor_tensor(state[part, q, :], state_in[ch * CPT + c][part, q, part], end_dec[part, ch * CPT + c, q:q + 1], new[:, q, :], ALU.mult, ALU.add)
                    else:
                        last = nc.vector.tensor_tensor(state[part, :, :], new, state_in[ch * CPT + c][part, :, part], ALU.add)
                    last.then_inc(s["stated"], 1)

            def back_gate(i, j, ch):
                b, t = j % 2, (MPS * i + j) * TPM + ch
                here = slice(ch * P, (ch + 1) * P)
                dve.wait_ge(s["yout"], t + 1)
                dve.wait_ge(s["oproj"], t - 1 if ch else t)
                dve.wait_ge(s["squared"], t - 1 if ch else t)
                dve.wait_ge(s["zevac"], 2 * (MPS * i + j + 1))
                nc.vector.tensor_tensor(g[ch], bank_y.rearrange("p (q t) -> p q t", q=PAIRS), z_gate[b][:, :, here], ALU.mult).then_inc(s["gated"], 1)

            def back_ms(i, j, ch):
                n, t = MPS * i + j, (MPS * i + j) * TPM + ch
                dve.wait_ge(x_loaded[ch], 16 * n + 16)
                dve.wait_ge(e_loaded2[ch], 16 * n + 16)
                gate_col = gate[:, bass.ds(t, 1)]
                nc.vector.scalar_tensor_tensor(x_tile[ch][:, :], e_tile[ch][:, :], gate_col, x_tile[ch][:, :], ALU.mult, ALU.add).then_inc(s["xplus"], 1)
                dve.wait_ge(s["oproj"], t + 1)
                dve.wait_ge(s["rmsd"], t - 1 if ch else t)
                nc.vector.tensor_scalar(ms[ch][:, :], bank_o[:, D_MODEL:D_MODEL + 1], 1.0 / D_INNER, RMS_EPS, ALU.mult, ALU.add).then_inc(s["meansq"], 1)

            def back_final(i, j, ch):
                n, t = MPS * i + j, (MPS * i + j) * TPM + ch
                dve.wait_ge(s["rmsd"], t + 1)
                dve.wait_ge(s["xplus"], t + 1)
                dve.wait_ge(o_stored[ch], 16 * n)
                nc.vector.scalar_tensor_tensor(o_tile[ch][:, :], bank_o[:, 0:D_MODEL], rms[ch][:, :], x_tile[ch][:, :], ALU.mult, ALU.add).then_inc(s["final"], 1)

            def body(i, js, last):
                for j in js:
                    left = MPS - 1 - j if last else MPS
                    back_state(i, j, 0, 0)
                    back_mask(i, j, 0)
                    back_state(i, j, 0, 1)
                    if left >= 2:
                        front_conv(i, j + 2)
                    back_gate(i, j, 0)
                    if left >= 1:
                        front_frac(i, j + 1)
                    back_mask(i, j, 1)
                    back_state(i, j, 1, 0)
                    back_ms(i, j, 0)
                    if left >= 1:
                        front_xdt(i, j + 1)
                    if left >= 2:
                        front_sums(i, j + 2)
                    back_final(i, j, 0)
                    back_gate(i, j, 1)
                    if left >= 1:
                        front_bc(i, j + 1)
                        front_sum(i, j + 1)
                    back_ms(i, j, 1)
                    back_state(i, j, 1, 1)
                    if left >= 3:
                        front_clip(i, j + 3)
                    if left >= 4:
                        front_halo(i, j + 4)
                    back_final(i, j, 1)

            nc.vector.memset(hidden[32:LORA + 1, :], 1.0).then_inc(m_ready, 1)
            nc.vector.memset(state_in[0][:, :, :], 0.0).then_inc(m_zero, 1)
            if halved:
                dve.wait_ge(table_in, 32)
                with dve.Fori(0, BATCH) as i:
                    for j in range(MPS):
                        front_halo(i, j)
                        front_clip(i, j)
                        front_conv(i, j)
                        front_sums(i, j)
                        front_frac(i, j)
                        front_xdt(i, j)
                        front_bc(i, j)
                        front_sum(i, j)
                        for ch in range(TPM):
                            back_levels(i, j, ch)
                            for part in range(CPT):
                                back_state(i, j, ch, part)
                            back_gate(i, j, ch)
                            back_ms(i, j, ch)
                            back_final(i, j, ch)
            else:
                front_halo(0, 0)
                front_clip(0, 0)
                front_halo(0, 1)
                front_conv(0, 0)
                front_sums(0, 0)
                front_clip(0, 1)
                front_halo(0, 2)
                front_conv(0, 1)
                front_frac(0, 0)
                front_xdt(0, 0)
                front_sums(0, 1)
                front_bc(0, 0)
                front_sum(0, 0)
                front_clip(0, 2)
                front_halo(0, 3)
                with dve.Fori(0, BATCH - 1) as i:
                    body(i, range(MPS), False)
                body(BATCH - 1, range(MPS), True)

        def gpsimd_mixer(pool, halved):
            wave_dec, quad_dec = (theta, lam) if halved else (wave, quad)

            def parity(j):
                return 0 if halved else j % 2

            def front_dt(i, j):
                m, n, b = MPS * i + j, 2 * i + j // 2, j % 2
                pool.wait_ge(dt_loaded[b], 32 * (n + 1))
                pool.wait_ge(s["lamsq"], m + 1)
                nc.gpsimd.tensor_tensor(theta, theta, dt_in[b], ALU.mult).then_inc(s["angle"], 1)
                pool.wait_ge(s["lamd"], m + 1)
                nc.gpsimd.tensor_tensor(lam, lam, dt_in[b], ALU.mult).then_inc(s["lamdt"], 1)

            def front_head(i, j):
                m, b = MPS * i + j, j % 2
                shape = [P, CPM * PAIRS, 2]
                pool.wait_ge(s["negd"], m + 1)
                nc.gpsimd.tensor_tensor(head_dec[b][:, :, :].rearrange("p c (q e) -> p (c q) e", e=2), end_dec[:, :, :].rearrange("p c q -> p (c q)")[:, :, None].broadcast_to(shape),
                                        k("ownhead")[:, None, :].broadcast_to(shape), ALU.mult).then_inc(s["headdec"], 1)

            def front_cb(i, j):
                m = MPS * i + j
                b_both, c_re, c_im, re, im = rep[:, 0:2, :], rep[:, 2:3, :], rep[:, 3:4, :], rep[:, 4, :], rep[:, 5, :]
                pool.wait_ge(s["repd"], 16 * REPS * (m + 1))
                pool.wait_ge(s["cown"], m)
                nc.gpsimd.tensor_tensor(rep[:, 4:6, :], c_re.broadcast_to([P, 2, MT]), b_both, ALU.mult).then_inc(s["cb"], 1)
                nc.gpsimd.tensor_tensor(cb_part, c_im.broadcast_to([P, 2, MT]), b_both, ALU.mult).then_inc(s["cb"], 1)
                pool.wait_ge(s["cb"], 4 * m + 2)
                nc.gpsimd.tensor_tensor(re, re, cb_part[:, 1, :], ALU.subtract).then_inc(s["cb"], 1)
                nc.gpsimd.tensor_tensor(im, im, cb_part[:, 0, :], ALU.add).then_inc(s["cb"], 1)

            def front_bc(i, j):
                m = MPS * i + j
                pool.wait_ge(s["trig"], m + 1)
                pool.wait_ge(s["expd"], m + 1)
                nc.gpsimd.tensor_tensor(quad_grow, quad, epos, ALU.mult).then_inc(s["quadgrow"], 1)
                pool.wait_ge(s["rsum"], 4 * (m + 1))
                nc.gpsimd.tensor_tensor(quad_dec, quad, eneg, ALU.mult).then_inc(s["quaddec"], 1)

            def front_products(i, j):
                m = MPS * i + j
                both = [P, PAIRS, MT]
                b_ends = rep[:, 1, :].rearrange("p (c t) -> p c t", c=CPM)[:, None, :, CH - 1:CH]
                by_chunk = quad_grow.rearrange("p q (c t) -> p q c t", c=CPM)
                pool.wait_ge(s["quadgrow"], m + 1)
                nc.gpsimd.tensor_tensor(by_chunk, by_chunk, b_ends.broadcast_to([P, PAIRS, CPM, CH]), ALU.mult).then_inc(s["bquad"], 1)
                pool.wait_ge(s["quaddec"], m + 1)
                pool.wait_ge(s["wavedec"], m + 1)
                nc.gpsimd.tensor_tensor(eneg, rep[:, 3:4, :].broadcast_to(both), quad_dec, ALU.mult).then_inc(s["cquad"], 1)
                pool.wait_ge(s["cquad"], m + 1)
                pool.wait_ge(s["cb"], 4 * (m + 1))
                v = quad if halved else quad_dec
                nc.gpsimd.tensor_tensor(v, rep[:, 5:6, :].broadcast_to(both), v, ALU.mult).then_inc(s["dquad"], 1)

            def back_levels(i, j, ch):
                m, t = MPS * i + j, (MPS * i + j) * TPM + ch
                here = slice(ch * P, (ch + 1) * P)
                pool.wait_ge(s["cown"], m + 1)
                pool.wait_ge(s["cin"], m + 1)
                for level in range(LEVELS):
                    pool.wait_ge(s["lexpd"], LEVELS * t + level + 1)
                    pool.wait_ge(s["lscored"], 2 * ((LEVELS + 1) * t + max(level - 1, 0)))
                    nc.gpsimd.tensor_tensor(level_b[level % 2], wave[:, :, here], level_e[level % 2], ALU.mult).then_inc(s["lbdec"], 1)

            def back_state(i, j, ch, c):
                b, u = j % 2, ((MPS * i + j) * TPM + ch) * CPT + c
                pool.wait_ge(s["stated"], 2 * u + 2)
                t = (MPS * i + j) * TPM + ch
                if c:
                    pool.wait_ge(s["yout"], t)
                elif not (j == 0 and ch == 0):
                    pool.wait_ge(s["yout"], t - 1)
                elif not isinstance(i, int):
                    pool.wait_ge(s["yout"], t)
                shape = [P, PAIRS, 2, HEADDIM]
                dst = state_in[(ch * CPT + c + 1) % CPM][:, :, :].rearrange("p q (e d) -> p q e d", e=2)
                if j == MPS - 1 and ch == TPM - 1 and c == CPT - 1:
                    by = zero_dec[:, :]
                elif halved:
                    by = None
                else:
                    by = head_dec[b][:, ch * CPT + c, :]
                own = k("ownhead")[:, None, :, None] if by is None else by.rearrange("p (q e) -> p q e", e=2)[:, :, :, None]
                nc.gpsimd.tensor_tensor(dst, state[:, :, None, :].broadcast_to(shape), own.broadcast_to(shape), ALU.mult).then_inc(s["statein"], 1)

            def back_gather(i, j, ch):
                n, t = MPS * i + j, (MPS * i + j) * TPM + ch
                pool.wait_ge(s["xplus"], TPM * n)
                pool.wait_ge(e_loaded2[ch], 16 * n)
                pool.sem_inc(passed, 1)
                nc.gpsimd.tensor_copy(e_index[ch][:, :], slot_of[:, bass.ds(t, 1)]).then_inc(s["eidx"], 1)
                pool.wait_ge(s["eidx"], t + 1)
                pool.sem_inc(passed, 1)
                pool.indirect_dma_start(e_tile[ch][:, :], None, expert_d, bass.IndirectOffsetOnAxis(ap=e_index[ch][:, :], axis=0)).then_inc(e_loaded2[ch], 16)

            def back_rms(i, j, ch):
                t = (MPS * i + j) * TPM + ch
                pool.wait_ge(s["meansq"], t + 1)
                pool.wait_ge(s["final"], t)
                nc.gpsimd.tensor_tensor(rms[ch][:, :], ms[ch][:, :], k("minushalf")[:, 0:1], ALU.pow).then_inc(s["rmsd"], 1)

            def body(i, js, last):
                for j in js:
                    left = MPS - 1 - j if last else MPS
                    back_gather(i, j, 0)
                    back_state(i, j, 0, 0)
                    back_gather(i, j, 1)
                    back_state(i, j, 0, 1)
                    if left >= 2:
                        front_dt(i, j + 2)
                    if left >= 1:
                        front_cb(i, j + 1)
                    back_rms(i, j, 0)
                    back_state(i, j, 1, 0)
                    if left >= 1:
                        front_bc(i, j + 1)
                        front_products(i, j + 1)
                    back_rms(i, j, 1)
                    back_state(i, j, 1, 1)
                    if left >= 1:
                        front_head(i, j + 1)

            pool.wait_ge(m_zero, 1)
            nc.gpsimd.memset(zero_dec[:, :], 0.0).then_inc(m_ready, 1)
            pool.wait_ge(m_ready, 2)
            if halved:
                with pool.Fori(0, BATCH) as i:
                    for j in range(MPS):
                        front_dt(i, j)
                        front_cb(i, j)
                        front_head(i, j)
                        front_bc(i, j)
                        front_products(i, j)
                        for ch in range(TPM):
                            back_gather(i, j, ch)
                            back_levels(i, j, ch)
                            for part in range(CPT):
                                back_state(i, j, ch, part)
                            back_rms(i, j, ch)
            else:
                front_dt(0, 0)
                front_dt(0, 1)
                front_cb(0, 0)
                front_bc(0, 0)
                front_products(0, 0)
                front_head(0, 0)
                with pool.Fori(0, BATCH - 1) as i:
                    body(i, range(MPS), False)
                body(BATCH - 1, range(MPS), True)

        with nc.Block() as block:
            @block.sync
            def _(sp):
                chunks_halved = sp.value_load(halve[0:1, 0:1], min_val=0, max_val=1)
                with sp.If(chunks_halved == 0):
                    sync_mixer(sp, False)
                with sp.If(chunks_halved != 0):
                    sync_mixer(sp, True)

            @block.tensor
            def _(pe):
                chunks_halved = pe.value_load(halve[0:1, 0:1], min_val=0, max_val=1)
                with pe.If(chunks_halved == 0):
                    tensor_mixer(pe, False)
                with pe.If(chunks_halved != 0):
                    tensor_mixer(pe, True)

            @block.scalar
            def _(act):
                chunks_halved = act.value_load(halve[0:1, 0:1], min_val=0, max_val=1)
                with act.If(chunks_halved == 0):
                    scalar_mixer(act, False)
                with act.If(chunks_halved != 0):
                    scalar_mixer(act, True)

            @block.vector
            def _(dve):
                chunks_halved = dve.value_load(halve[0:1, 0:1], min_val=0, max_val=1)
                with dve.If(chunks_halved == 0):
                    vector_mixer(dve, False)
                with dve.If(chunks_halved != 0):
                    vector_mixer(dve, True)

            @block.gpsimd
            def _(pool):
                chunks_halved = pool.value_load(halve[0:1, 0:1], min_val=0, max_val=1)
                with pool.If(chunks_halved == 0):
                    gpsimd_mixer(pool, False)
                with pool.If(chunks_halved != 0):
                    gpsimd_mixer(pool, True)


_OUT = (BATCH, SEQ, D_MODEL)


def kernel(**inputs):
    import numpy as np
    import concourse.bacc as bacc
    from concourse.bass_utils import run_bass_kernel_spmd

    a = {n.replace("L0_", ""): np.asarray(v) for n, v in inputs.items()}

    const = np.zeros((P, CONST_W), np.float32)

    def put(name, v):
        const[:, CONST[name][0]:CONST[name][0] + CONST[name][1]] = v
    row, colm = np.arange(P)[:, None], np.arange(P)[None, :]
    put("ident", row == colm)
    put("causal", (row <= colm) & (row // CH == colm // CH))
    put("before", row < colm)
    put("ones", 1.0)
    put("restart", (np.arange(MT) % CH != 0)[None, :])
    put("tilestart", (np.arange(TILES * EXPERTS) % TILES != 0)[None, :])
    put("first", (EXPERTS - np.arange(EXPERTS))[None, :])
    put("slot", np.arange(SLOT_TILES)[None, :])
    real = (row // NBLK) % 2 == 0
    put("quarter", np.where(real, 0.25, 0.0))
    put("halfpi", math.pi / 2)
    put("minushalf", -0.5)
    put("ownhead", row // (2 * NBLK) == np.arange(2)[None, :])

    halvings = np.zeros((P, 2 * LEVELS + 1, P), np.float32)
    for level in range(LEVELS):
        half = CH >> (level + 1)
        first = np.arange(P) % (2 * half) < half
        halvings[:, level] = np.where(first, 1.0, -1.0)
        halvings[:, LEVELS + level] = (row // (2 * half) == colm // (2 * half)) & first[:, None] & ~first[None, :]
    halvings[:, 2 * LEVELS] = row == colm

    def by_tile(v):
        return np.moveaxis(v.reshape(-1, P, *v.shape[1:]), 0, 1)

    bc = D_INNER + np.concatenate([np.arange(h, h + 2 * NBLK, 2) for h in (0, 1, 2 * NBLK, 2 * NBLK + 1)])
    xbc = np.concatenate([np.arange(D_INNER), bc])
    w = a["attn_in_proj_w"]
    w_in = np.concatenate([w[D_INNER:][xbc], w[:D_INNER]]).T
    w_small = np.concatenate([w[-HEADS:].T, a["ffn_router_w"]], axis=1)

    def spread(v):
        return np.broadcast_to(v.reshape(PAIRS, 2, 1, NBLK), (PAIRS, 2, 2, NBLK)).reshape(PAIRS, P).T

    lora2 = np.concatenate([a["attn_theta_w2"], a["attn_theta_base"].reshape(1, -1)])
    lora2 = np.broadcast_to(lora2.reshape(LORA + 1, PAIRS, 2, 1, NBLK), (LORA + 1, PAIRS, 2, 2, NBLK)).reshape(LORA + 1, PAIRS * P)
    cols = np.concatenate([
        by_tile(a["attn_conv_w"][xbc]).reshape(P, -1), by_tile(a["attn_conv_b"][xbc]).reshape(P, -1),
        by_tile(np.repeat(a["attn_D"], HEADDIM)), by_tile(a["attn_norm_w"]),
        spread(a["attn_lambda_base"]), spread(a["attn_viscosity_eta"])], axis=1)
    arrays = {
        "x": a["attn_x"].reshape(TOKENS, D_MODEL), "const": const, "halvings": halvings, "cols": cols, "w_in": by_tile(w_in), "w_small": by_tile(w_small),
        "w_lora1": by_tile(a["attn_theta_w1"]), "w_lora2": lora2, "w_out": by_tile(a["attn_out_proj_w"].T),
        "rows": np.concatenate([a[n].reshape(-1) for n in ("attn_dt_bias", "ffn_router_b", "attn_lambda_base", "attn_viscosity_eta")])[None, :],
        "w_exp": by_tile(np.moveaxis(a["ffn_expert_w"], 0, 1)).reshape(P, KT * EXPERTS, D_MODEL),
        "b_exp": a["ffn_expert_b"],
    }
    nc = bacc.Bacc("TRN2", target_bir_lowering=False, num_devices=1)
    arrays = {n: np.ascontiguousarray(v) for n, v in arrays.items()}
    aps = [nc.dram_tensor(n, v.shape, mybir.dt.from_np(v.dtype), kind="ExternalInput").ap() for n, v in arrays.items()]
    out = nc.dram_tensor("out", (TOKENS, D_MODEL), F32, kind="ExternalOutput").ap()
    mixer_and_experts(nc, *aps, out)
    r = run_bass_kernel_spmd(nc, [arrays], core_ids=[0])
    return r.results[0]["out"].reshape(_OUT)
```

```python
import concourse.bass as bass
from concourse import mybir
from contextlib import ExitStack
import math

F32 = mybir.dt.float32
I32 = mybir.dt.int32
BF16 = mybir.dt.bfloat16
ALU = mybir.AluOpType
ACT = mybir.ActivationFunctionType
AX_X = mybir.AxisListType.X

P = 128
BATCH, SEQ, D_MODEL = 8, 1024, 256
TOKENS = BATCH * SEQ
KT = D_MODEL // P
D_INNER, HEADS, HEADDIM, NBLK, LORA, D_CONV = 512, 8, 64, 32, 48, 4
PAIRS = HEADS // 2
TILES = TOKENS // P
EXPERTS = 8
SLOT_TILES = TILES + EXPERTS
SLOTS = SLOT_TILES * P
MT = 256
TPM = MT // P
CH = 64
CPT, CPM = P // CH, MT // CH
assert CPT == 2
MPS = SEQ // MT
MACROS = TOKENS // MT
XBC_T = 5
GROUP = 4
LN_EPS, RMS_EPS = 1e-5, 1e-5
ROUND = 1.5 * 2.0 ** 23
TWO_PI = 2.0 * math.pi
MAX_DECAY = 60.0
LEVELS = int(math.log2(CH))
TRIG = TWO_PI * (1.0 - 2.0 ** -22)

CONST, _at = {}, 0
for _n, _w in (("ident", P), ("causal", P), ("before", P), ("ones", P), ("restart", MT), ("tilestart", TILES * EXPERTS),
               ("first", EXPERTS), ("slot", SLOT_TILES), ("quarter", 1), ("halfpi", 1), ("minushalf", 8), ("ownhead", 2)):
    CONST[_n] = (_at, _w)
    _at += _w
CONST_W = _at
COLS, _at = {}, 0
for _n, _w in (("conv_w", XBC_T * D_CONV), ("conv_b", XBC_T), ("D", PAIRS), ("norm_w", PAIRS), ("lb", PAIRS), ("eta", PAIRS)):
    COLS[_n] = (_at, _w)
    _at += _w
COLS_W = _at


def mixer_and_experts(nc, x, const, halvings, cols, w_in, w_small, w_lora1, w_lora2, w_out, rows, w_exp, b_exp, ids_d, out):
    ctx = ExitStack()
    with ctx:
        def sb(name, shape, dt=F32):
            return ctx.enter_context(nc.sbuf_tensor(name, shape, dt))

        def sem(name):
            return ctx.enter_context(nc.semaphore(name))

        def scratch(name, shape):
            return nc.dram_tensor(name, shape, F32, kind="Internal").ap()

        xnT_d = scratch("xnT_d", (P, KT, TOKENS))
        dtT_d = scratch("dtT_d", (HEADS, TOKENS))
        xn_d = scratch("xn_d", (TOKENS, D_MODEL))
        expert_d = scratch("expert_d", (SLOTS, D_MODEL))
        bc_d = scratch("bc_d", (P, MT))

        cst = sb("cst", [P, CONST_W])
        col = sb("col", [P, COLS_W])
        win = sb("win", [P, KT, (XBC_T + PAIRS) * P])
        wsm = sb("wsm", [P, KT, 2 * HEADS])
        wl1 = sb("wl1", [P, KT, LORA])
        wl2 = sb("wl2", [LORA + 1, PAIRS * P])
        wout = sb("wout", [P, PAIRS, D_MODEL])
        rowc = sb("rowc", [P, 2 * HEADS])
        eta2 = sb("eta2", [P, PAIRS])
        dt_tok = sb("dt_tok", [P, TILES, HEADS])
        gate = sb("gate", [P, TILES])
        slot_of = sb("slot_of", [P, TILES], I32)
        tile_expert = sb("tile_expert", [P, SLOT_TILES], I32)
        halve = sb("halve", [P, 1], I32)

        class Region:

            def __init__(self, name, width):
                self.t, self.width, self.at = sb(name, [P, width]), width, 0

            def again(self):
                self.at = 0

            def take(self, *dims):
                n = math.prod(dims)
                assert self.at + n <= self.width
                v = self.t[:, self.at:self.at + n]
                self.at += n
                if len(dims) == 2:
                    v = v.rearrange("p (a b) -> p a b", a=dims[0])
                if len(dims) == 3:
                    v = v.rearrange("p (a b c) -> p a b c", a=dims[0], b=dims[1])
                return v

        r_tokens, r_route = Region("r_tokens", TILES * D_MODEL), Region("r_route", 6144)
        r_tiles, r_expw = Region("r_tiles", 6144), Region("r_expw", 6144)
        r_mixer = Region("r_mixer", 5200)

        pst = [ctx.enter_context(nc.psum_tensor(f"ps{n}", [P, 2, 512], F32)) for n in range(4)]

        def bank(n):
            return pst[n // 2][:, n % 2, :]

        def k(name):
            a, w = CONST[name]
            return cst[:, a:a + w]

        def c(name, n=0, w=1):
            a = COLS[name][0] + n
            return col[:, a:a + w]

        ident = k("ident")

        logits = r_route.take(TILES, EXPERTS)
        a_in = [r.take(GROUP, D_MODEL) for r in (r_tiles, r_tiles, r_expw, r_expw)]
        a_xn = [r_tokens.take(GROUP, D_MODEL) for _ in range(4)]
        a_xT = [r_tiles.take(KT, GROUP * P) for _ in range(2)]
        AHEAD = len(a_in)
        stats = sb("stats", [P, GROUP, nc.vector.BN_STATS_DIM])
        mv = [sb(f"mv{b}", [P, GROUP, nc.vector.BN_AGGR_DIM]) for b in range(2)]
        veps = sb("veps", [P, GROUP])
        rstd = [sb(f"rstd{b}", [P, GROUP]) for b in range(2)]
        shift = [sb(f"shift{b}", [P, GROUP]) for b in range(2)]

        weights_in = sem("weights_in")
        consts_in = sem("consts_in")
        N_WEIGHTS, N_CONSTS = 5, 4
        a_loaded = [sem(f"a_loaded{b}") for b in range(AHEAD)]
        a_stats, a_mv = sem("a_stats"), sem("a_mv")
        a_veps, a_rstd, a_shift, a_norm, a_turned, a_evac, a_small, a_small_evac, a_small_turned = (sem(n) for n in (
            "a_veps", "a_rstd", "a_shift", "a_norm", "a_turned", "a_evac", "a_small", "a_small_evac", "a_small_turned"))
        a_read = sem("a_read")
        a_stored = [sem(f"a_stored{b}") for b in range(2)]
        a_put = [sem(f"a_put{b}") for b in range(AHEAD)]
        passed = sem("passed")

        GROUPS = TILES // GROUP
        QUADS = GROUPS // AHEAD
        GT = GROUP * P
        a_T = [pst[0], pst[1]]
        a_S = [bank(4), bank(5)]
        a_small_T = [bank(6), bank(7)]
        a_sT = [r_tokens.take(GROUP * P) for _ in range(2)]

        def after(eng, signal, count):
            if not isinstance(count, int) or count > 0:
                eng.wait_ge(signal, count)

        def quads(eng, quad):
            quad(0)
            with eng.Fori(1, QUADS - 1) as i:
                quad(i)
            quad(QUADS - 1)

        with nc.Block() as block:
            @block.sync
            def _(sp):
                def put(g, b):
                    sp.wait_ge(a_norm, g + 1)
                    sp.dma_start(xn_d[bass.ds(g * GT, GT), :].rearrange("(t p) d -> p t d", p=P), a_xn[b]).then_inc(a_put[b], 16)

                def quad(i):
                    for b in range(AHEAD):
                        g = AHEAD * i + b
                        if not (isinstance(i, int) and i == 0):
                            put(g - AHEAD, b)
                        sp.dma_start(a_in[b], x[bass.ds(g * GT, GT), :].rearrange("(t p) d -> p t d", p=P)).then_inc(a_loaded[b], 16)
                        if isinstance(i, int) and g == 0:
                            for dst, src in ((cst[:, :], const), (wsm[:, :, :], w_small),
                                             (rowc[:, 0:HEADS], rows[0:1, 0:HEADS].broadcast_to([P, HEADS])),
                                             (rowc[:, HEADS:], rows[0:1, HEADS:2 * HEADS].broadcast_to([P, HEADS]))):
                                sp.dma_start(dst, src).then_inc(consts_in, 16)

                quads(sp, quad)
                for dst, src in ((col[:, :], cols), (win[:, :, :], w_in), (wl1[:, :, :], w_lora1), (wl2[:, :], w_lora2),
                                 (wout[:, :, :], w_out)):
                    sp.dma_start(dst, src).then_inc(weights_in, 16)
                for b in range(AHEAD):
                    put(GROUPS - AHEAD + b, b)
                for b in range(AHEAD):
                    sp.wait_ge(a_put[b], 16 * QUADS)
                sp.wait_ge(weights_in, 16 * N_WEIGHTS)

            @block.vector
            def _(dve):
                def moments(g, b, n):
                    dve.wait_ge(a_loaded[b], 16 * n + 16)
                    for t in range(GROUP):
                        nc.vector.bn_stats(stats[:, t, :], a_in[b][:, t, :]).then_inc(a_stats, 1)
                    for t in range(GROUP):
                        if t == 0:
                            dve.wait_ge(a_stats, GROUP * (g + 1))
                            dve.sem_inc(passed, 1)
                        nc.vector.bn_aggr(mv[b % 2][:, t, :], stats[:, t, :]).then_inc(a_mv, 1)
                    dve.wait_ge(a_mv, GROUP * (g + 1))
                    after(dve, a_rstd, g)
                    nc.vector.tensor_scalar(veps[:, :], mv[b % 2][:, :, 1], LN_EPS, None, ALU.add).then_inc(a_veps, 1)

                def normalise(g, b, n):
                    h = b % 2
                    dve.wait_ge(a_rstd, g + 1)
                    nc.vector.scalar_tensor_tensor(shift[h][:, :], mv[h][:, :, 0], -1.0, rstd[h][:, :], ALU.mult, ALU.mult).then_inc(a_shift, 1)
                    dve.wait_ge(a_shift, g + 1)
                    after(dve, a_turned, g - AHEAD + 1)
                    after(dve, a_put[b], 16 * n)
                    for t in range(GROUP):
                        last = nc.vector.tensor_scalar(a_xn[b][:, t, :], a_in[b][:, t, :], rstd[h][:, t:t + 1], shift[h][:, t:t + 1], ALU.mult, ALU.add)
                    last.then_inc(a_norm, 1)

                def read(g, b):
                    dve.wait_ge(a_small_turned, g + 1)
                    small = a_small_T[b % 2][:, 0:GROUP * 2 * HEADS].rearrange("p (t e) -> p t e", t=GROUP)
                    nc.vector.tensor_tensor(dt_tok[:, bass.ds(g * GROUP, GROUP), :], small[:, :, 0:HEADS],
                                            rowc[:, None, 0:HEADS].broadcast_to([P, GROUP, HEADS]), ALU.add).then_inc(a_read, 1)
                    nc.vector.tensor_tensor(logits[:, bass.ds(g * GROUP, GROUP), :], small[:, :, HEADS:],
                                            rowc[:, None, HEADS:].broadcast_to([P, GROUP, HEADS]), ALU.add).then_inc(a_read, 1)

                def quad(i):
                    for b in range(AHEAD):
                        g = AHEAD * i + b
                        if not (isinstance(i, int) and g == GROUPS - 1):
                            moments(g + 1, (b + 1) % AHEAD, i + (b + 1) // AHEAD)
                        normalise(g, b, i)
                        if not (isinstance(i, int) and g < 3):
                            read(g - 3, (b - 3) % AHEAD)

                moments(0, 0, 0)
                dve.wait_ge(consts_in, 16 * N_CONSTS)
                quads(dve, quad)
                for b in range(1, AHEAD):
                    read(GROUPS - AHEAD + b, b)

            @block.gpsimd
            def _(pool):
                pool.wait_ge(consts_in, 16 * N_CONSTS)

                def quad(i):
                    for b in range(AHEAD):
                        g = AHEAD * i + b
                        pool.wait_ge(a_veps, g + 1)
                        after(pool, a_norm, g - 1)
                        nc.gpsimd.tensor_tensor(rstd[b % 2][:, :], veps[:, :], k("minushalf")[:, 0:GROUP], ALU.pow).then_inc(a_rstd, 1)

                quads(pool, quad)

            @block.scalar
            def _(act):
                def store(g, b, n):
                    h = b % 2
                    act.wait_ge(a_turned, g + 1)
                    after(act, a_stored[h], 16 * n)
                    after(act, a_small, g - 1)
                    nc.scalar.activation(a_xT[h], a_T[h][:, :, :], ACT.Copy).then_inc(a_evac, 1)
                    act.wait_ge(a_evac, g + 1)
                    act.dma_start(xnT_d[:, :, bass.ds(g * GT, GT)], a_xT[h]).then_inc(a_stored[h], 16)

                def copy_small(g, b):
                    h = b % 2
                    act.wait_ge(a_small, g + 1)
                    after(act, a_small_turned, g - 1)
                    nc.scalar.activation(a_sT[h][0:2 * HEADS, :], a_S[h][0:2 * HEADS, :], ACT.Copy).then_inc(a_small_evac, 1)

                def quad(i):
                    for b in range(AHEAD):
                        g = AHEAD * i + b
                        store(g, b, 2 * i + b // 2)
                        if not (isinstance(i, int) and g == 0):
                            copy_small(g - 1, (b - 1) % AHEAD)

                quads(act, quad)
                copy_small(GROUPS - 1, AHEAD - 1)
                for b in range(2):
                    act.wait_ge(a_stored[b], 16 * (GROUPS // 2))

            @block.tensor
            def _(pe):
                pe.wait_ge(consts_in, 16 * N_CONSTS)

                def turn(g, b):
                    h = b % 2
                    pe.wait_ge(a_norm, g + 1)
                    after(pe, a_evac, g - 1)
                    for kt in range(KT):
                        for t in range(GROUP):
                            last = nc.tensor.transpose(a_T[h][:, kt, t * P:(t + 1) * P], a_xn[b][:, t, kt * P:(kt + 1) * P], ident)
                    last.then_inc(a_turned, 1)

                def small(g, b):
                    h = b % 2
                    pe.wait_ge(a_evac, g + 1)
                    after(pe, a_small_evac, g - 1)
                    for kt in range(KT):
                        last = nc.tensor.matmul(a_S[h][0:2 * HEADS, :], wsm[:, kt, :], a_xT[h][:, kt, :], start=(kt == 0), stop=(kt == KT - 1))
                    last.then_inc(a_small, 1)

                def turn_small(g, b):
                    h = b % 2
                    pe.wait_ge(a_small_evac, g + 1)
                    after(pe, a_read, 2 * (g - 1))
                    pe.sem_inc(passed, 1)
                    for t in range(GROUP):
                        last = nc.tensor.transpose(a_small_T[h][:, t * 2 * HEADS:(t + 1) * 2 * HEADS], a_sT[h][0:2 * HEADS, t * P:(t + 1) * P],
                                                   ident[0:2 * HEADS, 0:2 * HEADS])
                    last.then_inc(a_small_turned, 1)

                def quad(i):
                    for b in range(AHEAD):
                        g = AHEAD * i + b
                        turn(g, b)
                        if not (isinstance(i, int) and g == 0):
                            small(g - 1, (b - 1) % AHEAD)
                        if not (isinstance(i, int) and g < 2):
                            turn_small(g - 2, (b - 2) % AHEAD)

                quads(pe, quad)
                small(GROUPS - 1, AHEAD - 1)
                turn_small(GROUPS - 2, AHEAD - 2)
                turn_small(GROUPS - 1, AHEAD - 1)

        r_tokens.again(), r_route.again(), r_expw.again()
        logits = r_route.take(TILES, EXPERTS)
        f1, f2, f3, f4, f5, onehot = (r_route.take(TILES, EXPERTS) for _ in range(6))
        incl = r_route.take(EXPERTS, TILES)
        dtT = r_route.take(4, P)
        t64 = [r_route.take(TILES) for _ in range(4)]
        e8 = [r_route.take(EXPERTS) for _ in range(6)]
        ge = r_route.take(SLOT_TILES, EXPERTS)
        ends = r_route.take(SLOT_TILES)
        most = r_route.take(EXPERTS)
        lam_flat = r_tokens.take(2 * HEADS * NBLK)
        lam_rows = lam_flat.rearrange("p (n h k) -> p n h k", n=2, h=HEADS)
        e8i = sb("e8i", [P, EXPERTS], I32)
        ids = r_tokens.take(P + TILES + 1)
        row_id, tile_id, part_id = ids[:, 0:P], ids[:, P:P + TILES], ids[:, P + TILES:]
        row_hot = r_tokens.take(TILES * P // 2).bitcast(BF16).rearrange("p (t r) -> p t r", t=TILES)
        tile_hot = r_tokens.take(TILES, SLOT_TILES)
        id_hot = r_tokens.take(TILES * SLOT_TILES).bitcast(BF16).rearrange("p (n t s) -> p t n s", n=2, t=TILES)
        token_of = sb("token_of", [P, SLOT_TILES], I32)
        PARTS = 4
        PT = TILES // PARTS
        rv, rp, r_ew, ids_in = (sem(n) for n in ("rv", "rp", "r_ew", "ids_in"))
        row_ready, tile_ready, id_ready, part_ready, order_ready = (sem(n) for n in ("row_ready", "tile_ready", "id_ready", "part_ready", "order_ready"))
        w8 = r_expw.take(KT * EXPERTS, D_MODEL)
        b8 = r_expw.take(EXPERTS, D_MODEL)

        def over(v, *shape):
            return v.broadcast_to([P, *shape])

        with nc.Block() as block:
            @block.sync
            def _(sp):
                sp.dma_start(ids, ids_d).then_inc(ids_in, 16)
                sp.dma_start(w8, w_exp).then_inc(r_ew, 16)
                sp.dma_start(b8, b_exp.rearrange("e d -> (e d)")[None, :].broadcast_to([P, EXPERTS * D_MODEL]).rearrange("p (e d) -> p e d", e=EXPERTS)).then_inc(r_ew, 16)
                sp.dma_start(lam_flat, rows[0:1, 2 * HEADS:].broadcast_to([P, 2 * HEADS * NBLK])).then_inc(r_ew, 16)
                sp.wait_ge(ids_in, 16)
                sp.wait_ge(r_ew, 48)

            @block.vector
            def _(dve):
                done = [0]

                def step(ins):
                    done[0] += 1
                    ins.then_inc(rv, 1)
                    dve.wait_ge(rv, done[0])

                step(nc.vector.tensor_reduce(t64[0], logits, AX_X, ALU.max))
                step(nc.vector.tensor_tensor(f1, logits, over(t64[0][:, :, None], TILES, EXPERTS), ALU.is_equal))
                step(nc.vector.tensor_tensor(f1, f1, over(k("first")[:, None, :], TILES, EXPERTS), ALU.mult))
                step(nc.vector.tensor_reduce(t64[2], f1, AX_X, ALU.max))
                step(nc.vector.tensor_tensor(onehot, f1, over(t64[2][:, :, None], TILES, EXPERTS), ALU.is_equal))
                assert done[0] == 5
                dve.wait_ge(rp, 2)
                step(nc.vector.tensor_copy(f2.rearrange("p t e -> p (t e)"), bank(3)))
                by_expert = bank(2).rearrange("p (t e) -> p e t", t=TILES)
                step(nc.vector.tensor_copy(f3.rearrange("p a b -> p (a b)").rearrange("p (e t) -> p e t", e=EXPERTS), by_expert))
                counts = f3.rearrange("p a b -> p (a b)")
                step(nc.vector.tensor_tensor_scan(incl.rearrange("p e t -> p (e t)"), k("tilestart"), counts, 0.0, ALU.mult, ALU.add))
                step(nc.vector.tensor_scalar(e8[0], incl[:, :, TILES - 1], float(P - 1), None, ALU.add))
                step(nc.vector.tensor_copy(e8i[:, :], e8[0]))
                step(nc.vector.tensor_scalar(e8i[:, :], e8i[:, :], int(math.log2(P)), None, ALU.logical_shift_right))
                step(nc.vector.tensor_copy(e8[1], e8i[:, :]))
                step(nc.vector.tensor_tensor_scan(e8[2], k("ones")[:, 0:EXPERTS], e8[1], 0.0, ALU.mult, ALU.add))
                step(nc.vector.tensor_tensor(e8[3], e8[2], e8[1], ALU.subtract))
                step(nc.vector.tensor_scalar(e8[3], e8[3], float(P), None, ALU.mult))
                step(nc.vector.tensor_tensor(f4.rearrange("p a b -> p (a b)"), incl.rearrange("p e t -> p (e t)"), counts, ALU.subtract))
                earlier = f4.rearrange("p a b -> p (a b)").rearrange("p (e t) -> p t e", e=EXPERTS)
                step(nc.vector.tensor_tensor(f2, f2, earlier, ALU.add))
                step(nc.vector.tensor_tensor(f2, f2, over(e8[3][:, None, :], TILES, EXPERTS), ALU.add))
                step(nc.vector.tensor_tensor(f2, f2, onehot, ALU.mult))
                step(nc.vector.tensor_reduce(t64[3], f2, AX_X, ALU.add))
                step(nc.vector.tensor_copy(slot_of[:, :], t64[3]))
                step(nc.vector.tensor_scalar(tile_expert[:, :][:, 0:TILES], slot_of[:, :], int(math.log2(P)), None, ALU.logical_shift_right))
                step(nc.vector.tensor_copy(t64[1], tile_expert[:, :][:, 0:TILES]))
                step(nc.vector.scalar_tensor_tensor(t64[2], t64[1], float(-P), t64[3], ALU.mult, ALU.add))
                assert done[0] == 24
                dve.wait_ge(ids_in, 16)
                for n in range(PARTS):
                    part = slice(n * PT, (n + 1) * PT)
                    nc.vector.tensor_tensor(tile_hot[:, part, :], over(k("slot")[:, None, :], PT, SLOT_TILES), over(t64[1][:, part, None], PT, SLOT_TILES), ALU.is_equal).then_inc(tile_ready, 1)
                    nc.vector.tensor_tensor(row_hot[:, part, :], over(row_id[:, None, :], PT, P), over(t64[2][:, part, None], PT, P), ALU.is_equal).then_inc(row_ready, 1)
                step(nc.vector.tensor_tensor(ge, over(k("slot")[:, :, None], SLOT_TILES, EXPERTS), over(e8[2][:, None, :], SLOT_TILES, EXPERTS), ALU.is_ge))
                step(nc.vector.tensor_reduce(ends, ge, AX_X, ALU.add))
                step(nc.vector.tensor_scalar(ends, ends, float(EXPERTS - 1), None, ALU.min))
                step(nc.vector.tensor_copy(tile_expert[:, :], ends))
                dve.wait_ge(order_ready, 1)
                step(nc.vector.tensor_copy(ends, bank(6)[:, 0:SLOT_TILES]))
                step(nc.vector.scalar_tensor_tensor(ends, ends, float(P), bank(6)[:, SLOT_TILES:2 * SLOT_TILES], ALU.mult, ALU.add))
                step(nc.vector.tensor_copy(token_of[:, :], ends))

            @block.scalar
            def _(act):
                act.wait_ge(ids_in, 16)
                for n in range(PARTS):
                    part = slice(n * PT, (n + 1) * PT)
                    act.wait_ge(tile_ready, n + 1)
                    nc.scalar.activation(id_hot[:, part, 1, :], tile_hot[:, part, :], ACT.Identity, scale=part_id).then_inc(part_ready, 1)


            @block.tensor
            def _(pe):
                pe.wait_ge(rv, 5)
                flat = onehot.rearrange("p t e -> p (t e)")
                nc.tensor.matmul(bank(3), k("before"), flat, start=True, stop=True).then_inc(rp, 1)
                nc.tensor.matmul(bank(2), k("ones"), flat, start=True, stop=True).then_inc(rp, 1)
                for n in range(PARTS):
                    pe.wait_ge(row_ready, n + 1)
                    pe.wait_ge(id_ready, n + 1)
                    pe.wait_ge(part_ready, n + 1)
                    for t in range(n * PT, (n + 1) * PT):
                        last = nc.tensor.matmul(bank(6)[:, 0:2 * SLOT_TILES], row_hot[:, t, :], id_hot[:, t, :, :], start=(t == 0), stop=(t == TILES - 1))
                last.then_inc(order_ready, 1)

            @block.gpsimd
            def _(pool):
                pool.wait_ge(ids_in, 16)
                for n in range(PARTS):
                    part = slice(n * PT, (n + 1) * PT)
                    pool.wait_ge(tile_ready, n + 1)
                    nc.gpsimd.tensor_tensor(id_hot[:, part, 0, :], tile_hot[:, part, :], over(tile_id[:, part, None], PT, SLOT_TILES), ALU.mult).then_inc(id_ready, 1)

        r_tiles.again()
        e_in = [r_tiles.take(GROUP, D_MODEL) for _ in range(2)]
        e_xT = [r_tiles.take(KT, GROUP * P) for _ in range(2)]
        e_out = [r_tiles.take(GROUP, D_MODEL) for _ in range(2)]
        e_loaded, e_turned, e_evac, e_mm, e_added, e_stored = ([sem(f"{n}{b}") for b in range(2)] for n in (
            "e_loaded", "e_turned", "e_evac", "e_mm", "e_added", "e_stored"))
        e_listed = [sem(f"e_listed{b}") for b in range(2)]
        e_tokens = [sb(f"e_tokens{b}", [P, GROUP], I32) for b in range(2)]
        DT_STEPS = 11
        E_HALF = SLOT_TILES // GROUP // 2
        dv, da, dp, dt_stored = (sem(n) for n in ("dv", "da", "dp", "dt_stored"))
        dt_flat = dt_tok[:, :, :].rearrange("p t h -> p (t h)")
        e_T = [pst[0], pst[1]]
        e_Y = [pst[2], pst[3]]

        with nc.Block() as block:
            @block.sync
            def _(sp):
                sp.wait_ge(da, 4)
                for n in range(4):
                    sp.dma_start(dtT_d[:, n * 16 * P:(n + 1) * 16 * P].rearrange("h (t s) -> t h s", s=P),
                                 dtT[:, n, :]).then_inc(dt_stored, 16)
                sp.wait_ge(dt_stored, 64)

            @block.gpsimd
            def _(pool):
                with pool.Fori(0, E_HALF) as i:
                    for b in range(2):
                        pool.wait_ge(e_turned[b], i)
                        pool.sem_inc(passed, 1)
                        nc.gpsimd.tensor_copy(e_tokens[b][:, :], token_of[:, bass.ds((2 * i + b) * GROUP, GROUP)]).then_inc(e_listed[b], 1)
                        pool.wait_ge(e_listed[b], i + 1)
                        pool.sem_inc(passed, 1)
                        for t in range(GROUP):
                            pool.indirect_dma_start(e_in[b][:, t, :], None, xn_d, bass.IndirectOffsetOnAxis(ap=e_tokens[b][:, t:t + 1], axis=0)).then_inc(e_loaded[b], 16)

            @block.tensor
            def _(pe):
                def turn(i, b):
                    pe.wait_ge(e_loaded[b], 16 * GROUP * (i + 1))
                    pe.wait_ge(e_evac[b], i)
                    for t in range(GROUP):
                        for kt in range(KT):
                            last = nc.tensor.transpose(e_T[b][:, kt, t * P:(t + 1) * P], e_in[b][:, t, kt * P:(kt + 1) * P], ident)
                    last.then_inc(e_turned[b], 1)

                def products(i, b):
                    pe.wait_ge(e_evac[b], i + 1)
                    pe.wait_ge(e_added[b], GROUP * i)
                    for t in range(GROUP):
                        e = pe.value_load(tile_expert[0:1, bass.ds((2 * i + b) * GROUP + t, 1)], min_val=0, max_val=EXPERTS - 1)
                        for kt in range(KT):
                            last = nc.tensor.matmul(e_Y[b][:, t // 2, (t % 2) * D_MODEL:(t % 2 + 1) * D_MODEL],
                                                    e_xT[b][:, kt, t * P:(t + 1) * P],
                                                    w8[:, bass.ds(e + kt * EXPERTS, 1), :].rearrange("p o d -> p (o d)"),
                                                    start=(kt == 0), stop=(kt == KT - 1))
                    last.then_inc(e_mm[b], 1)

                turn(0, 0)
                with pe.Fori(0, E_HALF - 1) as i:
                    turn(i, 1)
                    products(i, 0)
                    turn(i + 1, 0)
                    products(i, 1)
                turn(E_HALF - 1, 1)
                products(E_HALF - 1, 0)
                pe.wait_ge(dv, DT_STEPS)
                for n in range(4):
                    last = nc.tensor.transpose(bank(0)[:, n * P:(n + 1) * P], dt_flat[:, n * P:(n + 1) * P], ident)
                last.then_inc(dp, 1)
                nc.tensor.matmul(bank(1), k("ones"), dt_flat, start=True, stop=True).then_inc(dp, 1)
                products(E_HALF - 1, 1)

            @block.scalar
            def _(act):
                def evacuate(i, b):
                    act.wait_ge(e_turned[b], i + 1)
                    act.wait_ge(e_mm[b], i)
                    nc.scalar.activation(e_xT[b], e_T[b][:, :, :], ACT.Copy).then_inc(e_evac[b], 1)

                def store(i, b):
                    act.wait_ge(e_added[b], GROUP * (i + 1))
                    act.dma_start(expert_d[bass.ds((2 * i + b) * GT, GT), :].rearrange("(t p) d -> p t d", p=P), e_out[b]).then_inc(e_stored[b], 16)

                act.wait_ge(dv, 2)
                nc.scalar.activation(f3, f1, ACT.Exp, scale=-1.0).then_inc(da, 1)
                nc.scalar.activation(onehot, f2, ACT.Exp).then_inc(da, 1)
                act.wait_ge(da, 2)
                act.wait_ge(dv, 3)
                nc.scalar.activation(f2, f4, ACT.Ln).then_inc(da, 1)
                evacuate(0, 0)
                evacuate(0, 1)
                with act.Fori(0, E_HALF - 1) as i:
                    for b in range(2):
                        evacuate(i + 1, b)
                        store(i, b)
                store(E_HALF - 1, 0)
                act.wait_ge(dp, 1)
                nc.scalar.activation(dtT.rearrange("p n s -> p (n s)"), bank(0), ACT.Copy).then_inc(da, 1)
                store(E_HALF - 1, 1)
                for b in range(2):
                    act.wait_ge(e_stored[b], 16 * E_HALF)

            @block.vector
            def _(dve):
                done = [0]

                def step(ins):
                    done[0] += 1
                    ins.then_inc(dv, 1)
                    dve.wait_ge(dv, done[0])

                u = dt_tok[:, :, :]
                step(nc.vector.scalar_tensor_tensor(f1, u, -1.0, u, ALU.mult, ALU.max))
                step(nc.vector.tensor_tensor(f2, logits, over(t64[0][:, :, None], TILES, EXPERTS), ALU.subtract))
                dve.wait_ge(da, 1)
                step(nc.vector.tensor_scalar(f4, f3, 1.0, None, ALU.add))
                step(nc.vector.tensor_scalar(f5, f4, -1.0, 2.0 ** -24, ALU.add, ALU.max))
                step(nc.vector.reciprocal(f5, f5))
                step(nc.vector.tensor_tensor(f5, f5, f3, ALU.mult))
                step(nc.vector.tensor_scalar(f1, f4, 1.0, None, ALU.is_equal))
                step(nc.vector.tensor_tensor(f1, f1, f3, ALU.mult))
                dve.wait_ge(da, 3)
                step(nc.vector.tensor_tensor(f4, f2, f5, ALU.mult))
                step(nc.vector.tensor_tensor(f4, f4, f1, ALU.max))
                step(nc.vector.scalar_tensor_tensor(u, u, 0.0, f4, ALU.max, ALU.add))
                assert done[0] == DT_STEPS
                step(nc.vector.tensor_reduce(t64[1], onehot, AX_X, ALU.add))
                step(nc.vector.reciprocal(gate[:, :], t64[1]))
                nc.vector.tensor_scalar(wl2[:, :], wl2[:, :], 1.0 / TWO_PI, None, ALU.mult)
                for q in range(PAIRS):
                    nc.vector.tensor_scalar(wout[:, q, :], wout[:, q, :], c("norm_w", q), None, ALU.mult)
                for n in range(2):
                    step(nc.vector.scalar_tensor_tensor(lam_rows[:, n], lam_rows[:, n], -1.0, lam_rows[:, n], ALU.mult, ALU.max))
                step(nc.vector.scalar_tensor_tensor(lam_rows[:, 0], lam_rows[:, 1], (math.pi / 2) ** 2, lam_rows[:, 0], ALU.mult, ALU.add))
                step(nc.vector.tensor_reduce(most, lam_rows[:, 0], AX_X, ALU.max))

                with dve.Fori(0, E_HALF) as i:
                    for b in range(2):
                        dve.wait_ge(e_mm[b], i + 1)
                        dve.wait_ge(e_stored[b], 16 * i)
                        for t in range(GROUP):
                            e = dve.value_load(tile_expert[0:1, bass.ds((2 * i + b) * GROUP + t, 1)], min_val=0, max_val=EXPERTS - 1)
                            nc.vector.tensor_tensor(e_out[b][:, t, :], e_Y[b][:, t // 2, (t % 2) * D_MODEL:(t % 2 + 1) * D_MODEL],
                                                    b8[:, bass.ds(e, 1), :].rearrange("p o d -> p (o d)"), ALU.add).then_inc(e_added[b], 1)

                dve.wait_ge(dp, 2)
                step(nc.vector.tensor_tensor(f1, bank(1).rearrange("p (t h) -> p t h", t=TILES), over(most[:, None, :], TILES, HEADS), ALU.mult))
                step(nc.vector.tensor_reduce(t64[1][:, 0:1], f1.rearrange("p t h -> p (t h)"), AX_X, ALU.max))
                step(nc.vector.tensor_scalar(t64[1][:, 0:1], t64[1][:, 0:1], MAX_DECAY, None, ALU.is_gt))
                step(nc.vector.tensor_copy(halve[:, :], t64[1][:, 0:1]))

        r_tokens.again(), r_route.again(), r_tiles.again(), r_expw.again()
        theta, lam, decay, phase, frac, wave, quad, eneg = (r_tokens.take(PAIRS, MT) for _ in range(8))
        epos = sb("epos", [P, PAIRS, MT])[:, :, :]
        quad_grow = sb("quad_grow", [P, PAIRS, MT])[:, :, :]
        rep = r_expw.take(6, MT)
        c_in = [r_tokens.take(PAIRS, MT) for _ in range(2)]
        c_own = [r_tokens.take(PAIRS, MT) for _ in range(2)]
        grow = [r_tokens.take(PAIRS, MT) for _ in range(2)]
        b_up = [r_tokens.take(PAIRS, MT) for _ in range(2)]
        z_gate = [r_route.take(PAIRS, MT) for _ in range(2)]
        x_skip = [r_route.take(PAIRS, MT) for _ in range(2)]
        x_dt = [r_route.take(TPM, D_INNER) for _ in range(2)]
        end_dec = sb("end_dec", [P, CPM, PAIRS])
        head_dec = [sb(f"head_dec{b}", [P, CPM, PAIRS * 2]) for b in range(2)]
        x_pre = [r_expw.take(XBC_T, MT + D_CONV - 1) for _ in range(2)]
        conv = r_expw.take(XBC_T, MT)
        xbc = r_mixer.take(XBC_T, MT)
        xn_in = [r_mixer.take(KT, MT) for _ in range(2)]
        dt_in = [r_mixer.take(PAIRS, MT) for _ in range(2)]
        zero_dec = sb("zero_dec", [P, PAIRS * 2])
        cb_part = sb("cb_part", [P, 2, MT])[:, :, :]
        hidden = sb("hidden", [LORA + 1, MT])
        b_tok = [r_tiles.take(PAIRS, P) for _ in range(2)]
        att = [r_tiles.take(HEADS, P) for _ in range(2)]
        g = [r_tiles.take(PAIRS, P) for _ in range(2)]
        gsq = r_tiles.take(PAIRS, P)
        state_in = [sb(f"state_in{b}", [P, PAIRS, P]) for b in range(CPM)]
        state = sb("state", [P, PAIRS, HEADDIM])
        level_signs, level_masks = r_mixer.take(LEVELS, P), r_tiles.take(LEVELS + 1, P)
        part_att = conv[:, 0:2, :].rearrange("p n (a t) -> p (n a) t", a=2)
        level_e, level_b, level_c = ([v[1][:, :, n * P:(n + 1) * P] for n in range(2)] for v in (b_up, c_in, c_own))
        x_tile = [sb(f"x_tile{b}", [P, D_MODEL]) for b in range(2)]
        e_tile = [sb(f"e_tile{b}", [P, D_MODEL]) for b in range(2)]
        o_tile = [sb(f"o_tile{b}", [P, D_MODEL]) for b in range(2)]
        e_index = [sb(f"e_index{b}", [P, 1], I32) for b in range(2)]
        ms = [sb(f"ms{b}", [P, 1]) for b in range(2)]
        rms = [sb(f"rms{b}", [P, 1]) for b in range(2)]

        bank_a, bank_b, bank_t, bank_u = bank(0), bank(1), bank(2), bank(3)
        bank_s, bank_y, bank_o = pst[2], bank(6), bank(7)

        made = {n: sem(n) for n in (
            "xproj", "zproj", "thproj",
            "xturned",
            "bturned", "scored", "yout", "oproj",
            "upd",
            "xevac", "zevac",
            "lamsq", "lamd",
            "silu", "xd", "shifted", "rounded",
            "trig", "negd", "expd",
            "bevac", "squared",
            "fabs",
            "halo", "convd",
            "clipped", "rsum", "psum", "fracd",
            "xdt",
            "grown", "bup", "wavedec", "cwave", "cin", "dwave", "cown",
            "masked", "gated", "meansq", "xplus", "final",
            "stated",
            "angle", "lamdt", "headdec",
            "cb",
            "quadgrow", "bquad", "quaddec", "cquad", "dquad",
            "rmsd", "eidx",
            "statein",
            "repd",
            "tail",
            "apart", "signed", "lcdec", "lmasked",
            "lsum",
            "lexpd",
            "lbdec",
            "lscored",
        )}
        s = made
        xn_loaded, dt_loaded = [sem(f"xn_loaded{b}") for b in range(2)], [sem(f"dt_loaded{b}") for b in range(2)]
        x_loaded, e_loaded2, o_stored = ([sem(f"{n}{b}") for b in range(2)] for n in ("x_loaded", "e_gathered", "o_stored"))
        m_ready, m_zero, table_in, bc_out = sem("m_ready"), sem("m_zero"), sem("table_in"), sem("bc_out")

        REPS = 4

        def expand(v, *shape):
            return v.broadcast_to([v.shape[0], *shape])



        def two_ago(m, halved, per):
            if halved:
                return per * m
            return per * (m - 1) if not (isinstance(m, int) and m == 0) else 0

        def updates(halved):
            return CPT if halved else 1

        def state_slot(j, ch, c, halved):
            return ch * CPT + c if halved else (TPM * j + ch) % CPM

        def reference(v, ch, level):
            half = CH >> (level + 1)
            blocks = v[:, :, ch * P:(ch + 1) * P].rearrange("p q (n w) -> p q n w", w=2 * half)
            return [blocks[:, q] for q in range(PAIRS)], [blocks[:, q, :, half - 1:half].broadcast_to([P, P // (2 * half), 2 * half]) for q in range(PAIRS)]

        def sync_mixer(sp, halved):
            def load(i, j, first=False):
                m, b = MPS * i + j, j % 2
                if not first:
                    sp.wait_ge(s["zproj"], two_ago(m, halved, 2))
                    sp.wait_ge(s["lamdt"], two_ago(m, halved, 1))
                    sp.wait_ge(s["angle"], two_ago(m, halved, 1))
                    sp.sem_inc(passed, 1)
                sp.dma_start(xn_in[b], xnT_d[:, :, bass.ds(m * MT, MT)]).then_inc(xn_loaded[b], 16)
                for e in range(2):
                    src = dtT_d.rearrange("(q e) t -> e q t", e=2)[e:e + 1, :, bass.ds(m * MT, MT)]
                    sp.dma_start(dt_in[b][e * HEADDIM:(e + 1) * HEADDIM, :, :],
                                 src.broadcast_to([HEADDIM, PAIRS, MT])).then_inc(dt_loaded[b], 16)

            def replicate(i, j):
                m = MPS * i + j
                sp.wait_ge(s["cown"], m)
                sp.sem_inc(passed, 1)
                sp.wait_ge(s["silu"], m + 1)
                sp.dma_start(bc_d, xbc[:, XBC_T - 1, :]).then_inc(bc_out, 16)
                sp.wait_ge(bc_out, 16 * m + 16)
                for at in range(0, P, NBLK):
                    sp.dma_start(rep[at:at + NBLK, 0:4, :], bc_d.rearrange("(n k) t -> k n t", n=4)).then_inc(s["repd"], 16)

            def load_x(i, j, ch):
                t = (MPS * i + j) * TPM + ch
                n = MPS * i + j
                sp.wait_ge(s["xplus"], TPM * n)
                sp.dma_start(x_tile[ch][:, :], x[bass.ds(t * P, P), :]).then_inc(x_loaded[ch], 16)

            def store(i, j, ch):
                t = (MPS * i + j) * TPM + ch
                sp.wait_ge(s["final"], t + 1)
                sp.dma_start(out[bass.ds(t * P, P), :], o_tile[ch][:, :]).then_inc(o_stored[ch], 16)

            def body(i, js, last):
                for j in js:
                    left = MPS - 1 - j if last else MPS
                    load_x(i, j, 0)
                    load_x(i, j, 1)
                    if left >= 3:
                        load(i, j + 3)
                    if left >= 2:
                        replicate(i, j + 2)
                    store(i, j, 0)
                    store(i, j, 1)

            if halved:
                sp.dma_start(level_signs, halvings[:, 0:LEVELS, :]).then_inc(table_in, 16)
                sp.dma_start(level_masks, halvings[:, LEVELS:, :]).then_inc(table_in, 16)
                sp.wait_ge(table_in, 32)
                with sp.Fori(0, BATCH) as i:
                    for j in range(MPS):
                        load(i, j)
                        replicate(i, j)
                        for ch in range(TPM):
                            load_x(i, j, ch)
                        for ch in range(TPM):
                            store(i, j, ch)
            else:
                load(0, 0, True)
                load(0, 1, True)
                replicate(0, 0)
                load(0, 2)
                replicate(0, 1)
                with sp.Fori(0, BATCH - 1) as i:
                    body(i, range(MPS), False)
                body(BATCH - 1, range(MPS), True)
            for ch in range(TPM):
                sp.wait_ge(o_stored[ch], 16 * MACROS)

        def tensor_mixer(pe, halved):

            def parity(j):
                return 0 if halved else j % 2

            def project(dst, n, b):
                for kt in range(KT):
                    last = nc.tensor.matmul(dst, win[:, kt, n * P:(n + 1) * P], xn_in[b][:, kt, :], start=(kt == 0), stop=(kt == KT - 1))
                return last

            def front_x(i, j):
                m, n, b = MPS * i + j, 2 * i + j // 2, j % 2
                pe.wait_ge(xn_loaded[b], 16 * n + 16)
                if not (isinstance(m, int) and m < 2):
                    pe.wait_ge(s["zevac"], two_ago(m, halved, 2))
                elif m == 1:
                    pe.wait_ge(s["zevac"], 2)
                project(bank_a[:, 0:MT], 0, b)
                project(bank_a[:, MT:], 1, b).then_inc(s["xproj"], 1)
                project(bank_b[:, 0:MT], 2, b)
                project(bank_b[:, MT:], 3, b).then_inc(s["xproj"], 1)
                pe.wait_ge(s["xevac"], 3 * m + 1)
                project(bank_a[:, 0:MT], 4, b)
                for kt in range(KT):
                    last = nc.tensor.matmul(bank_a[0:LORA, MT:], wl1[:, kt, :], xn_in[b][:, kt, :], start=(kt == 0), stop=(kt == KT - 1))
                last.then_inc(s["xproj"], 1)

            def front_theta(i, j):
                m = MPS * i + j
                pe.wait_ge(s["xevac"], 3 * m + 3)
                for q in range(PAIRS):
                    dst = (bank_b, bank_a)[q // 2][:, (q % 2) * MT:(q % 2 + 1) * MT]
                    last = nc.tensor.matmul(dst, wl2[:, q * P:(q + 1) * P], hidden[:, :], start=True, stop=True)
                    if q % 2:
                        last.then_inc(s["thproj"], 1)

            def front_z(i, j, ahead=0):
                m, b = MPS * i + j, j % 2
                for h, dst in enumerate((bank_b, bank_a)):
                    pe.wait_ge(s["clipped"], 2 * (m + ahead) + h + 1)
                    project(dst[:, 0:MT], XBC_T + 2 * h, b)
                    project(dst[:, MT:], XBC_T + 2 * h + 1, b).then_inc(s["zproj"], 1)

            def front_turn(i, j):
                m = MPS * i + j
                pe.wait_ge(s["silu"], m + 1)
                pe.wait_ge(s["bevac"], TPM * m)
                for ch in range(TPM):
                    pe.wait_ge(s["xdt"], TPM * m + ch)
                    for q in range(PAIRS):
                        last = nc.tensor.transpose(bank_t[:, q * P:(q + 1) * P], xbc[:, q, ch * P:(ch + 1) * P], ident)
                    last.then_inc(s["xturned"], 1)

            def back_turn(i, j, ch):
                m, b, t = MPS * i + j, parity(j), (MPS * i + j) * TPM + ch
                pe.wait_ge(s["bup"], 4 * (m + 1))
                pe.wait_ge(s["xdt"], TPM * (m + 1))
                pe.wait_ge(s["bevac"], t)
                for q in range(PAIRS):
                    last = nc.tensor.transpose(bank_t[:, q * P:(q + 1) * P], b_up[b][:, q, ch * P:(ch + 1) * P], ident)
                last.then_inc(s["bturned"], 1)

            def back_scores(i, j, ch):
                m, b, t = MPS * i + j, parity(j), (MPS * i + j) * TPM + ch
                here = slice(ch * P, (ch + 1) * P)
                pe.wait_ge(s["cown"], m + 1)
                if halved:
                    for level in range(LEVELS + 1):
                        ln, lb = LEVELS * t + level, level % 2
                        pe.wait_ge(s["lmasked"], 2 * ((LEVELS + 1) * t + level))
                        if level < LEVELS:
                            pe.wait_ge(s["lbdec"], ln + 1)
                            pe.wait_ge(s["lcdec"], ln + 1)
                        for e in range(2):
                            part = slice(e * HEADDIM, (e + 1) * HEADDIM)
                            for q in range(PAIRS):
                                lhs, rhs = (level_b[lb][part, q, :], level_c[lb][part, q, :]) if level < LEVELS else (wave[part, q, here], c_own[b][part, q, here])
                                last = nc.tensor.matmul(bank_s[:, e, q * P:(q + 1) * P], lhs, rhs, start=True, stop=True)
                            last.then_inc(s["lscored"], 1)
                    return
                pe.wait_ge(s["grown"], m + 1)
                pe.wait_ge(s["masked"], 2 * t)
                pe.wait_ge(s["bup"], 4 * (m + 1))
                pe.wait_ge(s["cin"], m + 1)
                for q in range(PAIRS):
                    for e in range(2):
                        part = slice(e * HEADDIM, (e + 1) * HEADDIM)
                        nc.tensor.matmul(bank_s[:, e, q * P:(q + 1) * P], grow[b][part, q, here], c_own[b][part, q, here], start=True, stop=True)
                first, second = slice(ch * P, ch * P + CH), slice(ch * P + CH, (ch + 1) * P)
                for q in range(PAIRS):
                    for e in range(2):
                        part = slice(e * HEADDIM, (e + 1) * HEADDIM)
                        last = nc.tensor.matmul(bank_s[0:CH, e, q * P + CH:(q + 1) * P], b_up[b][part, q, first], c_in[b][part, q, second], start=True, stop=True)
                        if q == PAIRS - 1:
                            last.then_inc(s["scored"], 1)

            def back_update(i, j, ch, c):
                b, t = parity(j), (MPS * i + j) * TPM + ch
                u, rows_c = updates(halved) * t + c, slice(c * CH, (c + 1) * CH) if halved else slice(0, P)
                pe.wait_ge(s["bevac"], t + 1)
                pe.wait_ge(s["stated"], 2 * u)
                for q in range(PAIRS):
                    last = nc.tensor.matmul(bank_u[:, q * P:(q + 1) * P], b_tok[ch][rows_c, q, :], x_dt[j % 2][rows_c, ch, q * P:(q + 1) * P], start=True, stop=True)
                last.then_inc(s["upd"], 1)

            def back_y(i, j, ch):
                b, t = parity(j), (MPS * i + j) * TPM + ch
                pe.wait_ge(s["masked"], 2 * t + 2)
                pe.wait_ge(s["cin"], MPS * i + j + 1)
                pe.wait_ge(s["gated"], t)
                pe.wait_ge(s["statein"], updates(halved) * (t + 1) - 1)
                pe.wait_ge(s["xd"], MPS * i + j + 1)
                for q in range(PAIRS):
                    dst = bank_y[:, q * P:(q + 1) * P]
                    for e in range(2):
                        nc.tensor.matmul(dst[e * HEADDIM:(e + 1) * HEADDIM, :], x_dt[j % 2][:, ch, q * P + e * HEADDIM:q * P + (e + 1) * HEADDIM],
                                         att[ch][:, e * PAIRS + q, :], start=True, stop=False, skip_group_check=True)
                    nc.tensor.matmul(dst, ident, x_skip[j % 2][:, q, ch * P:(ch + 1) * P], start=False, stop=False, skip_group_check=True)
                    for n in range(updates(halved)):
                        w = P // updates(halved)
                        last = nc.tensor.matmul(dst[:, n * w:(n + 1) * w], state_in[state_slot(j, ch, n, halved)][:, q, :],
                                                c_in[b][:, q, ch * P + n * w:ch * P + (n + 1) * w], start=False, stop=True, skip_group_check=True)
                last.then_inc(s["yout"], 1)

            def back_out(i, j, ch):
                t = (MPS * i + j) * TPM + ch
                pe.wait_ge(s["gated"], t + 1)
                pe.wait_ge(s["final"], t)
                for q in range(PAIRS):
                    nc.tensor.matmul(bank_o[:, 0:D_MODEL], g[ch][:, q, :], wout[:, q, :], start=(q == 0), stop=(q == PAIRS - 1))
                pe.wait_ge(s["squared"], t + 1)
                for q in range(PAIRS):
                    last = nc.tensor.matmul(bank_o[:, D_MODEL:D_MODEL + 1], gsq[:, q, :], k("ones")[:, 0:1], start=(q == 0), stop=(q == PAIRS - 1))
                last.then_inc(s["oproj"], 1)

            def body(i, js, last):
                for j in js:
                    left = MPS - 1 - j if last else MPS
                    back_turn(i, j, 0)
                    back_scores(i, j, 0)
                    back_update(i, j, 0, 0)
                    back_turn(i, j, 1)
                    if left >= 2:
                        front_theta(i, j + 2)
                    back_y(i, j, 0)
                    if left >= 1:
                        front_turn(i, j + 1)
                    back_scores(i, j, 1)
                    back_out(i, j, 0)
                    if left >= 1:
                        front_z(i, j + 1, min(left - 1, 1))
                    back_update(i, j, 1, 0)
                    back_y(i, j, 1)
                    if left >= 3:
                        front_x(i, j + 3)
                    back_out(i, j, 1)

            pe.wait_ge(m_ready, 2)
            if halved:
                with pe.Fori(0, BATCH) as i:
                    for j in range(MPS):
                        front_x(i, j)
                        front_theta(i, j)
                        front_z(i, j)
                        front_turn(i, j)
                        for ch in range(TPM):
                            back_turn(i, j, ch)
                            back_scores(i, j, ch)
                            for part in range(CPT):
                                back_update(i, j, ch, part)
                            back_y(i, j, ch)
                            back_out(i, j, ch)
            else:
                front_x(0, 0)
                front_theta(0, 0)
                front_z(0, 0)
                front_x(0, 1)
                front_theta(0, 1)
                front_turn(0, 0)
                pe.wait_ge(s["clipped"], 4)
                front_x(0, 2)
                with pe.Fori(0, BATCH - 1) as i:
                    body(i, range(MPS), False)
                body(BATCH - 1, range(MPS), True)

        def scalar_mixer(act, halved):

            def parity(j):
                return 0 if halved else j % 2

            def front_x(i, j):
                m, b = MPS * i + j, j % 2
                act.wait_ge(s["convd"], 15 * m)
                act.wait_ge(s["halo"], m)
                act.wait_ge(s["silu"], m)
                for n, (dst, w) in enumerate(((bank_a, 2), (bank_b, 2), (bank_a, 1))):
                    act.wait_ge(s["xproj"], 3 * m + n + 1)
                    src = dst[:, 0:w * MT].rearrange("p (n t) -> p n t", n=w)
                    nc.scalar.activation(x_pre[b][:, 2 * n:2 * n + w, D_CONV - 1:], src, ACT.Copy)
                    for d in range(w):
                        ct = 2 * n + d
                        last = nc.scalar.activation(conv[:, ct, :], src[:, d, :], ACT.Identity, bias=c("conv_b", ct),
                                                    scale=c("conv_w", ct * D_CONV + D_CONV - 1))
                    if n == 2:
                        act.wait_ge(s["thproj"], 2 * m)
                        last = nc.scalar.activation(hidden[0:LORA, :], bank_a[0:LORA, MT:], ACT.Tanh)
                    last.then_inc(s["xevac"], 1)

            def front_z(i, j):
                m, b = MPS * i + j, j % 2
                act.wait_ge(s["gated"], two_ago(m, halved, TPM))
                for h, src in enumerate((bank_b, bank_a)):
                    act.wait_ge(s["zproj"], 2 * m + h + 1)
                    nc.scalar.activation(z_gate[b][:, 2 * h:2 * h + 2, :], src.rearrange("p (n t) -> p n t", n=2), ACT.Silu).then_inc(s["zevac"], 1)

            def front_lambda(i, j):
                m = MPS * i + j
                act.wait_ge(s["clipped"], 2 * m + 2)
                act.wait_ge(s["rsum"], 4 * m)
                if halved:
                    act.wait_ge(s["cquad"], m)
                nc.scalar.activation(lam, theta, ACT.Square, scale=TWO_PI).then_inc(s["lamsq"], 1)
                act.wait_ge(s["lamsq"], m + 1)
                for q in range(PAIRS):
                    last = nc.scalar.activation(lam[:, q, :], lam[:, q, :], ACT.Identity, bias=c("lb", q), scale=c("eta", q))
                last.then_inc(s["lamd"], 1)

            def front_silu(i, j):
                m = MPS * i + j
                act.wait_ge(s["convd"], 15 * (m + 1))
                act.wait_ge(s["xturned"], TPM * m)
                act.wait_ge(s["xd"], m)
                act.wait_ge(s["repd"], 16 * REPS * m)
                nc.scalar.activation(xbc, conv, ACT.Silu).then_inc(s["silu"], 1)

            def front_skip(i, j):
                m, b = MPS * i + j, j % 2
                act.wait_ge(s["silu"], m + 1)
                act.wait_ge(s["yout"], two_ago(m, halved, TPM))
                for q in range(PAIRS):
                    last = nc.scalar.activation(x_skip[b][:, q, :], xbc[:, q, :], ACT.Copy, scale=c("D", q))
                last.then_inc(s["xd"], 1)

            def front_round(i, j):
                m = MPS * i + j
                act.wait_ge(s["psum"], 4 * (m + 1))
                act.wait_ge(s["trig"], m)
                nc.scalar.activation(frac, phase, ACT.Copy, bias=ROUND).then_inc(s["shifted"], 1)
                act.wait_ge(s["shifted"], m + 1)
                nc.scalar.activation(frac, frac, ACT.Copy, bias=-ROUND).then_inc(s["rounded"], 1)

            def front_trig(i, j):
                m = MPS * i + j
                act.wait_ge(s["fracd"], m + 1)
                act.wait_ge(s["cown"], m)
                if halved:
                    act.wait_ge(s["lscored"], 2 * (LEVELS + 1) * TPM * m)
                nc.scalar.activation(quad, frac, ACT.Abs).then_inc(s["fabs"], 1)
                nc.scalar.activation(wave, frac, ACT.Sin, scale=TRIG)
                act.wait_ge(s["fabs"], m + 1)
                nc.scalar.activation(quad, quad, ACT.Sin, scale=-TRIG, bias=k("halfpi")).then_inc(s["trig"], 1)

            def front_exp(i, j):
                m = MPS * i + j
                act.wait_ge(s["rsum"], 4 * (m + 1))
                act.wait_ge(s["cown"], m)
                act.wait_ge(s["headdec"], m)
                if halved:
                    act.wait_ge(s["stated"], 2 * CPM * m)
                nc.scalar.activation(eneg, decay, ACT.Exp, scale=-1.0)
                n = updates(halved) * TPM
                nc.scalar.activation(end_dec[:, 0:n, :], decay.rearrange("p q (c t) -> p c q t", c=n)[:, :, :, MT // n - 1], ACT.Exp, scale=-1.0).then_inc(s["negd"], 1)
                if halved:
                    act.wait_ge(s["tail"], m + 1)
                    nc.scalar.activation(epos, epos, ACT.Exp).then_inc(s["expd"], 1)
                else:
                    nc.scalar.activation(epos, decay, ACT.Exp).then_inc(s["expd"], 1)

            def back_b(i, j, ch):
                t = (MPS * i + j) * TPM + ch
                act.wait_ge(s["bturned"], t + 1)
                act.wait_ge(s["upd"], updates(halved) * (t - 1 if ch else t))
                nc.scalar.activation(b_tok[ch].rearrange("p q s -> p (q s)"), bank_t, ACT.Copy).then_inc(s["bevac"], 1)

            def back_levels(i, j, ch):
                t = (MPS * i + j) * TPM + ch
                for level in range(LEVELS):
                    act.wait_ge(s["signed"], LEVELS * t + level + 1)
                    nc.scalar.activation(level_e[level % 2], level_e[level % 2], ACT.Exp).then_inc(s["lexpd"], 1)

            def back_square(i, j, ch):
                t = (MPS * i + j) * TPM + ch
                act.wait_ge(s["gated"], t + 1)
                act.wait_ge(s["oproj"], t)
                nc.scalar.activation(gsq, g[ch], ACT.Square).then_inc(s["squared"], 1)

            def body(i, js, last):
                for j in js:
                    left = MPS - 1 - j if last else MPS
                    back_b(i, j, 0)
                    if left >= 1:
                        front_round(i, j + 1)
                    back_b(i, j, 1)
                    if left >= 1:
                        front_trig(i, j + 1)
                        front_exp(i, j + 1)
                    back_square(i, j, 0)
                    if left >= 1:
                        front_skip(i, j + 1)
                    if left >= 2:
                        front_lambda(i, j + 2)
                    if left >= 1:
                        front_z(i, j + 1)
                    if left >= 2:
                        front_silu(i, j + 2)
                    back_square(i, j, 1)
                    if left >= 3:
                        front_x(i, j + 3)

            act.wait_ge(m_ready, 2)
            if halved:
                with act.Fori(0, BATCH) as i:
                    for j in range(MPS):
                        front_x(i, j)
                        front_lambda(i, j)
                        front_silu(i, j)
                        front_z(i, j)
                        front_round(i, j)
                        front_trig(i, j)
                        front_skip(i, j)
                        front_exp(i, j)
                        for ch in range(TPM):
                            back_b(i, j, ch)
                            back_levels(i, j, ch)
                            back_square(i, j, ch)
            else:
                front_x(0, 0)
                front_lambda(0, 0)
                front_z(0, 0)
                front_silu(0, 0)
                front_x(0, 1)
                front_round(0, 0)
                front_exp(0, 0)
                front_trig(0, 0)
                front_skip(0, 0)
                front_lambda(0, 1)
                front_silu(0, 1)
                front_x(0, 2)
                with act.Fori(0, BATCH - 1) as i:
                    body(i, range(MPS), False)
                body(BATCH - 1, range(MPS), True)

        def vector_mixer(dve, halved):
            wave_dec, quad_dec = (theta, lam) if halved else (wave, quad)

            def parity(j):
                return 0 if halved else j % 2

            def front_halo(i, j):
                m, b = MPS * i + j, j % 2
                dst = x_pre[b][:, :, 0:D_CONV - 1]
                if j % MPS == 0:
                    nc.vector.memset(dst, 0.0).then_inc(s["halo"], 1)
                else:
                    dve.wait_ge(s["xevac"], 3 * m)
                    nc.vector.tensor_copy(dst, x_pre[1 - b][:, :, MT:]).then_inc(s["halo"], 1)

            def front_conv(i, j):
                m, b = MPS * i + j, j % 2
                dve.wait_ge(s["xevac"], 3 * m + 3)
                dve.wait_ge(s["halo"], m + 1)
                for tap in range(D_CONV - 1):
                    for ct in range(XBC_T):
                        if tap:
                            dve.wait_ge(s["convd"], 15 * m + (tap - 1) * XBC_T + ct + 1)
                        nc.vector.scalar_tensor_tensor(conv[:, ct, :], x_pre[b][:, ct, tap:tap + MT], c("conv_w", ct * D_CONV + tap),
                                                       conv[:, ct, :], ALU.mult, ALU.add).then_inc(s["convd"], 1)

            def front_clip(i, j):
                m = MPS * i + j
                dve.wait_ge(s["lamsq"], m)
                dve.wait_ge(s["psum"], 4 * m)
                if halved:
                    dve.wait_ge(s["dwave"], m)
                for h, src in enumerate((bank_b, bank_a)):
                    dve.wait_ge(s["thproj"], 2 * m + h + 1)
                    nc.vector.tensor_scalar(theta[:, 2 * h:2 * h + 2, :], src.rearrange("p (n t) -> p n t", n=2), 0.25, -0.25,
                                            ALU.min, ALU.max).then_inc(s["clipped"], 1)

            def front_sums(i, j):
                m = MPS * i + j
                restart = k("tilestart")[:, 0:MT] if halved else k("restart")
                assert TILES == CH
                dve.wait_ge(s["lamdt"], m + 1)
                dve.wait_ge(s["expd"], m)
                for q in range(PAIRS):
                    nc.vector.tensor_tensor_scan(decay[:, q, :], restart, lam[:, q, :], 0.0, ALU.mult, ALU.add).then_inc(s["rsum"], 1)
                dve.wait_ge(s["angle"], m + 1)
                dve.wait_ge(s["fracd"], m)
                for q in range(PAIRS):
                    start = k("quarter") if j % MPS == 0 else frac[:, q, MT - 1:MT]
                    nc.vector.tensor_tensor_scan(phase[:, q, :], expand(k("ones")[:, 0:1], MT), theta[:, q, :], start, ALU.mult, ALU.add).then_inc(s["psum"], 1)

            def front_frac(i, j):
                m = MPS * i + j
                dve.wait_ge(s["rounded"], m + 1)
                nc.vector.tensor_tensor(frac, phase, frac, ALU.subtract).then_inc(s["fracd"], 1)

            def front_xdt(i, j):
                m, b = MPS * i + j, j % 2
                dve.wait_ge(s["upd"], two_ago(m, halved, updates(halved) * TPM))
                dve.wait_ge(s["yout"], two_ago(m, halved, TPM))
                for ch in range(TPM):
                    dve.wait_ge(s["xturned"], TPM * m + ch + 1)
                    dt_col = dt_tok[:, bass.ds(m * TPM + ch, 1), :].rearrange("p o h -> p (o h)")[:, :, None]
                    nc.vector.tensor_tensor(x_dt[b][:, ch, :].rearrange("p (h d) -> p h d", h=HEADS), bank_t.rearrange("p (h d) -> p h d", h=HEADS),
                                            dt_col.broadcast_to([P, HEADS, HEADDIM]), ALU.mult).then_inc(s["xdt"], 1)

            def front_bc(i, j):
                m, b = MPS * i + j, parity(j)
                both = [P, PAIRS, MT]
                if halved:
                    by_chunk = [v.rearrange("p q (c t) -> p (q c) t", c=CPM) for v in (epos, decay)]
                    dve.wait_ge(s["quadgrow"], m)
                    dve.wait_ge(s["rsum"], 4 * (m + 1))
                    nc.vector.tensor_tensor(by_chunk[0], by_chunk[1], by_chunk[1][:, :, CH - 1:CH].broadcast_to([P, PAIRS * CPM, CH]), ALU.subtract).then_inc(s["tail"], 1)
                dve.wait_ge(s["trig"], m + 1)
                dve.wait_ge(s["expd"], m + 1)
                dve.wait_ge(s["yout"], two_ago(m, halved, TPM))
                nc.vector.tensor_tensor(grow[b], wave, epos, ALU.mult).then_inc(s["grown"], 1)
                dve.wait_ge(s["psum"], 4 * (m + 1))
                nc.vector.tensor_tensor(wave_dec, wave, eneg, ALU.mult).then_inc(s["wavedec"], 1)
                dve.wait_ge(s["repd"], 16 * REPS * (m + 1))
                dve.wait_ge(s["wavedec"], m + 1)
                nc.vector.tensor_tensor(c_in[b], rep[:, 2:3, :].broadcast_to(both), wave_dec, ALU.mult).then_inc(s["cwave"], 1)

            def front_sum(i, j):
                m, b = MPS * i + j, parity(j)
                dve.wait_ge(s["cb"], 4 * (m + 1))
                dve.wait_ge(s["wavedec"], m + 1)
                nc.vector.tensor_tensor(c_own[b], rep[:, 4:5, :].broadcast_to([P, PAIRS, MT]), wave if halved else wave_dec, ALU.mult).then_inc(s["dwave"], 1)
                dve.wait_ge(s["grown"], m + 1)
                dve.wait_ge(s["bquad"], m + 1)
                for c in range(CPM):
                    here = slice(c * CH, (c + 1) * CH)
                    nc.vector.scalar_tensor_tensor(b_up[b][:, :, here], grow[b][:, :, here], rep[:, 0, (c + 1) * CH - 1:(c + 1) * CH], quad_grow[:, :, here],
                                                   ALU.mult, ALU.subtract).then_inc(s["bup"], 1)
                dve.wait_ge(s["cquad"], m + 1)
                dve.wait_ge(s["cwave"], m + 1)
                nc.vector.tensor_tensor(c_in[b], c_in[b], eneg, ALU.add).then_inc(s["cin"], 1)
                dve.wait_ge(s["dquad"], m + 1)
                dve.wait_ge(s["dwave"], m + 1)
                nc.vector.tensor_tensor(c_own[b], c_own[b], quad if halved else quad_dec, ALU.add).then_inc(s["cown"], 1)

            def back_levels(i, j, ch):
                m, t = MPS * i + j, (MPS * i + j) * TPM + ch
                here = slice(ch * P, (ch + 1) * P)
                over_pairs = [P, PAIRS, P]
                dve.wait_ge(s["cown"], m + 1)

                def apart(level):
                    ln, dst = LEVELS * t + level, level_e[level % 2]
                    if level >= 2:
                        dve.wait_ge(s["lbdec"], ln - 1)
                        dve.wait_ge(s["lcdec"], ln - 1)
                    else:
                        dve.wait_ge(s["lbdec"], LEVELS * t)
                        dve.wait_ge(s["lcdec"], LEVELS * t)
                    own, ref = reference(decay, ch, level)
                    for q in range(PAIRS):
                        last = nc.vector.tensor_tensor(dst[:, q, :].rearrange("p (n w) -> p n w", w=CH >> level), own[q], ref[q], ALU.subtract)
                    last.then_inc(s["apart"], 1)
                    dve.wait_ge(s["apart"], ln + 1)
                    nc.vector.tensor_tensor(dst, dst, level_signs[:, level:level + 1, :].broadcast_to(over_pairs), ALU.mult).then_inc(s["signed"], 1)

                def add(level):
                    ln = (LEVELS + 1) * t + level
                    mask = level_masks[:, level:level + 1, :].broadcast_to(over_pairs)
                    for h in range(2):
                        dve.wait_ge(s["lscored"], 2 * ln + h + 1)
                        src, dst = bank_s[:, h, :].rearrange("p (h t) -> p h t", h=4), att[ch][:, 4 * h:4 * h + 4, :]
                        if level == 0:
                            nc.vector.tensor_tensor(dst, src, mask, ALU.mult).then_inc(s["lmasked"], 1)
                        else:
                            dve.wait_ge(s["lsum"], 2 * (LEVELS * t + level - 1) + h)
                            nc.vector.tensor_tensor(part_att, src, mask, ALU.mult).then_inc(s["lmasked"], 1)
                            dve.wait_ge(s["lmasked"], 2 * ln + h + 1)
                            last = nc.vector.tensor_tensor(dst, dst, part_att, ALU.add).then_inc(s["lsum"], 1)
                            if level == LEVELS:
                                dve.wait_ge(s["lsum"], 2 * (LEVELS * t + level - 1) + h + 1)
                                dve.sem_inc(s["masked"], 1)

                dve.wait_ge(s["yout"], t - 1 if ch else t)
                apart(0)
                for level in range(LEVELS + 1):
                    if level + 1 < LEVELS:
                        apart(level + 1)
                    if level < LEVELS:
                        dve.wait_ge(s["lexpd"], LEVELS * t + level + 1)
                        if level >= 2:
                            dve.wait_ge(s["lscored"], 2 * ((LEVELS + 1) * t + level - 1))
                        nc.vector.tensor_tensor(level_c[level % 2], c_own[0][:, :, here], level_e[level % 2], ALU.mult).then_inc(s["lcdec"], 1)
                    add(level)

            def back_mask(i, j, ch):
                t = (MPS * i + j) * TPM + ch
                dve.wait_ge(s["yout"], t - 1 if ch else t)
                for h in range(2):
                    dve.wait_ge(s["scored"], 2 * t + h + 1)
                    nc.vector.tensor_tensor(att[ch][:, 4 * h:4 * h + 4, :], bank_s[:, h, :].rearrange("p (h t) -> p h t", h=4),
                                            k("causal")[:, None, :].broadcast_to([P, 4, P]), ALU.mult).then_inc(s["masked"], 1)

            def back_state(i, j, ch, c):
                u = ((MPS * i + j) * TPM + ch) * updates(halved) + c
                old = state_in[state_slot(j, ch, c, halved)]
                dve.wait_ge(s["upd"], u + 1)
                dve.wait_ge(s["statein"], u)
                for e in range(2):
                    part = slice(e * HEADDIM, (e + 1) * HEADDIM)
                    new = bank_u[part, :].rearrange("p (q d) -> p q d", q=PAIRS)[:, :, part]
                    if halved:
                        for q in range(PAIRS):
                            last = nc.vector.scalar_tensor_tensor(state[part, q, :], old[part, q, part], end_dec[part, ch * CPT + c, q:q + 1], new[:, q, :], ALU.mult, ALU.add)
                    else:
                        last = nc.vector.tensor_tensor(state[part, :, :], new, old[part, :, part], ALU.add)
                    last.then_inc(s["stated"], 1)

            def back_gate(i, j, ch):
                b, t = j % 2, (MPS * i + j) * TPM + ch
                here = slice(ch * P, (ch + 1) * P)
                dve.wait_ge(s["yout"], t + 1)
                dve.wait_ge(s["oproj"], t - 1 if ch else t)
                dve.wait_ge(s["squared"], t - 1 if ch else t)
                dve.wait_ge(s["zevac"], 2 * (MPS * i + j + 1))
                nc.vector.tensor_tensor(g[ch], bank_y.rearrange("p (q t) -> p q t", q=PAIRS), z_gate[b][:, :, here], ALU.mult).then_inc(s["gated"], 1)

            def back_ms(i, j, ch):
                n, t = MPS * i + j, (MPS * i + j) * TPM + ch
                dve.wait_ge(x_loaded[ch], 16 * n + 16)
                dve.wait_ge(e_loaded2[ch], 16 * n + 16)
                gate_col = gate[:, bass.ds(t, 1)]
                nc.vector.scalar_tensor_tensor(x_tile[ch][:, :], e_tile[ch][:, :], gate_col, x_tile[ch][:, :], ALU.mult, ALU.add).then_inc(s["xplus"], 1)
                dve.wait_ge(s["oproj"], t + 1)
                dve.wait_ge(s["rmsd"], t - 1 if ch else t)
                nc.vector.tensor_scalar(ms[ch][:, :], bank_o[:, D_MODEL:D_MODEL + 1], 1.0 / D_INNER, RMS_EPS, ALU.mult, ALU.add).then_inc(s["meansq"], 1)

            def back_final(i, j, ch):
                n, t = MPS * i + j, (MPS * i + j) * TPM + ch
                dve.wait_ge(s["rmsd"], t + 1)
                dve.wait_ge(s["xplus"], t + 1)
                dve.wait_ge(o_stored[ch], 16 * n)
                nc.vector.scalar_tensor_tensor(o_tile[ch][:, :], bank_o[:, 0:D_MODEL], rms[ch][:, :], x_tile[ch][:, :], ALU.mult, ALU.add).then_inc(s["final"], 1)

            def body(i, js, last):
                for j in js:
                    left = MPS - 1 - j if last else MPS
                    back_mask(i, j, 0)
                    back_state(i, j, 0, 0)
                    if left >= 3:
                        front_halo(i, j + 3)
                    if left >= 1:
                        front_frac(i, j + 1)
                    if left >= 2:
                        front_clip(i, j + 2)
                    back_gate(i, j, 0)
                    if left >= 1:
                        front_xdt(i, j + 1)
                    if left >= 2:
                        front_conv(i, j + 2)
                    back_ms(i, j, 0)
                    back_mask(i, j, 1)
                    if left >= 1:
                        front_bc(i, j + 1)
                    back_gate(i, j, 1)
                    back_final(i, j, 0)
                    if left >= 1:
                        front_sum(i, j + 1)
                    back_ms(i, j, 1)
                    back_state(i, j, 1, 0)
                    if left >= 2:
                        front_sums(i, j + 2)
                    back_final(i, j, 1)

            nc.vector.memset(hidden[32:LORA + 1, :], 1.0).then_inc(m_ready, 1)
            nc.vector.memset(state_in[0][:, :, :], 0.0).then_inc(m_zero, 1)
            if halved:
                dve.wait_ge(table_in, 32)
                with dve.Fori(0, BATCH) as i:
                    for j in range(MPS):
                        front_halo(i, j)
                        front_clip(i, j)
                        front_conv(i, j)
                        front_sums(i, j)
                        front_frac(i, j)
                        front_xdt(i, j)
                        front_bc(i, j)
                        front_sum(i, j)
                        for ch in range(TPM):
                            back_levels(i, j, ch)
                            for part in range(CPT):
                                back_state(i, j, ch, part)
                            back_gate(i, j, ch)
                            back_ms(i, j, ch)
                            back_final(i, j, ch)
            else:
                front_halo(0, 0)
                front_halo(0, 1)
                front_clip(0, 0)
                front_conv(0, 0)
                front_sums(0, 0)
                front_frac(0, 0)
                front_xdt(0, 0)
                front_conv(0, 1)
                front_clip(0, 1)
                front_bc(0, 0)
                front_halo(0, 2)
                front_sum(0, 0)
                front_sums(0, 1)
                with dve.Fori(0, BATCH - 1) as i:
                    body(i, range(MPS), False)
                body(BATCH - 1, range(MPS), True)

        def gpsimd_mixer(pool, halved):
            wave_dec, quad_dec = (theta, lam) if halved else (wave, quad)

            def parity(j):
                return 0 if halved else j % 2

            def front_dt(i, j):
                m, n, b = MPS * i + j, 2 * i + j // 2, j % 2
                pool.wait_ge(dt_loaded[b], 32 * (n + 1))
                pool.wait_ge(s["lamsq"], m + 1)
                nc.gpsimd.tensor_tensor(theta, theta, dt_in[b], ALU.mult).then_inc(s["angle"], 1)
                pool.wait_ge(s["lamd"], m + 1)
                nc.gpsimd.tensor_tensor(lam, lam, dt_in[b], ALU.mult).then_inc(s["lamdt"], 1)

            def front_head(i, j):
                m, b = MPS * i + j, j % 2
                n = updates(halved) * TPM
                shape = [P, n * PAIRS, 2]
                pool.wait_ge(s["negd"], m + 1)
                nc.gpsimd.tensor_tensor(head_dec[b][:, 0:n, :].rearrange("p c (q e) -> p (c q) e", e=2), end_dec[:, 0:n, :].rearrange("p c q -> p (c q)")[:, :, None].broadcast_to(shape),
                                        k("ownhead")[:, None, :].broadcast_to(shape), ALU.mult).then_inc(s["headdec"], 1)

            def front_cb(i, j):
                m = MPS * i + j
                b_both, c_re, c_im, re, im = rep[:, 0:2, :], rep[:, 2:3, :], rep[:, 3:4, :], rep[:, 4, :], rep[:, 5, :]
                pool.wait_ge(s["repd"], 16 * REPS * (m + 1))
                pool.wait_ge(s["cown"], m)
                nc.gpsimd.tensor_tensor(rep[:, 4:6, :], c_re.broadcast_to([P, 2, MT]), b_both, ALU.mult).then_inc(s["cb"], 1)
                nc.gpsimd.tensor_tensor(cb_part, c_im.broadcast_to([P, 2, MT]), b_both, ALU.mult).then_inc(s["cb"], 1)
                pool.wait_ge(s["cb"], 4 * m + 2)
                nc.gpsimd.tensor_tensor(re, re, cb_part[:, 1, :], ALU.subtract).then_inc(s["cb"], 1)
                nc.gpsimd.tensor_tensor(im, im, cb_part[:, 0, :], ALU.add).then_inc(s["cb"], 1)

            def front_bc(i, j):
                m = MPS * i + j
                pool.wait_ge(s["trig"], m + 1)
                pool.wait_ge(s["expd"], m + 1)
                nc.gpsimd.tensor_tensor(quad_grow, quad, epos, ALU.mult).then_inc(s["quadgrow"], 1)
                pool.wait_ge(s["rsum"], 4 * (m + 1))
                nc.gpsimd.tensor_tensor(quad_dec, quad, eneg, ALU.mult).then_inc(s["quaddec"], 1)

            def front_products(i, j):
                m = MPS * i + j
                both = [P, PAIRS, MT]
                b_ends = rep[:, 1, :].rearrange("p (c t) -> p c t", c=CPM)[:, None, :, CH - 1:CH]
                by_chunk = quad_grow.rearrange("p q (c t) -> p q c t", c=CPM)
                pool.wait_ge(s["quadgrow"], m + 1)
                nc.gpsimd.tensor_tensor(by_chunk, by_chunk, b_ends.broadcast_to([P, PAIRS, CPM, CH]), ALU.mult).then_inc(s["bquad"], 1)
                pool.wait_ge(s["quaddec"], m + 1)
                pool.wait_ge(s["wavedec"], m + 1)
                nc.gpsimd.tensor_tensor(eneg, rep[:, 3:4, :].broadcast_to(both), quad_dec, ALU.mult).then_inc(s["cquad"], 1)
                pool.wait_ge(s["cquad"], m + 1)
                pool.wait_ge(s["cb"], 4 * (m + 1))
                v = quad if halved else quad_dec
                nc.gpsimd.tensor_tensor(v, rep[:, 5:6, :].broadcast_to(both), v, ALU.mult).then_inc(s["dquad"], 1)

            def back_levels(i, j, ch):
                m, t = MPS * i + j, (MPS * i + j) * TPM + ch
                here = slice(ch * P, (ch + 1) * P)
                pool.wait_ge(s["cown"], m + 1)
                pool.wait_ge(s["cin"], m + 1)
                for level in range(LEVELS):
                    pool.wait_ge(s["lexpd"], LEVELS * t + level + 1)
                    pool.wait_ge(s["lscored"], 2 * ((LEVELS + 1) * t + max(level - 1, 0)))
                    nc.gpsimd.tensor_tensor(level_b[level % 2], wave[:, :, here], level_e[level % 2], ALU.mult).then_inc(s["lbdec"], 1)

            def back_state(i, j, ch, c):
                b, u = j % 2, ((MPS * i + j) * TPM + ch) * updates(halved) + c
                pool.wait_ge(s["stated"], 2 * u + 2)
                t = (MPS * i + j) * TPM + ch
                if not halved:
                    if j:
                        pool.wait_ge(s["yout"], t - 2)
                    elif not isinstance(t, int) or t > 0:
                        pool.wait_ge(s["yout"], t)
                elif c:
                    pool.wait_ge(s["yout"], t)
                elif not (j == 0 and ch == 0):
                    pool.wait_ge(s["yout"], t - 1)
                elif not isinstance(i, int):
                    pool.wait_ge(s["yout"], t)
                shape = [P, PAIRS, 2, HEADDIM]
                dst = state_in[(state_slot(j, ch, c, halved) + 1) % CPM][:, :, :].rearrange("p q (e d) -> p q e d", e=2)
                if j == MPS - 1 and ch == TPM - 1 and c == updates(halved) - 1:
                    by = zero_dec[:, :]
                elif halved:
                    by = None
                else:
                    by = head_dec[b][:, ch, :]
                own = k("ownhead")[:, None, :, None] if by is None else by.rearrange("p (q e) -> p q e", e=2)[:, :, :, None]
                nc.gpsimd.tensor_tensor(dst, state[:, :, None, :].broadcast_to(shape), own.broadcast_to(shape), ALU.mult).then_inc(s["statein"], 1)

            def back_gather(i, j, ch):
                n, t = MPS * i + j, (MPS * i + j) * TPM + ch
                pool.wait_ge(s["xplus"], TPM * n)
                pool.wait_ge(e_loaded2[ch], 16 * n)
                pool.sem_inc(passed, 1)
                nc.gpsimd.tensor_copy(e_index[ch][:, :], slot_of[:, bass.ds(t, 1)]).then_inc(s["eidx"], 1)
                pool.wait_ge(s["eidx"], t + 1)
                pool.sem_inc(passed, 1)
                pool.indirect_dma_start(e_tile[ch][:, :], None, expert_d, bass.IndirectOffsetOnAxis(ap=e_index[ch][:, :], axis=0)).then_inc(e_loaded2[ch], 16)

            def back_rms(i, j, ch):
                t = (MPS * i + j) * TPM + ch
                pool.wait_ge(s["meansq"], t + 1)
                pool.wait_ge(s["final"], t)
                nc.gpsimd.tensor_tensor(rms[ch][:, :], ms[ch][:, :], k("minushalf")[:, 0:1], ALU.pow).then_inc(s["rmsd"], 1)

            def body(i, js, last):
                for j in js:
                    left = MPS - 1 - j if last else MPS
                    back_gather(i, j, 0)
                    back_gather(i, j, 1)
                    back_state(i, j, 0, 0)
                    if left >= 1:
                        front_cb(i, j + 1)
                        front_bc(i, j + 1)
                    back_rms(i, j, 0)
                    if left >= 1:
                        front_products(i, j + 1)
                    if left >= 2:
                        front_dt(i, j + 2)
                    back_rms(i, j, 1)
                    if left >= 1:
                        front_head(i, j + 1)
                    back_state(i, j, 1, 0)

            pool.wait_ge(m_zero, 1)
            nc.gpsimd.memset(zero_dec[:, :], 0.0).then_inc(m_ready, 1)
            pool.wait_ge(m_ready, 2)
            if halved:
                with pool.Fori(0, BATCH) as i:
                    for j in range(MPS):
                        front_dt(i, j)
                        front_cb(i, j)
                        front_head(i, j)
                        front_bc(i, j)
                        front_products(i, j)
                        for ch in range(TPM):
                            back_gather(i, j, ch)
                            back_levels(i, j, ch)
                            for part in range(CPT):
                                back_state(i, j, ch, part)
                            back_rms(i, j, ch)
            else:
                front_dt(0, 0)
                front_cb(0, 0)
                front_bc(0, 0)
                front_products(0, 0)
                front_dt(0, 1)
                front_head(0, 0)
                with pool.Fori(0, BATCH - 1) as i:
                    body(i, range(MPS), False)
                body(BATCH - 1, range(MPS), True)

        with nc.Block() as block:
            @block.sync
            def _(sp):
                chunks_halved = sp.value_load(halve[0:1, 0:1], min_val=0, max_val=1)
                with sp.If(chunks_halved == 0):
                    sync_mixer(sp, False)
                with sp.If(chunks_halved != 0):
                    sync_mixer(sp, True)

            @block.tensor
            def _(pe):
                chunks_halved = pe.value_load(halve[0:1, 0:1], min_val=0, max_val=1)
                with pe.If(chunks_halved == 0):
                    tensor_mixer(pe, False)
                with pe.If(chunks_halved != 0):
                    tensor_mixer(pe, True)

            @block.scalar
            def _(act):
                chunks_halved = act.value_load(halve[0:1, 0:1], min_val=0, max_val=1)
                with act.If(chunks_halved == 0):
                    scalar_mixer(act, False)
                with act.If(chunks_halved != 0):
                    scalar_mixer(act, True)

            @block.vector
            def _(dve):
                chunks_halved = dve.value_load(halve[0:1, 0:1], min_val=0, max_val=1)
                with dve.If(chunks_halved == 0):
                    vector_mixer(dve, False)
                with dve.If(chunks_halved != 0):
                    vector_mixer(dve, True)

            @block.gpsimd
            def _(pool):
                chunks_halved = pool.value_load(halve[0:1, 0:1], min_val=0, max_val=1)
                with pool.If(chunks_halved == 0):
                    gpsimd_mixer(pool, False)
                with pool.If(chunks_halved != 0):
                    gpsimd_mixer(pool, True)


_OUT = (BATCH, SEQ, D_MODEL)


def kernel(**inputs):
    import numpy as np
    import concourse.bacc as bacc
    from concourse.bass_utils import run_bass_kernel_spmd

    a = {n.replace("L0_", ""): np.asarray(v) for n, v in inputs.items()}

    const = np.zeros((P, CONST_W), np.float32)

    def put(name, v):
        const[:, CONST[name][0]:CONST[name][0] + CONST[name][1]] = v
    row, colm = np.arange(P)[:, None], np.arange(P)[None, :]
    put("ident", row == colm)
    put("causal", row <= colm)
    put("before", row < colm)
    put("ones", 1.0)
    put("restart", (np.arange(MT) % P != 0)[None, :])
    put("tilestart", (np.arange(TILES * EXPERTS) % TILES != 0)[None, :])
    put("first", (EXPERTS - np.arange(EXPERTS))[None, :])
    put("slot", np.arange(SLOT_TILES)[None, :])
    real = (row // NBLK) % 2 == 0
    put("quarter", np.where(real, 0.25, 0.0))
    put("halfpi", math.pi / 2)
    put("minushalf", -0.5)
    put("ownhead", row // (2 * NBLK) == np.arange(2)[None, :])

    halvings = np.zeros((P, 2 * LEVELS + 1, P), np.float32)
    for level in range(LEVELS):
        half = CH >> (level + 1)
        first = np.arange(P) % (2 * half) < half
        halvings[:, level] = np.where(first, 1.0, -1.0)
        halvings[:, LEVELS + level] = (row // (2 * half) == colm // (2 * half)) & first[:, None] & ~first[None, :]
    halvings[:, 2 * LEVELS] = row == colm

    def by_tile(v):
        return np.moveaxis(v.reshape(-1, P, *v.shape[1:]), 0, 1)

    bc = D_INNER + np.concatenate([np.arange(h, h + 2 * NBLK, 2) for h in (0, 1, 2 * NBLK, 2 * NBLK + 1)])
    xbc = np.concatenate([np.arange(D_INNER), bc])
    w = a["attn_in_proj_w"]
    w_in = np.concatenate([w[D_INNER:][xbc], w[:D_INNER]]).T
    w_small = np.concatenate([w[-HEADS:].T, a["ffn_router_w"]], axis=1)

    def spread(v):
        return np.broadcast_to(v.reshape(PAIRS, 2, 1, NBLK), (PAIRS, 2, 2, NBLK)).reshape(PAIRS, P).T

    lora2 = np.concatenate([a["attn_theta_w2"], a["attn_theta_base"].reshape(1, -1)])
    lora2 = np.broadcast_to(lora2.reshape(LORA + 1, PAIRS, 2, 1, NBLK), (LORA + 1, PAIRS, 2, 2, NBLK)).reshape(LORA + 1, PAIRS * P)
    cols = np.concatenate([
        by_tile(a["attn_conv_w"][xbc]).reshape(P, -1), by_tile(a["attn_conv_b"][xbc]).reshape(P, -1),
        by_tile(np.repeat(a["attn_D"], HEADDIM)), by_tile(a["attn_norm_w"]),
        spread(a["attn_lambda_base"]), spread(a["attn_viscosity_eta"])], axis=1)
    arrays = {
        "x": a["attn_x"].reshape(TOKENS, D_MODEL), "const": const, "halvings": halvings, "cols": cols, "w_in": by_tile(w_in), "w_small": by_tile(w_small),
        "w_lora1": by_tile(a["attn_theta_w1"]), "w_lora2": lora2, "w_out": by_tile(a["attn_out_proj_w"].T),
        "rows": np.concatenate([a[n].reshape(-1) for n in ("attn_dt_bias", "ffn_router_b", "attn_lambda_base", "attn_viscosity_eta")])[None, :],
        "w_exp": by_tile(np.moveaxis(a["ffn_expert_w"], 0, 1)).reshape(P, KT * EXPERTS, D_MODEL),
        "b_exp": a["ffn_expert_b"],
        "ids": np.concatenate([np.broadcast_to(colm, (P, P)), np.broadcast_to(np.arange(TILES), (P, TILES)), row], axis=1).astype(np.float32),
    }
    nc = bacc.Bacc("TRN2", target_bir_lowering=False, num_devices=1)
    arrays = {n: np.ascontiguousarray(v) for n, v in arrays.items()}
    aps = [nc.dram_tensor(n, v.shape, mybir.dt.from_np(v.dtype), kind="ExternalInput").ap() for n, v in arrays.items()]
    out = nc.dram_tensor("out", (TOKENS, D_MODEL), F32, kind="ExternalOutput").ap()
    mixer_and_experts(nc, *aps, out)
    r = run_bass_kernel_spmd(nc, [arrays], core_ids=[0])
    return r.results[0]["out"].reshape(_OUT)
```
